# Optimizing a Trainium2 kernel written in Bass

```python
import numpy as np
import jax
import jax.numpy as jnp

def _softmax(x, axis=-1):
    return jax.nn.softmax(x, axis=axis)

def _gelu(x):
    return jax.nn.gelu(x, approximate=True)

def _silu(x):
    return jax.nn.silu(x)

def _sigmoid(x):
    return jax.nn.sigmoid(x)

def _layernorm(x, axis=-1, eps=1e-05):
    m = jnp.mean(x, axis=axis, keepdims=True)
    v = jnp.var(x, axis=axis, keepdims=True)
    return (x - m) / jnp.sqrt(v + eps)

def _scatter_add(tgt, idx, src, axis=0):
    return tgt.at[idx].add(src)

def _segment_sum(src, seg, n):
    return jax.ops.segment_sum(src, seg, n)
kernel_name = 'mk_recurrent_d2_jaxref_r4_41cfc6'

def setup_inputs(seed: int=0):
    np.random.seed(seed)
    _w = jnp.asarray

    def _L0_attn_setup():
        import jax, jax.numpy as jnp
        import numpy as np
        NUM_HEADS = 16
        WINDOW = 64

        def _rel_pos_bias(rel_bias, window):
            coords = jnp.arange(window)
            rel = coords[:, None] - coords[None, :] + (window - 1)
            bias = rel_bias[rel]
            return jnp.transpose(bias, (2, 0, 1))
        key = jax.random.key(seed)
        ks = jax.random.split(key, 5)
        B, S, D = (8, 1024, 256)
        x = jax.random.normal(ks[0], (B, S, D), dtype=jnp.float32)
        qkv_w = jax.random.normal(ks[1], (D, 3 * D), dtype=jnp.float32) * (1.0 / np.sqrt(D))
        qkv_b = jnp.zeros((3 * D,), dtype=jnp.float32)
        proj_w = jax.random.normal(ks[2], (D, D), dtype=jnp.float32) * (1.0 / np.sqrt(D))
        proj_b = jnp.zeros((D,), dtype=jnp.float32)
        rel_bias = jax.random.normal(ks[3], (2 * WINDOW - 1, NUM_HEADS), dtype=jnp.float32) * 0.02
        return {'x': x, 'qkv_w': qkv_w, 'qkv_b': qkv_b, 'proj_w': proj_w, 'proj_b': proj_b, 'rel_bias': rel_bias}
    _L0_attn_in = _L0_attn_setup()

    def _L0_ffn_setup():
        import math
        import jax, jax.numpy as jnp
        import numpy as np
        CAPACITY_FACTOR = 1.25
        key = jax.random.key(seed)
        ks = jax.random.split(key, 5)
        B, S, H, F, E = (4, 1024, 256, 256, 32)
        scale_in = 1.0 / math.sqrt(H)
        scale_mid = 1.0 / math.sqrt(F)
        return {'x': jax.random.normal(ks[0], (B, S, H), dtype=jnp.float32), 'w_router': jax.random.normal(ks[1], (H, E), dtype=jnp.float32) * scale_in, 'w_gate': jax.random.normal(ks[2], (E, H, F), dtype=jnp.float32) * scale_in, 'w_up': jax.random.normal(ks[3], (E, H, F), dtype=jnp.float32) * scale_in, 'w_down': jax.random.normal(ks[4], (E, F, H), dtype=jnp.float32) * scale_mid}
    _L0_ffn_in = _L0_ffn_setup()

    def _L1_attn_setup():
        import jax, jax.numpy as jnp
        import numpy as np
        EPS = 1e-08

        def unit_projection(x):
            f = jnp.fft.fft(x)
            f = f / (jnp.abs(f) + EPS)
            return jnp.fft.ifft(f).real

        def bind(a, b):
            return jnp.fft.ifft(jnp.fft.fft(a) * jnp.fft.fft(b)).real

        def unbind(s, a):
            return jnp.fft.ifft(jnp.fft.fft(s) * jnp.conj(jnp.fft.fft(a))).real
        key = jax.random.key(seed)
        B, S, D = (4, 1024, 256)
        ks = jax.random.split(key, 7)
        scale = 1.0 / np.sqrt(D)
        x = jax.random.normal(ks[0], (B, S, D), dtype=jnp.float32)
        Wq = jax.random.uniform(ks[1], (D, D), jnp.float32, -scale, scale)
        bq = jax.random.uniform(ks[2], (D,), jnp.float32, -scale, scale)
        Wk = jax.random.uniform(ks[3], (D, D), jnp.float32, -scale, scale)
        bk = jax.random.uniform(ks[4], (D,), jnp.float32, -scale, scale)
        Wv = jax.random.uniform(ks[5], (D, D), jnp.float32, -scale, scale)
        bv = jax.random.uniform(ks[6], (D,), jnp.float32, -scale, scale)
        return {'x': x, 'Wq': Wq, 'bq': bq, 'Wk': Wk, 'bk': bk, 'Wv': Wv, 'bv': bv}
    _L1_attn_in = _L1_attn_setup()

    def _L1_ffn_setup():
        import jax, jax.numpy as jnp
        import numpy as np
        N_EMBED = 256
        FFN_HIDDEN = 1024
        NUM_EXPERTS = 8
        TOP_K = 2
        key = jax.random.key(seed)
        ks = jax.random.split(key, 8)
        d, f, E = (N_EMBED, FFN_HIDDEN, NUM_EXPERTS)
        s_d = 1.0 / np.sqrt(d)
        s_f = 1.0 / np.sqrt(f)
        return {'x': jax.random.normal(ks[0], (2, 512, d), dtype=jnp.float32), 'Wg': jax.random.uniform(ks[1], (d, E), jnp.float32, -s_d, s_d), 'bg': jax.random.uniform(ks[2], (E,), jnp.float32, -s_d, s_d), 'W1': jax.random.uniform(ks[3], (E, d, f), jnp.float32, -s_d, s_d), 'b1': jax.random.uniform(ks[4], (E, f), jnp.float32, -s_d, s_d), 'W2': jax.random.uniform(ks[5], (E, f, d), jnp.float32, -s_f, s_f), 'b2': jax.random.uniform(ks[6], (E, d), jnp.float32, -s_f, s_f)}
    _L1_ffn_in = _L1_ffn_setup()
    _d = {'L0_attn_x': _L0_attn_in['x'], 'L0_attn_qkv_w': _L0_attn_in['qkv_w'], 'L0_attn_qkv_b': _L0_attn_in['qkv_b'], 'L0_attn_proj_w': _L0_attn_in['proj_w'], 'L0_attn_proj_b': _L0_attn_in['proj_b'], 'L0_attn_rel_bias': _L0_attn_in['rel_bias'], 'L0_ffn_w_router': _L0_ffn_in['w_router'], 'L0_ffn_w_gate': _L0_ffn_in['w_gate'], 'L0_ffn_w_up': _L0_ffn_in['w_up'], 'L0_ffn_w_down': _L0_ffn_in['w_down'], 'L1_attn_Wq': _L1_attn_in['Wq'], 'L1_attn_bq': _L1_attn_in['bq'], 'L1_attn_Wk': _L1_attn_in['Wk'], 'L1_attn_bk': _L1_attn_in['bk'], 'L1_attn_Wv': _L1_attn_in['Wv'], 'L1_attn_bv': _L1_attn_in['bv'], 'L1_ffn_Wg': _L1_ffn_in['Wg'], 'L1_ffn_bg': _L1_ffn_in['bg'], 'L1_ffn_W1': _L1_ffn_in['W1'], 'L1_ffn_b1': _L1_ffn_in['b1'], 'L1_ffn_W2': _L1_ffn_in['W2'], 'L1_ffn_b2': _L1_ffn_in['b2']}
    _x0 = _d['L0_attn_x']
    _d['L0_attn_x'] = jax.random.normal(jax.random.fold_in(jax.random.key(seed), 1), (4, 1024, 256), dtype=_x0.dtype)
    del _x0
    return _d

def reference(L0_attn_x, L0_attn_qkv_w, L0_attn_qkv_b, L0_attn_proj_w, L0_attn_proj_b, L0_attn_rel_bias, L0_ffn_w_router, L0_ffn_w_gate, L0_ffn_w_up, L0_ffn_w_down, L1_attn_Wq, L1_attn_bq, L1_attn_Wk, L1_attn_bk, L1_attn_Wv, L1_attn_bv, L1_ffn_Wg, L1_ffn_bg, L1_ffn_W1, L1_ffn_b1, L1_ffn_W2, L1_ffn_b2):

    def _L0_attn_ref(x, qkv_w, qkv_b, proj_w, proj_b, rel_bias):
        import jax, jax.numpy as jnp
        import numpy as np
        NUM_HEADS = 16
        WINDOW = 64

        def _rel_pos_bias(rel_bias, window):
            coords = jnp.arange(window)
            rel = coords[:, None] - coords[None, :] + (window - 1)
            bias = rel_bias[rel]
            return jnp.transpose(bias, (2, 0, 1))
        B, S, D = x.shape
        H, W = (NUM_HEADS, WINDOW)
        hd = D // H
        nW = S // W
        scale = 1.0 / np.sqrt(hd)
        xw = x.reshape(B, nW, W, D)
        qkv = xw @ qkv_w + qkv_b
        qkv = qkv.reshape(B, nW, W, 3, H, hd)
        q, k, v = (qkv[..., 0, :, :], qkv[..., 1, :, :], qkv[..., 2, :, :])
        attn = jnp.einsum('bnqhd,bnkhd->bnhqk', q, k) * scale
        attn = attn + _rel_pos_bias(rel_bias, W)[None, None]
        attn = jax.nn.softmax(attn, axis=-1)
        out = jnp.einsum('bnhqk,bnkhd->bnqhd', attn, v)
        out = out.reshape(B, S, D)
        return out @ proj_w + proj_b

    def _L0_ffn_ref(x, w_router, w_gate, w_up, w_down):
        import math
        import jax, jax.numpy as jnp
        import numpy as np
        CAPACITY_FACTOR = 1.25
        B, S, H = x.shape
        E = w_gate.shape[0]
        T = B * S
        C = int(math.ceil(CAPACITY_FACTOR * T / E))
        xt = x.reshape(T, H)
        logits = xt @ w_router
        probs = jax.nn.softmax(logits, axis=-1)
        top1 = jnp.argmax(probs, axis=-1)
        gate = jnp.take_along_axis(probs, top1[:, None], axis=1)[:, 0]
        onehot = jax.nn.one_hot(top1, E, dtype=jnp.int32)
        pos = jnp.cumsum(onehot, axis=0)[jnp.arange(T), top1] - 1
        accepted = pos < C
        slot = jnp.where(accepted, top1 * C + pos, E * C)
        buf = jnp.zeros((E * C + 1, H), dtype=x.dtype).at[slot].set(xt)
        buf = buf[:E * C].reshape(E, C, H)
        g = jnp.einsum('ech,ehf->ecf', buf, w_gate)
        u = jnp.einsum('ech,ehf->ecf', buf, w_up)
        y = jnp.einsum('ecf,efh->ech', jax.nn.silu(g) * u, w_down)
        out_tok = y.reshape(E * C, H)[jnp.clip(slot, 0, E * C - 1)]
        out_tok = jnp.where(accepted[:, None], out_tok * gate[:, None], 0.0)
        return (xt + out_tok).reshape(B, S, H)

    def _L1_attn_ref(x, Wq, bq, Wk, bk, Wv, bv):
        import jax, jax.numpy as jnp
        import numpy as np
        EPS = 1e-08

        def unit_projection(x):
            f = jnp.fft.fft(x)
            f = f / (jnp.abs(f) + EPS)
            return jnp.fft.ifft(f).real

        def bind(a, b):
            return jnp.fft.ifft(jnp.fft.fft(a) * jnp.fft.fft(b)).real

        def unbind(s, a):
            return jnp.fft.ifft(jnp.fft.fft(s) * jnp.conj(jnp.fft.fft(a))).real
        query = unit_projection(jnp.einsum('bsd,ed->bse', x, Wq) + bq)
        keys = unit_projection(jnp.einsum('bsd,ed->bse', x, Wk) + bk)
        values = unit_projection(jnp.einsum('bsd,ed->bse', x, Wv) + bv)
        x_k = bind(keys, values)
        s = jnp.cumsum(x_k, axis=1)
        out = unbind(s, query)
        return out

    def _L1_ffn_ref(x, Wg, bg, W1, b1, W2, b2):
        import jax, jax.numpy as jnp
        import numpy as np
        N_EMBED = 256
        FFN_HIDDEN = 1024
        NUM_EXPERTS = 8
        TOP_K = 2
        gate_scores = jax.nn.softmax(x @ Wg + bg, axis=-1)
        topk_scores, topk_idx = jax.lax.top_k(gate_scores, TOP_K)
        topk_scores = topk_scores / (jnp.sum(topk_scores, axis=-1, keepdims=True) + 1e-08)
        onehot = jax.nn.one_hot(topk_idx, NUM_EXPERTS, dtype=x.dtype)
        combine_w = jnp.einsum('bsk,bske->bse', topk_scores, onehot)
        output = jnp.zeros_like(x)
        for e in range(NUM_EXPERTS):
            h = jax.nn.gelu(x @ W1[e] + b1[e])
            y = h @ W2[e] + b2[e]
            output = output + y * combine_w[..., e:e + 1]
        return output
    x = L0_attn_x
    xn = _layernorm(x, axis=-1)
    s = _L0_attn_ref(xn, L0_attn_qkv_w, L0_attn_qkv_b, L0_attn_proj_w, L0_attn_proj_b, L0_attn_rel_bias)
    g = _silu(_L0_ffn_ref(xn, L0_ffn_w_router, L0_ffn_w_gate, L0_ffn_w_up, L0_ffn_w_down))
    x = x + s * g
    xn = _layernorm(x, axis=-1)
    s = _L1_attn_ref(xn, L1_attn_Wq, L1_attn_bq, L1_attn_Wk, L1_attn_bk, L1_attn_Wv, L1_attn_bv)
    g = _silu(_L1_ffn_ref(xn, L1_ffn_Wg, L1_ffn_bg, L1_ffn_W1, L1_ffn_b1, L1_ffn_W2, L1_ffn_b2))
    x = x + s * g
    return x

_drawn_inputs = setup_inputs


def setup_inputs(seed=0):
    import zlib

    import numpy as np

    out = dict(_drawn_inputs(seed))
    spreads = {'L0_attn_qkv_b': (0.0, 0.1), 'L0_attn_proj_b': (0.0, 0.1)}
    factors = {'L0_attn_rel_bias': 8.0,
     'L1_attn_bq': 2.953,
     'L1_attn_bk': 4.019,
     'L1_attn_bv': 3.942,
     'L1_ffn_b1': 5.128,
     'L1_ffn_b2': 3.621}
    for name, (base, spread) in spreads.items():
        noise = np.random.default_rng([zlib.crc32(name.encode()), seed]).standard_normal(out[name].shape)
        drawn = base * np.exp(spread * noise) if base else spread * noise
        out[name] = jnp.asarray(drawn.astype(out[name].dtype))
    for name, factor in factors.items():
        out[name] = (out[name] * factor).astype(out[name].dtype)
    return out
```

```python
import numpy as np
import concourse.bass as bass
from concourse import mybir

F32 = mybir.dt.float32
I32 = mybir.dt.int32
ALU = mybir.AluOpType
ACT = mybir.ActivationFunctionType
AX = mybir.AxisListType

P = 128
BATCH, SEQ, D = 4, 1024, 256
T = BATCH * SEQ
NT = T // P
KD = D // P
LN_EPS = 1e-5
HEADS, WIN = 16, 64
HD = D // HEADS
PAIRS = HEADS // 2
E0, F0 = 32, 256
CAP = -(-5 * T // (4 * E0))
SLOTS0 = E0 * CAP
E1, F1, TOPK = 8, 1024, 2
TILES1 = (T * TOPK + E1 * (P - 1)) // P
SLOTS1 = TILES1 * P
UNIT_EPS, TOPK_EPS = 1e-8, 1e-8

CONST_COLS = {}


def constants():
    p = np.arange(P)
    parts = [
        ("ident", np.eye(P)),
        ("before", (p[:, None] < p[None, :])),
        ("upto", (p[:, None] <= p[None, :])),
        ("ones", np.ones((P, P))),
        ("head_scale", np.stack([(p // HD % 2 == e) * HD ** -0.5 for e in range(2)], 1)),
        ("iota0", np.tile(np.arange(E0), (P, 1))),
        ("iota0_low", np.tile(np.arange(E0) - E0, (P, 1))),
        ("iota1_low", np.tile(np.arange(E1) - E1, (P, 1))),
        ("tile_start", np.tile(np.arange(TILES1) * P, (P, 1))),
    ]
    at = 0
    for name, a in parts:
        CONST_COLS[name] = (at, at + a.shape[1])
        at += a.shape[1]
    const = np.concatenate([a for _, a in parts], 1).astype(np.float32)
    n, f = np.arange(D), np.arange(P)
    ang = 2 * np.pi * (np.outer(n, f) % D) / D
    alt = (-1.0) ** n
    dft = np.concatenate([np.cos(ang), -np.sin(ang), alt[:, None]], 1)
    dft[:, P] = 0.0
    w = np.where(f == 0, 1.0, 2.0)[:, None] / D
    inv_im = -w * np.sin(ang.T)
    inv_im[0] = alt / D
    inv = np.stack([w * np.cos(ang.T), inv_im], 1)
    return const, dft.astype(np.float32), inv.astype(np.float32)


CONSTS = constants()


class Mark:

    def __init__(self, stage):
        self.stage, self.awaited, self.count = stage, False, 0


def named(marks):
    if isinstance(marks, Mark):
        return [marks]
    return [x for m in marks or () for x in named(m)]


class Queue:

    def __init__(self, name):
        self.name, self.steps = name, []

    def add(self, stage, issue, after, dma=False):
        waits = named(after)
        for m in waits:
            m.awaited = True
        mark = Mark(f"{self.name}_{stage}")
        self.steps.append((issue, waits, mark, dma))
        return mark

    def count(self):
        values = {}
        for _, _, mark, dma in self.steps:
            if dma or mark.awaited:
                values[mark.stage] = values.get(mark.stage, 0) + (16 if dma else 1)
                mark.count = values[mark.stage]
        return values

    def emit(self, engine, sems):
        seen = {}
        for issue, waits, mark, dma in self.steps:
            for m in waits:
                if seen.get(m.stage, 0) < m.count:
                    engine.wait_ge(sems[m.stage], m.count)
                    seen[m.stage] = m.count
            instruction = issue(engine)
            if dma:
                instruction.then_inc(sems[mark.stage], 16)
            elif mark.awaited:
                instruction.then_inc(sems[mark.stage], 1)


def build(nc, a, out, stop_at=None):
    pe, dve, act, pool, sp = Queue("pe"), Queue("dve"), Queue("act"), Queue("pool"), Queue("sp")

    def mm(stage, o, lhsT, rhs, start, stop, after=()):
        return pe.add(stage, lambda e: e.matmul(o, lhsT, rhs, start=start, stop=stop), after)

    def turn(stage, o, i, ident, after=()):
        return pe.add(stage, lambda e: e.transpose(o, i, ident), after)

    def activate(stage, o, i, func, after=(), bias=0.0, scale=1.0):
        if func == ACT.Copy:
            return act.add(stage, lambda e: e.activation(o, i, func), after)
        return act.add(stage, lambda e: e.activation(o, i, func, bias=bias, scale=scale), after)

    def tt(stage, o, i0, i1, op, after=(), on=dve):
        return on.add(stage, lambda e: e.tensor_tensor(o, i0, i1, op), after)

    def ts(stage, o, i, s1, s2, op0, op1=None, after=(), on=dve):
        if op1 is None:
            return on.add(stage, lambda e: e.tensor_scalar(o, i, s1, None, op0), after)
        return on.add(stage, lambda e: e.tensor_scalar(o, i, s1, s2, op0, op1), after)

    def stt(stage, o, i0, s, i1, op0, op1, after=()):
        return dve.add(stage, lambda e: e.scalar_tensor_tensor(out=o, in0=i0, scalar=s, in1=i1, op0=op0, op1=op1),
                       after)

    def reduce(stage, o, i, op, after=()):
        return dve.add(stage, lambda e: e.tensor_reduce(o, i, AX.X, op), after)

    def copy(stage, o, i, after=(), on=dve):
        return on.add(stage, lambda e: e.tensor_copy(o, i), after)

    def recip(stage, o, i, after=()):
        return dve.add(stage, lambda e: e.reciprocal(o, i), after)

    def fill(stage, o, value, after=(), on=dve):
        return on.add(stage, lambda e: e.memset(o, value), after)

    def dma(stage, o, i, after=(), on=sp):
        return on.add(stage, lambda e: e.dma_start(o, i), after, dma=True)

    top = [16512]

    def place(name, shape, dtype=F32):
        size = 4
        for n in shape[1:]:
            size *= n
        t = nc.alloc_sbuf_tensor_at(name, list(shape), dtype, offset=top[0])
        top[0] += -(-size // 32) * 32
        assert top[0] <= 229344, (name, top[0])
        return t

    PS = nc.alloc_psum_tensor("PS", [P, 8, 512], F32)
    bank_busy = [[] for _ in range(8)]

    def dram(name, shape):
        return nc.dram_tensor(name, shape, F32, kind="Internal").ap()

    table0, result0 = dram("table0", (SLOTS0, D)), dram("result0", (SLOTS0, D))
    table1, result1 = dram("table1", (SLOTS1, D)), dram("result1", (SLOTS1, D))
    x1_dram, s1_dram = dram("x1_dram", (T, D)), dram("s1_dram", (T, D))

    const = place("const", [P, CONSTS[0].shape[1]])
    C = {n: const[:, lo:hi] for n, (lo, hi) in CONST_COLS.items()}
    const_in = dma("const", const[:, :], a["const"])
    ident = C["ident"]
    gate_eff = place("gate_eff", [P, NT])
    slot_put = place("slot_put", [P, NT], I32)
    slot_get = place("slot_get", [P, NT], I32)
    slot1 = place("slot1", [P, TOPK, NT], I32)
    weight1 = place("weight1", [P, TOPK, NT])
    tile_expert = place("tile_expert", [1, TILES1], I32)
    stats = place("stats", [P, NT, 6])
    mean_var = place("mean_var", [P, NT, 2])
    rstd = place("rstd", [P, NT])
    persistent_top = top[0]
    X = place("X", [P, NT, D])
    XN = place("XN", [P, NT, D])
    after_xn = top[0]
    XT = place("XT", [P, KD, T])
    after_xt = top[0]
    S = place("S", [P, NT, D])
    work = top[0]

    zeros = S[:, 0:8, :].rearrange("p t d -> p (t d)")
    zeroed = fill("zero", zeros, 0.0, on=pool)
    table_zeroed = [None, None]
    for n, (table, slots) in enumerate(((table0, SLOTS0), (table1, SLOTS1))):
        flat = table.rearrange("(p r) d -> p (r d)", p=P)
        width = slots * D // P
        for lo in range(0, width, 8 * D):
            hi = min(lo + 8 * D, width)
            table_zeroed[n] = dma(f"zero{n}", flat[:, lo:hi], zeros[:, 0:hi - lo], [zeroed], on=pool)

    x_view = a["x"].rearrange("(t p) d -> p t d", p=P)
    x_in = [dma(f"x{i}", X[:, 4 * i:4 * i + 4, :], x_view[:, 4 * i:4 * i + 4, :]) for i in range(NT // 4)]

    def layernorm(L, ready):
        normed, turned = [None] * NT, []
        for g in range(0, NT, 8):
            for t in range(g, g + 8):
                s = dve.add("ln_stat", lambda e, t=t: e.bn_stats(stats[:, t, :], X[:, t, :]), ready(t))
                m = dve.add("ln_aggr", lambda e, t=t: e.bn_aggr(mean_var[:, t, :], stats[:, t, :]), [s])
            r = ts("ln_var", rstd[:, g:g + 8], mean_var[:, g:g + 8, 1], LN_EPS, None, ALU.add, after=[m])
            r = activate("ln_sqrt", rstd[:, g:g + 8], rstd[:, g:g + 8], ACT.Sqrt, [r])
            r = recip("ln_rstd", rstd[:, g:g + 8], rstd[:, g:g + 8], [r])
            for t in range(g, g + 8):
                normed[t] = ts("ln_xn", XN[:, t, :], X[:, t, :], mean_var[:, t, 0:1], rstd[:, t:t + 1],
                               ALU.subtract, ALU.mult, [r])
            for t in range(g, g + 8, 2):
                b = (t // 2) % 2
                out_v = PS[:, b, :].rearrange("p (k n) -> p k n", k=KD)
                for k in range(KD):
                    for j in range(2):
                        m = turn("ln_turn", out_v[:, k, j * P:(j + 1) * P], XN[:, t + j, k * P:(k + 1) * P], ident,
                                 [normed[t + j], const_in, bank_busy[b]])
                c = activate("ln_xt", XT[:, :, t * P:(t + 2) * P], out_v, ACT.Copy, [m])
                bank_busy[b] = [c]
                turned.append(c)
        return normed, turned

    def router_logits(L, router, router_in, n_e, turned, banks):
        per = 512 // n_e
        marks = []
        for i, b in enumerate(banks):
            for t in range(i * per, min((i + 1) * per, NT)):
                for k in range(KD):
                    o = PS[:, b, (t - i * per) * n_e:(t - i * per + 1) * n_e]
                    m = mm("router", o, XT[:, k, t * P:(t + 1) * P], router[:, k, :], k == 0, k == KD - 1,
                           [turned[t // 2], router_in, bank_busy[b]])
            marks.append(m)
        return marks

    def over_experts(v, n_e):
        return v.unsqueeze(2).to_broadcast([P, NT, n_e])

    def over_tiles(v, n_e):
        return v.unsqueeze(1).to_broadcast([P, NT, n_e])

    def first_best(scores, best, iota_low, n_e, tmp, hot, first, ready):
        m = tt("route", tmp, scores, over_experts(best, n_e), ALU.is_equal, [ready])
        m = stt("route", tmp, tmp, -float(n_e), over_tiles(iota_low, n_e), ALU.mult, ALU.add, [m])
        m = reduce("route", first, tmp, ALU.min, [m])
        m = ts("route", first, first, float(n_e), None, ALU.add, after=[m])
        return tt("route", hot, over_tiles(iota_low, n_e), over_experts(first, n_e), ALU.is_equal, [m])

    def count_before(hot, n_e, hot_ready, banks, reset, reset_ready, totals, running, pos):
        w = NT * n_e
        flat = hot.rearrange("p t e -> p (t e)")
        n = -(-w // 512)
        m = None
        for i in range(n):
            lo, hi = i * 512, min((i + 1) * 512, w)
            m = mm("count", PS[:, banks[i], 0:hi - lo], C["before"], flat[:, lo:hi], True, True,
                   [hot_ready, const_in, bank_busy[banks[i]]])
            m = mm("count", PS[:, banks[n + i], 0:hi - lo], C["ones"], flat[:, lo:hi], True, True,
                   [bank_busy[banks[n + i]]])
        tot_te, pos_flat = totals.rearrange("p e t -> p t e"), pos.rearrange("p t e -> p (t e)")
        per = 512 // n_e
        for i in range(n):
            t0, t1 = i * per, min((i + 1) * per, NT)
            src = PS[:, banks[n + i], 0:(t1 - t0) * n_e].rearrange("p (t e) -> p t e", e=n_e)
            c = copy("route", tot_te[:, t0:t1, :], src, [m])
            bank_busy[banks[n + i]] = [c]
        f = lambda v: v.rearrange("p e t -> p (e t)")
        s = dve.add("route", lambda e: e.tensor_tensor_scan(f(running), f(reset), f(totals), 0.0,
                                                            ALU.mult, ALU.add), [c, reset_ready])
        d = tt("route", f(running), f(running), f(totals), ALU.subtract, [s])
        run_te = running.rearrange("p e t -> p t e")
        for i in range(n):
            t0, t1 = i * per, min((i + 1) * per, NT)
            src = PS[:, banks[i], 0:(t1 - t0) * n_e].rearrange("p (t e) -> p t e", e=n_e)
            c = tt("route", pos[:, t0:t1, :], src, run_te[:, t0:t1, :], ALU.add, [d])
            bank_busy[banks[i]] = [c]
        return c

    def make_reset(reset, after):
        m = fill("route", reset, 1.0, after)
        return fill("route", reset[:, :, 0:1], 0.0, [m])

    top[0] = work
    router0 = place("router0", [P, KD, E0])
    router0_in = dma("router0", router0[:, :, :], a["w_router"].rearrange("(k p) e -> p k e", p=P))
    l0_work = top[0]
    normed0, turned0 = layernorm(0, lambda t: [x_in[t // 4]])
    lg_marks = router_logits(0, router0, router0_in, E0, turned0, [2, 3])

    score = place("score0", [P, NT, E0])
    tmp0 = place("tmp0", [P, NT, E0])
    hot0 = place("hot0", [P, NT, E0])
    totals0 = place("totals0", [P, E0, NT])
    running0 = place("running0", [P, E0, NT])
    reset0 = place("reset0", [P, E0, NT])
    best0 = place("best0", [P, NT])
    first0 = place("first0", [P, NT])
    pos0 = place("pos0", [P, NT])
    taken0 = place("taken0", [P, NT])
    routing0_top = top[0]
    per = 512 // E0
    for i in range(2):
        m = copy("route", score[:, i * per:(i + 1) * per, :],
                 PS[:, 2 + i, :].rearrange("p (t e) -> p t e", e=E0), [lg_marks[i]])
        bank_busy[2 + i] = [m]
    reset_ready = make_reset(reset0[:, :, :], [])
    mb = reduce("route", best0[:, :], score[:, :, :], ALU.max, [m])
    hot_ready = first_best(score[:, :, :], best0[:, :], C["iota0_low"], E0, tmp0[:, :, :], hot0[:, :, :],
                           first0[:, :], mb)
    m = tt("route", score[:, :, :], score[:, :, :], over_experts(best0[:, :], E0), ALU.subtract, [hot_ready])
    m = activate("route_exp", score[:, :, :], score[:, :, :], ACT.Exp, [m])
    m = reduce("route", gate_eff[:, :], score[:, :, :], ALU.add, [m])
    gate_ready = recip("route", gate_eff[:, :], gate_eff[:, :], [m])
    m = count_before(hot0[:, :, :], E0, hot_ready, [4, 5, 6, 7], reset0[:, :, :], reset_ready,
                     totals0[:, :, :], running0[:, :, :], tmp0[:, :, :])
    m = tt("route", tmp0[:, :, :], tmp0[:, :, :], hot0[:, :, :], ALU.mult, [m])
    m = reduce("route", pos0[:, :], tmp0[:, :, :], ALU.add, [m])
    tk = ts("route", taken0[:, :], pos0[:, :], float(CAP), None, ALU.is_lt, after=[m])
    m = stt("route", pos0[:, :], first0[:, :], float(CAP), pos0[:, :], ALU.mult, ALU.add, [tk])
    m = ts("route", pos0[:, :], pos0[:, :], float(SLOTS0), None, ALU.add, after=[m])
    m2 = tt("route", gate_eff[:, :], gate_eff[:, :], taken0[:, :], ALU.mult, [gate_ready, tk])
    gate0_ready = m2
    m = stt("route", pos0[:, :], taken0[:, :], -float(2 * SLOTS0), pos0[:, :], ALU.mult, ALU.add, [m, m2])
    m = ts("route", pos0[:, :], pos0[:, :], float(2 * SLOTS0), None, ALU.add, after=[m])
    put_ready = copy("route", slot_put[:, :], pos0[:, :], [m])
    m = ts("route", pos0[:, :], pos0[:, :], float(SLOTS0 - 1), None, ALU.min, after=[m])
    get_ready = copy("route", slot_get[:, :], pos0[:, :], [m])

    def scatter(stage, table, slots, idx, row, after):
        return pool.add(stage, lambda e: e.indirect_dma_start(
            out=table, out_offset=bass.IndirectOffsetOnAxis(ap=idx, axis=0), in_=row, in_offset=None,
            bounds_check=slots - 1, oob_is_err=False), after, dma=True)

    def gather(stage, table, slots, idx, row, after):
        return pool.add(stage, lambda e: e.indirect_dma_start(
            out=row, out_offset=None, in_=table, in_offset=bass.IndirectOffsetOnAxis(ap=idx, axis=0),
            bounds_check=slots - 1, oob_is_err=False), after, dma=True)

    for t in range(NT):
        scattered0 = scatter("scatter0", table0, SLOTS0, slot_put[:, t:t + 1], XN[:, t, :],
                             [put_ready, normed0[t], table_zeroed[0]])

    UNITS, UW, UT = NT // 2, 4, 2 * P
    top[0] = l0_work
    qkv_w = place("qkv_w", [P, KD, 3 * D])
    proj_w = place("proj_w", [P, 2, D])
    qkv_b = place("qkv_b", [P, 3 * KD])
    q_bias = place("q_bias", [P, 2, KD])
    v_bias = place("v_bias", [P, D])
    proj_b = place("proj_b", [P, D])
    rel = place("rel", [P, 4, KD, WIN])
    Q2 = place("Q2", [P, 2, KD, UW, 2, WIN])
    KT = place("KT", [P, 2, KD, UT])
    V = place("V", [P, 2, 2, PAIRS, 2 * HD + 1])
    sc = place("sc", [P, 2, KD, UW, WIN])
    sc_max = place("sc_max", [P, 2, KD, UW])
    prob = place("prob", [P, 2, KD, UW, WIN])
    PT = place("PT", [P, 4, KD, 2, P])
    inv_sum = place("inv_sum", [P, 2, PAIRS])
    O = place("O", [P, UW, PAIRS, HD])
    OT = place("OT", [P, 2, UT])
    w_after = [put_ready, get_ready, gate0_ready]
    qkv_w_in = dma("qkv_w", qkv_w[:, :, :], a["qkv_w"].rearrange("(k p) n -> p k n", p=P), w_after)
    attn_in = [dma("attn_w", proj_w[:, :, :], a["proj_w"], w_after),
               dma("attn_w", qkv_b[:, :], a["qkv_b"], w_after),
               dma("attn_w", v_bias[:, :], a["v_b"].partition_broadcast(P), w_after),
               dma("attn_w", proj_b[:, :], a["proj_b"].partition_broadcast(P), w_after),
               dma("attn_w", rel[:, :, :, :], a["rel"], w_after)]
    attn_in = attn_in[-1]
    qb = None
    for e in range(2):
        qb = ts("q_bias", q_bias[:, e, :], qkv_b[:, 0:KD], C["head_scale"][:, e:e + 1], None, ALU.mult,
                after=[attn_in, const_in])
    v_ones = fill("v_ones", V[:, :, :, :, HD:HD + 1], 1.0, [attn_in])
    MISC = [4, 5]

    class Turns:
        n = 0

    def misc_bank():
        b = MISC[Turns.n % 2]
        Turns.n += 1
        return b

    qkv_done, scores_done = {}, {}
    q2_free, kt_free, v_free = [[], []], [[], []], [[], []]
    sc_free, prob_free = [[], []], [[], []]
    pt_free, o_free, ot_free = [], [], []
    attn_done = []

    def qkv(u):
        i = u % 2
        tok = slice(u * UT, (u + 1) * UT)
        done = []
        for which in range(2):
            b = misc_bank()
            for c in range(KD):
                for k in range(KD):
                    col = which * D + c * P
                    m = mm("qkv", PS[:, b, c * UT:(c + 1) * UT], qkv_w[:, k, col:col + P], XT[:, k, tok],
                           k == 0, k == KD - 1, [qkv_w_in, turned0[u], bank_busy[b]])
            for c in range(KD):
                src = PS[:, b, c * UT:(c + 1) * UT]
                if which == 0:
                    for e in range(2):
                        m2 = activate("q_out", Q2[:, i, c, :, e, :], src.rearrange("p (w q) -> p w q", w=UW),
                                      ACT.Identity, [m, qb, q2_free[i]], bias=q_bias[:, e, c:c + 1],
                                      scale=C["head_scale"][:, e:e + 1])
                else:
                    m2 = activate("k_out", KT[:, i, c, :], src, ACT.Identity, [m, attn_in, kt_free[i]],
                                  bias=qkv_b[:, KD + c:KD + c + 1])
            bank_busy[b] = [m2]
            done.append(m2)
        b = misc_bank()
        for j in range(2):
            for k in range(KD):
                m = mm("qkv", PS[:, b, j * D:(j + 1) * D], XT[:, k, (2 * u + j) * P:(2 * u + j + 1) * P],
                       qkv_w[:, k, 2 * D:3 * D], k == 0, k == KD - 1, [bank_busy[b]])
        for e in range(2):
            src = PS[:, b, :].rearrange("p (j r e h) -> p j r e h", j=2, r=PAIRS, e=2)[:, :, :, e, :]
            vb = v_bias[:, :].rearrange("p (r e h) -> p r e h", r=PAIRS, e=2)[:, :, e, :]
            for j in range(2):
                m2 = tt("v_out", V[:, i, j, :, e * (HD + 1):e * (HD + 1) + HD], src[:, j], vb, ALU.add,
                        [m, v_ones, v_free[i]])
        bank_busy[b] = [m2]
        qkv_done[u] = done + [m2]

    def scores(u):
        i = u % 2
        marks = []
        for g in range(4):
            for c in range(KD):
                for w in range(UW):
                    m = mm("scores", PS[:, g, (c * UW + w) * WIN:(c * UW + w + 1) * WIN],
                           Q2[32 * g:32 * g + 32, i, c, w, :, :].rearrange("p e q -> p (e q)"),
                           KT[32 * g:32 * g + 32, i, c, w * WIN:(w + 1) * WIN], True, True,
                           [qkv_done[u], bank_busy[g]])
            marks.append(m)
        q2_free[i] = [m]
        kt_free[i] = [m]
        probs = []
        for g in range(4):
            j = g % 2
            for c in range(KD):
                src = PS[:, g, c * UW * WIN:(c + 1) * UW * WIN].rearrange("p (w k) -> p w k", w=UW)
                m = tt("sc_bias", sc[:, j, c, :, :], src,
                       rel[:, g, c, :].unsqueeze(1).to_broadcast([P, UW, WIN]), ALU.add,
                       [marks[g], attn_in, sc_free[j]])
            bank_busy[g] = [m]
            flat = sc[:, j, :, :, :].rearrange("p c w k -> p (c w) k")
            mx = sc_max[:, j, :, :].rearrange("p c w -> p (c w)")
            m = reduce("sc_max", mx, flat, ALU.max, [m])
            m = tt("sc_sub", flat, flat, mx.unsqueeze(2).to_broadcast([P, KD * UW, WIN]), ALU.subtract, [m])
            m = activate("sc_exp", prob[:, j, :, :, :].rearrange("p c w k -> p (c w k)"),
                         sc[:, j, :, :, :].rearrange("p c w k -> p (c w k)"), ACT.Exp, [m, prob_free[j]])
            sc_free[j] = [m]
            b = misc_bank()
            for c in range(KD):
                for wp in range(2):
                    m2 = turn("p_turn", PS[:, b, (c * 2 + wp) * P:(c * 2 + wp + 1) * P],
                              prob[:, j, c, 2 * wp:2 * wp + 2, :].rearrange("p w k -> p (w k)"), ident,
                              [m, bank_busy[b]])
            prob_free[j] = [m2]
            m3 = activate("pt_out", PT[:, g, :, :, :].rearrange("p c w n -> p (c w n)"), PS[:, b, :], ACT.Copy,
                          [m2, pt_free[0] if pt_free else None])
            bank_busy[b] = [m3]
            probs.append(m3)
        scores_done[u] = probs

    def attend(u):
        i = u % 2
        norm = None
        for wp in range(2):
            for w2 in range(2):
                for g in range(4):
                    for c in range(KD):
                        pair = 4 * c + g
                        m = mm("pv", PS[:, 6 + w2, pair * (2 * HD + 1):(pair + 1) * (2 * HD + 1)],
                               PT[64 * w2:64 * w2 + 64, g, c, wp, :], V[64 * w2:64 * w2 + 64, i, wp, pair, :],
                               True, True, [scores_done[u], bank_busy[6], bank_busy[7]])
            av = PS[:, 6:8, 0:PAIRS * (2 * HD + 1)].rearrange("p w (r n) -> p w r n", r=PAIRS)
            r = recip("pv_inv", inv_sum[:, :, :], av[:, :, :, HD], [m, norm])
            for e in range(2):
                rows = slice(64 * e, 64 * e + 64)
                norm = tt("pv_norm", O[rows, 2 * wp:2 * wp + 2, :, :],
                          av[rows, :, :, e * (HD + 1):e * (HD + 1) + HD],
                          inv_sum[rows, :, :].unsqueeze(3).to_broadcast([64, 2, PAIRS, HD]), ALU.mult,
                          [r, o_free])
            bank_busy[6] = [norm]
            bank_busy[7] = [norm]
        v_free[i] = [m]
        pt_free[:] = [m]
        b = misc_bank()
        for w in range(UW):
            m = turn("o_turn", PS[:, b, w * P:(w + 1) * P], O[:, w, :, :].rearrange("p r h -> p (r h)"), ident,
                     [norm, bank_busy[b]])
        o_free[:] = [m]
        m2 = activate("ot_out", OT[:, :, :].rearrange("p e (w q) -> p w e q", w=UW),
                      PS[:, b, :].rearrange("p (w e q) -> p w e q", w=UW, e=2), ACT.Copy, [m] + ot_free)
        bank_busy[b] = [m2]
        b = misc_bank()
        for j in range(2):
            for e in range(2):
                m = mm("proj", PS[:, b, j * D:(j + 1) * D], OT[:, e, j * P:(j + 1) * P], proj_w[:, e, :],
                       e == 0, e == 1, [m2, bank_busy[b]])
        ot_free[:] = [m]
        m3 = tt("s_out", S[:, 2 * u:2 * u + 2, :], PS[:, b, :].rearrange("p (j d) -> p j d", j=2),
                proj_b[:, :].unsqueeze(1).to_broadcast([P, 2, D]), ALU.add, [m, table_zeroed])
        bank_busy[b] = [m3]
        attn_done.append(m3)

    qkv(0)
    for u in range(UNITS):
        scores(u)
        if u + 1 < UNITS:
            qkv(u + 1)
        attend(u)

    top[0] = l0_work
    GROUP = 4
    GT = GROUP * CAP // P
    rows0 = place("rows0", [P, 2, GT, D])
    rowsT = place("rowsT", [P, 2, KD, GROUP * CAP])
    wgt0 = place("wgt0", [P, 2, 3, KD, F0])
    silu0 = place("silu0", [P, 2, KD, CAP])
    hT0 = place("hT0", [P, 2, KD, CAP])
    y0 = place("y0", [P, 2, 2, D])
    l0_free = attn_done[-1:] + [ot_free[0]]
    w_free, rows_free, rowsT_free = [l0_free] * 2, [l0_free] * 2, [l0_free] * 2
    silu_free, h_free, y_free = [l0_free] * 2, [l0_free] * 2, [l0_free] * 2
    y_written = []
    tail = CAP - P
    for grp in range(E0 // GROUP):
        gi = grp % 2
        base = grp * GROUP * CAP
        rows_in = dma(f"rows0_{gi}", rows0[:, gi, :, :],
                      table0[base:base + GT * P, :].rearrange("(t p) d -> p t d", p=P),
                      [scattered0, rows_free[gi]])
        for t in range(0, GT, 2):
            n = min(2, GT - t)
            b = (t // 2) % 2
            o = PS[:, b, :].rearrange("p (k n) -> p k n", k=KD)
            for k in range(KD):
                for j in range(n):
                    m = turn("rows_turn", o[:, k, j * P:(j + 1) * P], rows0[:, gi, t + j, k * P:(k + 1) * P], ident,
                             [rows_in, bank_busy[b]])
            rt = activate("rowsT_out", rowsT[:, gi, :, t * P:(t + n) * P], o[:, :, 0:n * P], ACT.Copy,
                          [m, rowsT_free[gi]])
            bank_busy[b] = [rt]
        rows_free[gi] = [m]
        for j in range(GROUP):
            ex = grp * GROUP + j
            i = ex % 2
            for n, name in enumerate(("w_gate", "w_up", "w_down")):
                w_in = dma(f"w0_{i}", wgt0[:, i, n, :, :], a[name][ex].rearrange("(k p) n -> p k n", p=P), w_free[i])
            g_b, u_b, y_b = 2 + i, 4 + i, 6 + i
            for n, b in enumerate((g_b, u_b)):
                for f in range(KD):
                    for k in range(KD):
                        m = mm("gate_up", PS[:, b, f * CAP:(f + 1) * CAP], wgt0[:, i, n, k, f * P:(f + 1) * P],
                               rowsT[:, gi, k, j * CAP:(j + 1) * CAP], k == 0, k == KD - 1,
                               [w_in, rt, bank_busy[b]])
            both = lambda b: PS[:, b, 0:KD * CAP].rearrange("p (f n) -> p f n", f=KD)
            s = activate("silu0", silu0[:, i, :, :], both(g_b), ACT.Silu, [m, silu_free[i]])
            bank_busy[g_b] = [s]
            h = tt("h0", hT0[:, i, :, :], silu0[:, i, :, :], both(u_b), ALU.mult, [s, h_free[i]])
            bank_busy[u_b] = [h]
            silu_free[i] = [h]
            for f in range(KD):
                m = mm("down0", PS[:, y_b, 0:D], hT0[:, i, f, 0:P], wgt0[:, i, 2, f, :], f == 0, f == KD - 1,
                       [h, bank_busy[y_b]])
            for f in range(KD):
                m = mm("down0", PS[0:tail, y_b, D:2 * D], hT0[:, i, f, P:CAP], wgt0[:, i, 2, f, :], f == 0,
                       f == KD - 1)
            w_free[i] = [m]
            h_free[i] = [m]
            c1 = copy("y0", y0[:, i, 0, :], PS[:, y_b, 0:D], [m, y_free[i]])
            c2 = copy("y0", y0[0:tail, i, 1, :], PS[0:tail, y_b, D:2 * D], [])
            bank_busy[y_b] = [c2]
            at = ex * CAP
            dma(f"y0_{i}", result0[at:at + P, :], y0[:, i, 0, :], [c2])
            d2 = dma(f"y0_{i}", result0[at + P:at + CAP, :], y0[0:tail, i, 1, :], [c2])
            y_free[i] = [d2]
        rowsT_free[gi] = [m]
    y_written = y_free[0] + y_free[1]

    top[0] = l0_work
    got0 = place("got0", [P, 2, 4, D])
    got_free = [[m], [m]]
    x1_ready = []
    x1_view = x1_dram.rearrange("(t p) d -> p t d", p=P)
    for q in range(NT // 4):
        i = q % 2
        for j in range(4):
            t = 4 * q + j
            gm = gather(f"got0_{i}", result0, SLOTS0, slot_get[:, t:t + 1], got0[:, i, j, :],
                        [get_ready, y_written, got_free[i]])
        for j in range(4):
            t = 4 * q + j
            m = stt("mix0", got0[:, i, j, :], got0[:, i, j, :], gate_eff[:, t:t + 1], XN[:, t, :], ALU.mult, ALU.add,
                    [gm, gate0_ready])
        m = activate("silu_mix0", got0[:, i, :, :], got0[:, i, :, :], ACT.Silu, [m])
        four = slice(4 * q, 4 * q + 4)
        m = tt("mix0", got0[:, i, :, :], got0[:, i, :, :], S[:, four, :], ALU.mult, [m, attn_done[-1]])
        m = tt("mix0", X[:, four, :], X[:, four, :], got0[:, i, :, :], ALU.add, [m])
        got_free[i] = [m]
        x1_saved = dma("x1_save", x1_view[:, four, :], X[:, four, :], [m])
        x1_ready.append(m)

    out_view = out.rearrange("(t p) d -> p t d", p=P)
    if stop_at == "layer0":
        finish = [dma("out", out_view, X[:, :, :], [x1_ready[-1]]), x1_saved]
        return replay(nc, (pe, dve, act, pool, sp), finish + y_written + table_zeroed, sp)

    top[0] = work
    router1 = place("router1", [P, KD, E1])
    router1_b = place("router1_b", [P, E1])
    sc1 = place("sc1", [P, NT, E1])
    prob1 = place("prob1", [P, NT, E1])
    tmp1 = place("tmp1", [P, NT, E1])
    hot1 = place("hot1", [P, TOPK, NT, E1])
    both1 = place("both1", [P, NT, E1])
    totals1 = place("totals1", [P, E1, NT])
    running1 = place("running1", [P, E1, NT])
    reset1 = place("reset1", [P, E1, NT])
    best1 = place("best1", [P, TOPK, NT])
    first1 = place("first1", [P, NT])
    sum1 = place("sum1", [P, NT])
    pad_i = place("pad_i", [P, E1], I32)
    pad_f = place("pad_f", [P, E1])
    pad_end = place("pad_end", [P, E1])
    pad_base = place("pad_base", [P, E1])
    owner = place("owner", [P, TILES1, E1])
    owner_f = place("owner_f", [P, TILES1])
    l0_end = [x1_ready[-1]]
    router1_in = [dma("router1", router1[:, :, :], a["Wg"].rearrange("(k p) e -> p k e", p=P), l0_end),
                  dma("router1", router1_b[:, :], a["bg"].partition_broadcast(P), l0_end)][-1]
    normed1, turned1 = layernorm(1, lambda t: [x1_ready[t // 4]])
    lg = router_logits(1, router1, router1_in, E1, turned1, [2])
    m = tt("route", sc1[:, :, :], PS[:, 2, 0:NT * E1].rearrange("p (t e) -> p t e", e=E1),
           over_tiles(router1_b[:, :], E1), ALU.add, [lg[0]])
    bank_busy[2] = [m]
    m = reduce("route", first1[:, :], sc1[:, :, :], ALU.max, [m])
    m = tt("route", sc1[:, :, :], sc1[:, :, :], over_experts(first1[:, :], E1), ALU.subtract, [m])
    m = activate("route_exp", prob1[:, :, :], sc1[:, :, :], ACT.Exp, [m])
    m = reduce("route", sum1[:, :], prob1[:, :, :], ALU.add, [m])
    m = recip("route", sum1[:, :], sum1[:, :], [m])
    m = tt("route", prob1[:, :, :], prob1[:, :, :], over_experts(sum1[:, :], E1), ALU.mult, [m])
    for k in range(TOPK):
        m = reduce("route", best1[:, k, :], prob1[:, :, :], ALU.max, [m])
        m = first_best(prob1[:, :, :], best1[:, k, :], C["iota1_low"], E1, tmp1[:, :, :], hot1[:, k, :, :],
                       first1[:, :], m)
        if k == 0:
            m = stt("route", prob1[:, :, :], hot1[:, k, :, :], -2.0, prob1[:, :, :], ALU.mult, ALU.add, [m])
    hot1_ready = tt("route", both1[:, :, :], hot1[:, 0, :, :], hot1[:, 1, :, :], ALU.add, [m])
    m = tt("route", sum1[:, :], best1[:, 0, :], best1[:, 1, :], ALU.add, [hot1_ready])
    m = ts("route", sum1[:, :], sum1[:, :], TOPK_EPS, None, ALU.add, after=[m])
    m = recip("route", sum1[:, :], sum1[:, :], [m])
    for k in range(TOPK):
        weight1_ready = tt("route", weight1[:, k, :], best1[:, k, :], sum1[:, :], ALU.mult, [m])
    reset_ready = make_reset(reset1[:, :, :], [x1_ready[-1]])
    m = count_before(both1[:, :, :], E1, hot1_ready, [3, 4], reset1[:, :, :], reset_ready,
                     totals1[:, :, :], running1[:, :, :], tmp1[:, :, :])
    m = tt("route", pad_f[:, :], running1[:, :, NT - 1], totals1[:, :, NT - 1], ALU.add, [m])
    m = ts("route", pad_f[:, :], pad_f[:, :], float(P - 1), None, ALU.add, after=[m])
    m = copy("route", pad_i[:, :], pad_f[:, :], [m])
    m = ts("route", pad_i[:, :], pad_i[:, :], 7, 7, ALU.logical_shift_right, ALU.logical_shift_left, after=[m])
    m = copy("route", pad_f[:, :], pad_i[:, :], [m])
    ones8 = C["ones"][:, 0:E1]
    m = dve.add("route", lambda e: e.tensor_tensor_scan(pad_end[:, :], ones8, pad_f[:, :], 0.0, ALU.mult, ALU.add),
                [m, const_in])
    m = tt("route", pad_base[:, :], pad_end[:, :], pad_f[:, :], ALU.subtract, [m])
    pos_ready = tt("route", both1[:, :, :], tmp1[:, :, :], over_tiles(pad_base[:, :], E1), ALU.add, [m])
    m = pos_ready
    for k in range(TOPK):
        m = tt("route", tmp1[:, :, :], both1[:, :, :], hot1[:, k, :, :], ALU.mult, [m])
        m = reduce("route", first1[:, :], tmp1[:, :, :], ALU.add, [m])
        m = copy("route", slot1[:, k, :], first1[:, :], [m])
    slot1_ready = m
    m = tt("route", owner[:, :, :], pad_end[:, :].unsqueeze(1).to_broadcast([P, TILES1, E1]),
           C["tile_start"].unsqueeze(2).to_broadcast([P, TILES1, E1]), ALU.is_le, [m])
    m = reduce("route", owner_f[:, :], owner[:, :, :], ALU.add, [m])
    m = ts("route", owner_f[:, :], owner_f[:, :], float(E1 - 1), None, ALU.min, after=[m])
    owner_ready = copy("route", tile_expert[:, :], owner_f[0:1, :], [m])
    for t in range(NT):
        for k in range(TOPK):
            scattered1 = scatter("scatter1", table1, SLOTS1, slot1[:, k, t:t + 1], XN[:, t, :],
                                 [slot1_ready, normed1[t], table_zeroed[1]])
    routing1_end = [owner_ready, weight1_ready, slot1_ready]

    top[0] = persistent_top
    W1 = place("W1", [P, E1, KD, F1])
    assert top[0] == after_xn
    w1_marks = []
    for ex in range(E1):
        w1_in = dma("w1", W1[:, ex, :, :], a["W1"][ex].rearrange("(k p) n -> p k n", p=P), [x1_saved, scattered1])
    top[0] = after_xt
    NB = D + 1
    dft = place("dft", [P, KD, NB])
    inv = place("inv", [P, 2, D])
    Wn = place("Wn", [P, KD, D])
    Wf = place("Wf", [P, 3, KD, NB])
    bn = place("bn", [P, 3, KD])
    bf = place("bf", [P, 3, 2])
    b_rep = place("b_rep", [P, KD, P])
    nyq_b = place("nyq_b", [P, 3])
    nyq = place("nyq", [P, 3, NT])
    nyq_abs = place("nyq_abs", [P, 3, NT])
    nyq_sum = place("nyq_sum", [P, NT])
    nyq_scan = place("nyq_scan", [P, NT])
    nyq_reset = place("nyq_reset", [P, NT])
    nyq_T = place("nyq_T", [NT, P])
    CH = 512
    Z = place("Z", [P, 2, 3, 2, CH])
    SQ = place("SQ", [P, 3, 2, CH])
    MAG = place("MAG", [P, 3, CH])
    PR = place("PR", [P, 4, CH])
    RUN = place("RUN", [P, 2, 2, CH])
    U = place("U", [P, 2, 2, CH])
    s1 = place("s1", [P, 2, 2, D])
    free1 = [attn_done[-1]] + l0_end + routing1_end
    dft_in = [dma("dft", dft[:, :, :], a["dft"].rearrange("(k p) n -> p k n", p=P), free1),
              dma("dft", inv[:, :, :], a["inv"], free1),
              dma("dft", bn[:, :, :], a["attn1_b"], free1)][-1]
    QQ, KK, VV = 0, 1, 2
    wf_ready, wn_free = None, free1
    for n, name in enumerate(("Wq", "Wk", "Wv")):
        wn_in = dma("wn", Wn[:, :, :], a[name].rearrange("(k p) n -> p k n", p=P), wn_free)
        for c in range(KD):
            for k in range(KD):
                m = mm("wf", PS[:, c, 0:NB], Wn[:, k, c * P:(c + 1) * P], dft[:, k, :], k == 0, k == KD - 1,
                       [wn_in, dft_in, bank_busy[c]])
            wf_ready = copy("wf_out", Wf[:, n, c, :], PS[:, c, 0:NB], [m])
            bank_busy[c] = [wf_ready]
        wn_free = [m]
        for part in range(2):
            for k in range(KD):
                m = mm("bf", PS[:, 2, 2 * n + part:2 * n + part + 1], dft[:, k, part * P:(part + 1) * P],
                       bn[:, n, k:k + 1], k == 0, k == KD - 1, [bank_busy[2]])
        r = copy("b_rep", b_rep[:, :, :], bn[:, n, :].unsqueeze(2).to_broadcast([P, KD, P]), [dft_in, m])
        for k in range(KD):
            m = mm("bf", PS[:, 2, 8 + n:9 + n], b_rep[:, k, :], dft[:, k, D:NB], k == 0, k == KD - 1, [r])
    copy("bf_out", bf[:, :, :], PS[:, 2, 0:6].rearrange("p (n r) -> p n r", n=3), [m])
    bf_ready = copy("bf_out", nyq_b[:, :], PS[:, 2, 8:11], [m])
    bank_busy[2] = [bf_ready]

    for t in range(NT):
        for k in range(KD):
            m = mm("nyq", PS[:, 3, 3 * t:3 * t + 3], XT[:, k, t * P:(t + 1) * P],
                   Wf[:, :, k, D:NB].rearrange("p n o -> p (n o)"), k == 0, k == KD - 1,
                   [wf_ready, turned1[t // 2], bank_busy[3]])
    m = tt("nyq", nyq[:, :, :], PS[:, 3, 0:3 * NT].rearrange("p (t n) -> p n t", n=3),
           nyq_b[:, :].unsqueeze(2).to_broadcast([P, 3, NT]), ALU.add, [m, bf_ready])
    bank_busy[3] = [m]
    m = stt("nyq", nyq_abs[:, :, :], nyq[:, :, :], -1.0, nyq[:, :, :], ALU.mult, ALU.max, [m])
    m = ts("nyq", nyq_abs[:, :, :], nyq_abs[:, :, :], UNIT_EPS, None, ALU.add, after=[m])
    m = recip("nyq", nyq_abs[:, :, :], nyq_abs[:, :, :], [m])
    m = tt("nyq", nyq[:, :, :], nyq[:, :, :], nyq_abs[:, :, :], ALU.mult, [m])
    m = tt("nyq", nyq_sum[:, :], nyq[:, KK, :], nyq[:, VV, :], ALU.mult, [m])
    mm("nyq", PS[:, 2, 0:NT], C["upto"], nyq_sum[:, :], True, True, [m, bank_busy[2]])
    m2 = mm("nyq", PS[:, 3, 0:NT], C["ones"], nyq_sum[:, :], True, True, [bank_busy[3]])
    r = fill("nyq", nyq_reset[:, :], 1.0, free1)
    r = fill("nyq", nyq_reset[:, :].rearrange("p (b t) -> p b t", b=BATCH)[:, :, 0:1], 0.0, [r])
    m = copy("nyq", nyq_sum[:, :], PS[:, 3, 0:NT], [m2])
    s = dve.add("nyq", lambda e: e.tensor_tensor_scan(nyq_scan[:, :], nyq_reset[:, :], nyq_sum[:, :], 0.0, ALU.mult,
                                                      ALU.add), [m, r])
    m = tt("nyq", nyq_scan[:, :], nyq_scan[:, :], nyq_sum[:, :], ALU.subtract, [s])
    m = tt("nyq", nyq_scan[:, :], PS[:, 2, 0:NT], nyq_scan[:, :], ALU.add, [m])
    bank_busy[2] = [m]
    m = tt("nyq", nyq_scan[:, :], nyq_scan[:, :], nyq[:, QQ, :], ALU.mult, [m])
    m = turn("nyq_turn", PS[0:NT, 3, 0:P], nyq_scan[:, :], ident, [m])
    nyq_ready = copy("nyq", nyq_T[:, :], PS[0:NT, 3, 0:P], [m])
    bank_busy[3] = [nyq_ready]

    banks = [0, 1, 2, 3, 4, 5]
    z_free, run_free, u_free, s1_free = [[], []], [[], []], [[], []], [[], []]
    pr_free, sq_free, mag_free = [], [], []
    run_last = None
    per_batch = SEQ // CH
    for ch in range(T // CH):
        i = ch % 2
        tok = slice(ch * CH, (ch + 1) * CH)
        z_ready, mag_ready = {}, {}
        for n in (KK, VV, QQ):
            sq = []
            for part in range(2):
                b = banks[2 * n + part]
                for k in range(KD):
                    m = mm("dft", PS[:, b, :], Wf[:, n, k, part * P:(part + 1) * P], XT[:, k, tok], k == 0,
                           k == KD - 1, [wf_ready, turned1[min(2 * ch + 1, len(turned1) - 1)], bank_busy[b]])
                bias = bf[:, n, part:part + 1]
                zz = activate("z", Z[:, i, n, part, :], PS[:, b, :], ACT.Identity, [m, bf_ready, z_free[i]], bias=bias)
                s = activate("zsq", SQ[:, n, part, :], PS[:, b, :], ACT.Square, [m, sq_free], bias=bias)
                bank_busy[b] = [s]
                sq.append(s)
            z_ready[n] = zz
            m = tt("mag", MAG[:, n, :], SQ[:, n, 0, :], SQ[:, n, 1, :], ALU.add, [sq[1], mag_free])
            if n == QQ:
                sq_free = [m]
            mag_ready[n] = activate("mag_sqrt", MAG[:, n, :], MAG[:, n, :], ACT.Sqrt, [m])
        z = lambda n, part: Z[:, i, n, part, :]
        m = ts("inv", MAG[:, VV, :], MAG[:, VV, :], UNIT_EPS, None, ALU.add, after=[mag_ready[VV]])
        m = stt("inv", MAG[:, KK, :], MAG[:, KK, :], UNIT_EPS, MAG[:, VV, :], ALU.add, ALU.mult, [m, mag_ready[KK]])
        m = recip("inv", MAG[:, KK, :], MAG[:, KK, :], [m])
        kr = tt("bind", z(KK, 0), z(KK, 0), MAG[:, KK, :], ALU.mult, [m, z_ready[KK]])
        ki = tt("bind", z(KK, 1), z(KK, 1), MAG[:, KK, :], ALU.mult, [m])
        w = [kr, ki, z_ready[VV]] + pr_free
        tt("bind", PR[:, 0, :], z(KK, 0), z(VV, 0), ALU.mult, w)
        m = tt("bind", PR[:, 1, :], z(KK, 1), z(VV, 1), ALU.mult, w)
        tt("bind", PR[:, 2, :], z(KK, 0), z(VV, 1), ALU.mult, w)
        m2 = tt("bind", PR[:, 3, :], z(KK, 1), z(VV, 0), ALU.mult, w)
        fresh = ch % per_batch == 0
        runs = []
        for part, (x0, x1, op, mk) in enumerate(((0, 1, ALU.subtract, m), (2, 3, ALU.add, m2))):
            initial = 0.0 if fresh else RUN[:, 1 - i, part, CH - 1:CH]
            runs.append(dve.add("running", lambda e, o=RUN[:, i, part, :], x0=x0, x1=x1, op=op, initial=initial:
                                e.tensor_tensor_scan(o, PR[:, x0, :], PR[:, x1, :], initial, ALU.add, op),
                                [mk, run_last, run_free[i]]))
        run_last = runs[1]
        m = ts("inv", MAG[:, QQ, :], MAG[:, QQ, :], UNIT_EPS, None, ALU.add, after=[mag_ready[QQ]])
        m = recip("inv", MAG[:, QQ, :], MAG[:, QQ, :], [m])
        tt("unbind", z(QQ, 0), z(QQ, 0), MAG[:, QQ, :], ALU.mult, [m, z_ready[QQ]])
        qi = tt("unbind", z(QQ, 1), z(QQ, 1), MAG[:, QQ, :], ALU.mult, [m])
        mag_free = [qi]
        w = [qi] + runs
        run = lambda part: RUN[:, i, part, :]
        tt("unbind", PR[:, 0, :], run(0), z(QQ, 0), ALU.mult, w)
        m = tt("unbind", PR[:, 1, :], run(1), z(QQ, 1), ALU.mult, w)
        tt("unbind", PR[:, 2, :], run(1), z(QQ, 0), ALU.mult, w)
        m2 = tt("unbind", PR[:, 3, :], run(0), z(QQ, 1), ALU.mult, w)
        run_free[i], z_free[i] = [m2], [m2]
        ur = tt("unbind", U[:, i, 0, :], PR[:, 0, :], PR[:, 1, :], ALU.add, [m, u_free[i]])
        ui = tt("unbind", U[:, i, 1, :], PR[:, 2, :], PR[:, 3, :], ALU.subtract, [m2, u_free[i]])
        pr_free = [ui]
        ny = dma(f"nyq_row{i}", U[0:1, i, 1, :].rearrange("o (t n) -> o t n", n=P),
                 nyq_T[4 * ch:4 * ch + 4, :], [nyq_ready, ui])
        for half in range(2):
            b = 6 + half
            for j in range(2):
                c0 = (2 * half + j) * P
                for part in range(2):
                    m = mm("idft", PS[:, b, j * D:(j + 1) * D], U[:, i, part, c0:c0 + P], inv[:, part, :],
                           part == 0, part == 1, [ur, ny, bank_busy[b]])
            c = activate("s1_out", s1[:, half, :, :].rearrange("p j d -> p (j d)"), PS[:, b, :], ACT.Copy,
                         [m, s1_free[half]])
            bank_busy[b] = [c]
            row = ch * CH + half * 2 * P
            sv = dma(f"s1_save{half}", s1_dram[row:row + 2 * P, :].rearrange("(t p) d -> p t d", p=P),
                     s1[:, half, :, :], [c])
            s1_free[half] = [sv]
        u_free[i] = [m]
    attn1_end = [m, pr_free[0], c]
    s1_saved = s1_free[0] + s1_free[1]

    top[0] = after_xn
    KF = F1 // P
    W2 = place("W2", [P, E1, KF, D])
    b1 = place("b1", [P, E1, F1])
    b2 = place("b2", [P, E1, D])
    xg = place("xg", [P, 3, D])
    xgT = place("xgT", [P, 2, KD, P])
    hid = place("hid", [P, 2, F1])
    hidT = place("hidT", [P, 2, KF, P])
    y1 = place("y1", [P, 2, D])
    free2 = attn1_end + s1_saved
    for ex in range(E1):
        w2_in = dma("w2", W2[:, ex, :, :], a["W2"][ex].rearrange("(k p) n -> p k n", p=P), free2)
    b_in = [dma("b12", b1[:, :, :], a["b1"].partition_broadcast(P), free2),
            dma("b12", b2[:, :, :], a["b2"].partition_broadcast(P), free2)][-1]
    xg_free, xgT_free, hid_free, hidT_free, y1_free = ([free2] * 3, [free2] * 2, [free2] * 2, [free2] * 2,
                                                        [free2] * 2)
    expert_on = {}

    def load_expert(queue, n):
        def issue(e):
            expert_on[queue.name] = e.value_load(tile_expert[0:1, n:n + 1], min_val=0, max_val=E1 - 1)
        return issue

    class Quiet:
        def then_inc(self, *_):
            raise AssertionError("a register load is not waited for")

    def on_expert(queue, stage, issue, after):
        return queue.add(stage, issue, after)

    xg_in, h_state = {}, {}

    def load_rows(n):
        xg_in[n] = dma(f"xg{n % 3}", xg[:, n % 3, :], table1[n * P:(n + 1) * P, :], [scattered1, xg_free[n % 3]])

    def first_matmul(n):
        i = n % 2
        for k in range(KD):
            m = turn("xg_turn", PS[:, 6, k * P:(k + 1) * P], xg[:, n % 3, k * P:(k + 1) * P], ident,
                     [xg_in[n], bank_busy[6]])
        xg_free[n % 3] = [m]
        xt = copy("xgT_out", xgT[:, i, :, :].rearrange("p k n -> p (k n)"), PS[:, 6, 0:KD * P], [m, xgT_free[i]])
        bank_busy[6] = [xt]
        pe.add("expert", load_expert(pe, n), [owner_ready])
        marks = []
        for half in range(2):
            b = 2 * i + half
            for k in range(KD):
                def issue(e, b=b, k=k, half=half):
                    ex = expert_on["pe"]
                    return e.matmul(PS[:, b, :], xgT[:, i, k, :],
                                    W1[:, bass.ds(ex, 1), k, half * 512:(half + 1) * 512].rearrange("p o n -> p (o n)"),
                                    start=(k == 0), stop=(k == KD - 1))
                m = pe.add("w1", issue, [xt, w1_in, bank_busy[b]])
            marks.append(m)
        xgT_free[i] = [m]
        dve.add("expert", load_expert(dve, n), [owner_ready])
        hs = []
        for half in range(2):
            b = 2 * i + half

            def issue(e, b=b, half=half):
                ex = expert_on["dve"]
                return e.tensor_tensor(hid[:, i, half * 512:(half + 1) * 512], PS[:, b, :],
                                       b1[:, bass.ds(ex, 1), half * 512:(half + 1) * 512].rearrange("p o n -> p (o n)"),
                                       ALU.add)
            m = dve.add("b1", issue, [marks[half], b_in, hid_free[i]])
            bank_busy[b] = [m]
            hs.append(activate("gelu", hid[:, i, half * 512:(half + 1) * 512], hid[:, i, half * 512:(half + 1) * 512],
                               ACT.Gelu_apprx_tanh, [m]))
        h_state[n] = hs

    def second_matmul(n):
        i = n % 2
        outs = []
        for half in range(2):
            b = 4 + half
            for j in range(4):
                c = half * 4 + j
                m = turn("h_turn", PS[:, b, j * P:(j + 1) * P], hid[:, i, c * P:(c + 1) * P], ident,
                         [h_state[n][half], bank_busy[b]])
            o = hidT[:, i, half * 4:half * 4 + 4, :].rearrange("p k n -> p (k n)")
            if half == 0:
                c = activate("hT_out", o, PS[:, b, :], ACT.Copy, [m, hidT_free[i]])
            else:
                c = copy("hT_out", o, PS[:, b, :], [m, hidT_free[i]])
            bank_busy[b] = [c]
            outs.append(c)
        hid_free[i] = [m]
        pe.add("expert", load_expert(pe, n), [owner_ready])
        for c in range(KF):
            def issue(e, c=c):
                ex = expert_on["pe"]
                return e.matmul(PS[:, 7, 0:D], hidT[:, i, c, :],
                                W2[:, bass.ds(ex, 1), c, :].rearrange("p o n -> p (o n)"),
                                start=(c == 0), stop=(c == KF - 1))
            m = pe.add("w2", issue, [outs[c // 4], w2_in, bank_busy[7]])
        hidT_free[i] = [m]
        dve.add("expert", load_expert(dve, n), [owner_ready])

        def issue(e):
            ex = expert_on["dve"]
            return e.tensor_tensor(y1[:, i, :], PS[:, 7, 0:D], b2[:, bass.ds(ex, 1), :].rearrange("p o n -> p (o n)"),
                                   ALU.add)
        m = dve.add("b2", issue, [m, b_in, y1_free[i]])
        bank_busy[7] = [m]
        y1_free[i] = [dma(f"y1_{i}", result1[n * P:(n + 1) * P, :], y1[:, i, :], [m])]

    for n in range(3):
        load_rows(n)
    for n in range(TILES1):
        first_matmul(n)
        if n:
            second_matmul(n - 1)
        if n + 3 < TILES1:
            load_rows(n + 3)
    second_matmul(TILES1 - 1)
    y1_written = y1_free[0] + y1_free[1]

    top[0] = persistent_top
    NB2 = 3
    xe = place("xe", [P, NB2, 4, D])
    se = place("se", [P, NB2, 4, D])
    ge = place("ge", [P, NB2, TOPK, 4, D])
    experts_done = [hidT_free[0], hidT_free[1]]
    e_free = [experts_done] * NB2
    s1_view = s1_dram.rearrange("(t p) d -> p t d", p=P)
    stored = []
    for q in range(NT // 4):
        i = q % NB2
        four = slice(4 * q, 4 * q + 4)
        dma(f"xe{i}", xe[:, i, :, :], x1_view[:, four, :], [x1_saved, e_free[i]])
        x_ready = dma(f"xe{i}", se[:, i, :, :], s1_view[:, four, :], [s1_saved, e_free[i]])
        for j in range(4):
            for k in range(TOPK):
                gm = gather(f"ge{i}", result1, SLOTS1, slot1[:, k, 4 * q + j:4 * q + j + 1], ge[:, i, k, j, :],
                            [y1_written, slot1_ready, e_free[i]])
        for j in range(4):
            t = 4 * q + j
            m = ts("mix1", ge[:, i, 0, j, :], ge[:, i, 0, j, :], weight1[:, 0, t:t + 1], None, ALU.mult,
                   after=[gm, weight1_ready])
            m = stt("mix1", ge[:, i, 0, j, :], ge[:, i, 1, j, :], weight1[:, 1, t:t + 1], ge[:, i, 0, j, :],
                    ALU.mult, ALU.add, [m])
        m = activate("silu1", ge[:, i, 0, :, :], ge[:, i, 0, :, :], ACT.Silu, [m])
        m = tt("mix1", ge[:, i, 0, :, :], ge[:, i, 0, :, :], se[:, i, :, :], ALU.mult, [m, x_ready])
        m = tt("mix1", xe[:, i, :, :], xe[:, i, :, :], ge[:, i, 0, :, :], ALU.add, [m])
        o = dma(f"out{i}", out_view[:, four, :], xe[:, i, :, :], [m])
        e_free[i] = [o]
        stored.append(o)
    replay(nc, (pe, dve, act, pool, sp), stored, sp)


def replay(nc, queues, finish, sp):
    sp.add("end", lambda e: e.nop(), finish)
    sems = {}
    for q in queues:
        for stage in q.count():
            sems[stage] = nc.alloc_semaphore(stage)
    pe, dve, act, pool, sp = queues
    with nc.Block() as block:
        block.tensor(lambda e: pe.emit(e, sems))
        block.vector(lambda e: dve.emit(e, sems))
        block.scalar(lambda e: act.emit(e, sems))
        block.gpsimd(lambda e: pool.emit(e, sems))
        block.sync(lambda e: sp.emit(e, sems))


STOP_AT = None


def kernel(**inputs):
    import concourse.bacc as bacc
    from concourse.bass_utils import run_bass_kernel_spmd

    as_np = {k: np.ascontiguousarray(v) for k, v in inputs.items()}
    const, dft, inv = CONSTS
    rel_at = np.arange(WIN)[:, None] - np.arange(WIN)[None, :] + WIN - 1
    rel = as_np["L0_attn_rel_bias"][rel_at].transpose(2, 0, 1)
    rel = rel.reshape(KD, 4, 2, WIN, WIN).transpose(2, 3, 1, 0, 4).reshape(P, 4, KD, WIN)
    proj = as_np["L0_attn_proj_w"].reshape(PAIRS, 2, HD, D).transpose(0, 2, 1, 3).reshape(P, 2, D)
    attn1_b = np.stack([as_np[f"L1_attn_b{c}"].reshape(KD, P).T for c in "qkv"], 1)
    data = {
        "const": const, "dft": dft, "inv": inv,
        "x": as_np["L0_attn_x"].reshape(T, D),
        "qkv_w": as_np["L0_attn_qkv_w"], "proj_w": proj, "proj_b": as_np["L0_attn_proj_b"],
        "qkv_b": as_np["L0_attn_qkv_b"].reshape(3 * KD, P).T, "v_b": as_np["L0_attn_qkv_b"][2 * D:],
        "rel": rel, "w_router": as_np["L0_ffn_w_router"], "w_gate": as_np["L0_ffn_w_gate"],
        "w_up": as_np["L0_ffn_w_up"], "w_down": as_np["L0_ffn_w_down"],
        "Wq": as_np["L1_attn_Wq"], "Wk": as_np["L1_attn_Wk"], "Wv": as_np["L1_attn_Wv"], "attn1_b": attn1_b,
        "Wg": as_np["L1_ffn_Wg"], "bg": as_np["L1_ffn_bg"], "W1": as_np["L1_ffn_W1"], "b1": as_np["L1_ffn_b1"],
        "W2": as_np["L1_ffn_W2"], "b2": as_np["L1_ffn_b2"],
    }
    nc = bacc.Bacc("TRN2", target_bir_lowering=False, num_devices=1)
    arrays, a = {}, {}
    for name, v in data.items():
        arrays[f"in_{name}"] = np.ascontiguousarray(v)
        a[name] = nc.dram_tensor(f"in_{name}", v.shape, mybir.dt.from_np(v.dtype), kind="ExternalInput").ap()
    out = nc.dram_tensor("out", (T, D), F32, kind="ExternalOutput").ap()
    build(nc, a, out, STOP_AT)
    r = run_bass_kernel_spmd(nc, [arrays], core_ids=[0])
    return r.results[0]["out"].reshape(BATCH, SEQ, D)
```

```python
import numpy as np
import concourse.bass as bass
from concourse import mybir

F32 = mybir.dt.float32
I32 = mybir.dt.int32
ALU = mybir.AluOpType
ACT = mybir.ActivationFunctionType
AX = mybir.AxisListType

P = 128
BATCH, SEQ, D = 4, 1024, 256
T = BATCH * SEQ
NT = T // P
KD = D // P
LN_EPS = 1e-5
HEADS, WIN = 16, 64
HD = D // HEADS
PAIRS = HEADS // 2
E0, F0 = 32, 256
CAP = -(-5 * T // (4 * E0))
SLOTS0 = E0 * CAP
E1, F1, TOPK = 8, 1024, 2
TILES1 = (T * TOPK + E1 * (P - 1)) // P
SLOTS1 = TILES1 * P
UNIT_EPS, TOPK_EPS = 1e-8, 1e-8

CONST_COLS = {}


def constants():
    p = np.arange(P)
    parts = [
        ("ident", np.eye(P)),
        ("before", (p[:, None] < p[None, :])),
        ("upto", (p[:, None] <= p[None, :])),
        ("ones", np.ones((P, P))),
        ("head_scale", np.stack([(p // HD % 2 == e) * HD ** -0.5 for e in range(2)], 1)),
        ("iota0", np.tile(np.arange(E0), (P, 1))),
        ("iota0_low", np.tile(np.arange(E0) - E0, (P, 1))),
        ("iota1_low", np.tile(np.arange(E1) - E1, (P, 1))),
        ("tile_start", np.tile(np.arange(TILES1) * P, (P, 1))),
    ]
    at = 0
    for name, a in parts:
        CONST_COLS[name] = (at, at + a.shape[1])
        at += a.shape[1]
    const = np.concatenate([a for _, a in parts], 1).astype(np.float32)
    n, f = np.arange(D), np.arange(P)
    ang = 2 * np.pi * (np.outer(n, f) % D) / D
    alt = (-1.0) ** n
    dft = np.concatenate([np.cos(ang), -np.sin(ang), alt[:, None]], 1)
    dft[:, P] = 0.0
    w = np.where(f == 0, 1.0, 2.0)[:, None] / D
    inv_im = -w * np.sin(ang.T)
    inv_im[0] = alt / D
    inv = np.stack([w * np.cos(ang.T), inv_im], 1)
    return const, dft.astype(np.float32), inv.astype(np.float32)


CONSTS = constants()


class Mark:

    def __init__(self, stage):
        self.stage, self.awaited, self.count = stage, False, 0


def named(marks):
    if isinstance(marks, Mark):
        return [marks]
    return [x for m in marks or () for x in named(m)]


class Queue:

    def __init__(self, name):
        self.name, self.steps = name, []

    def add(self, stage, issue, after, dma=False):
        waits = named(after)
        for m in waits:
            m.awaited = True
        mark = Mark(f"{self.name}_{stage}")
        self.steps.append((issue, waits, mark, dma))
        return mark

    def count(self):
        values = {}
        for _, _, mark, dma in self.steps:
            if dma or mark.awaited:
                values[mark.stage] = values.get(mark.stage, 0) + (16 if dma else 1)
                mark.count = values[mark.stage]
        return values

    def emit(self, engine, sems):
        seen = {}
        for issue, waits, mark, dma in self.steps:
            need = {}
            for m in waits:
                need[m.stage] = max(need.get(m.stage, 0), m.count)
            for name, count in need.items():
                if seen.get(name, 0) < count:
                    engine.wait_ge(sems[name], count)
                    seen[name] = count
            instruction = issue(engine)
            if dma:
                instruction.then_inc(sems[mark.stage], 16)
            elif mark.awaited:
                instruction.then_inc(sems[mark.stage], 1)


def build(nc, a, out, stop_at=None):
    pe, dve, act, pool, sp = Queue("pe"), Queue("dve"), Queue("act"), Queue("pool"), Queue("sp")

    def mm(stage, o, lhsT, rhs, start, stop, after=()):
        return pe.add(stage, lambda e: e.matmul(o, lhsT, rhs, start=start, stop=stop), after)

    def turn(stage, o, i, ident, after=()):
        return pe.add(stage, lambda e: e.transpose(o, i, ident), after)

    def activate(stage, o, i, func, after=(), bias=0.0, scale=1.0):
        if func == ACT.Copy:
            return act.add(stage, lambda e: e.activation(o, i, func), after)
        return act.add(stage, lambda e: e.activation(o, i, func, bias=bias, scale=scale), after)

    def tt(stage, o, i0, i1, op, after=(), on=dve):
        return on.add(stage, lambda e: e.tensor_tensor(o, i0, i1, op), after)

    def ts(stage, o, i, s1, s2, op0, op1=None, after=(), on=dve):
        if op1 is None:
            return on.add(stage, lambda e: e.tensor_scalar(o, i, s1, None, op0), after)
        return on.add(stage, lambda e: e.tensor_scalar(o, i, s1, s2, op0, op1), after)

    def stt(stage, o, i0, s, i1, op0, op1, after=()):
        return dve.add(stage, lambda e: e.scalar_tensor_tensor(out=o, in0=i0, scalar=s, in1=i1, op0=op0, op1=op1),
                       after)

    def reduce(stage, o, i, op, after=()):
        return dve.add(stage, lambda e: e.tensor_reduce(o, i, AX.X, op), after)

    def copy(stage, o, i, after=(), on=dve):
        return on.add(stage, lambda e: e.tensor_copy(o, i), after)

    def recip(stage, o, i, after=()):
        return dve.add(stage, lambda e: e.reciprocal(o, i), after)

    def fill(stage, o, value, after=(), on=dve):
        return on.add(stage, lambda e: e.memset(o, value), after)

    def dma(stage, o, i, after=(), on=sp):
        return on.add(stage, lambda e: e.dma_start(o, i), after, dma=True)

    top = [16512]

    def place(name, shape, dtype=F32):
        size = 4
        for n in shape[1:]:
            size *= n
        t = nc.alloc_sbuf_tensor_at(name, list(shape), dtype, offset=top[0])
        top[0] += -(-size // 32) * 32
        assert top[0] <= 229344, (name, top[0])
        return t

    PS = nc.alloc_psum_tensor("PS", [P, 8, 512], F32)
    bank_busy = [[] for _ in range(8)]

    def dram(name, shape):
        return nc.dram_tensor(name, shape, F32, kind="Internal").ap()

    table0, result0 = dram("table0", (SLOTS0, D)), dram("result0", (SLOTS0, D))
    table1, result1 = dram("table1", (SLOTS1, D)), dram("result1", (SLOTS1, D))
    x1_dram, s1_dram = dram("x1_dram", (T, D)), dram("s1_dram", (T, D))

    const = place("const", [P, CONSTS[0].shape[1]])
    C = {n: const[:, lo:hi] for n, (lo, hi) in CONST_COLS.items()}
    const_in = dma("const", const[:, :], a["const"])
    ident = C["ident"]
    gate_eff = place("gate_eff", [P, NT])
    slot_put = place("slot_put", [P, NT], I32)
    slot_get = place("slot_get", [P, NT], I32)
    slot1 = place("slot1", [P, TOPK, NT], I32)
    weight1 = place("weight1", [P, TOPK, NT])
    tile_expert = place("tile_expert", [1, TILES1], I32)
    stats = place("stats", [P, NT, 6])
    mean_var = place("mean_var", [P, NT, 2])
    rstd = place("rstd", [P, NT])
    zeros = place("zeros", [P, D])
    persistent_top = top[0]
    X = place("X", [P, NT, D])
    xn_base = top[0]
    XN = place("XN", [P, NT, D])
    after_xn = top[0]
    XT = place("XT", [P, NT // 2, KD, 2 * P])
    after_xt = top[0]
    s_base = top[0]
    S = place("S", [P, NT, D])
    work = top[0]

    x_view = a["x"].rearrange("(t p) d -> p t d", p=P)
    x_in = [dma(f"x{i}", X[:, 4 * i:4 * i + 4, :], x_view[:, 4 * i:4 * i + 4, :]) for i in range(NT // 4)]

    zeroed = fill("zero", zeros[:, :], 0.0, on=pool)

    def zero_table(n, table, slots, after):
        rows = slots // P
        return dma(f"zero{n}", table.rearrange("(p r) d -> p r d", p=P),
                   zeros[:, :].unsqueeze(1).to_broadcast([P, rows, D]), [zeroed, after], on=pool)

    table0_zeroed = zero_table(0, table0, SLOTS0, x_in[-1])
    table1_zeroed = zero_table(1, table1, SLOTS1, x_in[-1])

    normed, turned = [None] * NT, [None] * (NT // 2)

    def ln_statistics(g, ready):
        for t in range(g, g + 8):
            s = dve.add("ln_stat", lambda e, t=t: e.bn_stats(stats[:, t, :], X[:, t, :]), ready(t))
            m = dve.add("ln_aggr", lambda e, t=t: e.bn_aggr(mean_var[:, t, :], stats[:, t, :]), [s])
        r = ts("ln_var", rstd[:, g:g + 8], mean_var[:, g:g + 8, 1], LN_EPS, None, ALU.add, after=[m])
        return activate("ln_sqrt", rstd[:, g:g + 8], rstd[:, g:g + 8], ACT.Sqrt, [r])

    def ln_normalize(g, root, banks):
        r = recip("ln_rstd", rstd[:, g:g + 8], rstd[:, g:g + 8], [root])
        for t in range(g, g + 8):
            normed[t] = ts("ln_xn", XN[:, t, :], X[:, t, :], mean_var[:, t, 0:1], rstd[:, t:t + 1],
                           ALU.subtract, ALU.mult, [r])
        for t in range(g, g + 8, 2):
            b = banks[(t // 2) % 2]
            out_v = PS[:, b, :].rearrange("p (k n) -> p k n", k=KD)
            for k in range(KD):
                for j in range(2):
                    m = turn("ln_turn", out_v[:, k, j * P:(j + 1) * P], XN[:, t + j, k * P:(k + 1) * P], ident,
                             [normed[t + j], const_in, bank_busy[b]])
            turned[t // 2] = activate("ln_xt", XT[:, t // 2, :, :], out_v, ACT.Copy, [m])
            bank_busy[b] = [turned[t // 2]]

    def router_logits(g, router, router_in, n_e, banks):
        per = 512 // n_e
        for t in range(g, g + 8):
            b = banks[t // per]
            for k in range(KD):
                o = PS[:, b, (t % per) * n_e:(t % per + 1) * n_e]
                m = mm("router", o, XT[:, t // 2, k, (t % 2) * P:(t % 2 + 1) * P], router[:, k, :], k == 0,
                       k == KD - 1, [turned[t // 2], router_in, bank_busy[b]])
        return m

    def over_experts(v, n_e):
        return v.unsqueeze(2).to_broadcast([P, NT, n_e])

    def over_tiles(v, n_e):
        return v.unsqueeze(1).to_broadcast([P, NT, n_e])

    def first_best(scores, best, iota_low, n_e, tmp, hot, first, ready):
        m = tt("route", tmp, scores, over_experts(best, n_e), ALU.is_equal, [ready])
        m = stt("route", tmp, tmp, -float(n_e), over_tiles(iota_low, n_e), ALU.mult, ALU.add, [m])
        m = reduce("route", first, tmp, ALU.min, [m])
        m = ts("route", first, first, float(n_e), None, ALU.add, after=[m])
        return tt("route", hot, over_tiles(iota_low, n_e), over_experts(first, n_e), ALU.is_equal, [m])

    def count_before(hot, n_e, hot_ready, banks, reset, reset_ready, totals, running, pos):
        w = NT * n_e
        flat = hot.rearrange("p t e -> p (t e)")
        n = -(-w // 512)
        m = None
        for i in range(n):
            lo, hi = i * 512, min((i + 1) * 512, w)
            m = mm("count", PS[:, banks[i], 0:hi - lo], C["before"], flat[:, lo:hi], True, True,
                   [hot_ready, const_in, bank_busy[banks[i]]])
            m = mm("count", PS[:, banks[n + i], 0:hi - lo], C["ones"], flat[:, lo:hi], True, True,
                   [bank_busy[banks[n + i]]])
        tot_te, pos_flat = totals.rearrange("p e t -> p t e"), pos.rearrange("p t e -> p (t e)")
        per = 512 // n_e
        for i in range(n):
            t0, t1 = i * per, min((i + 1) * per, NT)
            src = PS[:, banks[n + i], 0:(t1 - t0) * n_e].rearrange("p (t e) -> p t e", e=n_e)
            c = copy("route", tot_te[:, t0:t1, :], src, [m])
            bank_busy[banks[n + i]] = [c]
        f = lambda v: v.rearrange("p e t -> p (e t)")
        s = dve.add("route", lambda e: e.tensor_tensor_scan(f(running), f(reset), f(totals), 0.0,
                                                            ALU.mult, ALU.add), [c, reset_ready])
        d = tt("route", f(running), f(running), f(totals), ALU.subtract, [s])
        run_te = running.rearrange("p e t -> p t e")
        for i in range(n):
            t0, t1 = i * per, min((i + 1) * per, NT)
            src = PS[:, banks[i], 0:(t1 - t0) * n_e].rearrange("p (t e) -> p t e", e=n_e)
            c = tt("route", pos[:, t0:t1, :], src, run_te[:, t0:t1, :], ALU.add, [d])
            bank_busy[banks[i]] = [c]
        return c

    def make_reset(reset, after):
        m = fill("route", reset, 1.0, after)
        return fill("route", reset[:, :, 0:1], 0.0, [m])

    def scatter(stage, table, slots, idx, row, after):
        return pool.add(stage, lambda e: e.indirect_dma_start(
            out=table, out_offset=bass.IndirectOffsetOnAxis(ap=idx, axis=0), in_=row, in_offset=None,
            bounds_check=slots - 1, oob_is_err=False), after, dma=True)

    def gather(stage, table, slots, idx, row, after):
        return pool.add(stage, lambda e: e.indirect_dma_start(
            out=row, out_offset=None, in_=table, in_offset=bass.IndirectOffsetOnAxis(ap=idx, axis=0),
            bounds_check=slots - 1, oob_is_err=False), after, dma=True)

    top[0] = work
    router0 = place("router0", [P, KD, E0])
    qkv_w = place("qkv_w", [P, KD, 3 * D])
    proj_w = place("proj_w", [P, 2, D])
    qkv_b = place("qkv_b", [P, 3 * KD])
    q_bias = place("q_bias", [P, 2, KD])
    v_bias = place("v_bias", [P, 2, D])
    proj_b = place("proj_b", [P, D])
    rel = place("rel", [P, KD, 4, WIN])
    best0 = place("best0", [P, NT])
    first0 = place("first0", [P, NT])
    pos0 = place("pos0", [P, NT])
    taken0 = place("taken0", [P, NT])
    l0_work = top[0]
    router0_in = dma("router0", router0[:, :, :], a["w_router"].rearrange("(k p) e -> p k e", p=P))
    qkv_w_in = dma("qkv_w", qkv_w[:, :, :], a["qkv_w"].rearrange("(k p) n -> p k n", p=P))
    attn_in = [dma("attn_w", proj_w[:, :, :], a["proj_w"]),
               dma("attn_w", qkv_b[:, :], a["qkv_b"]),
               dma("attn_w", v_bias[:, 0, :], a["v_b"].partition_broadcast(P)),
               dma("attn_w", v_bias[:, 1, :], a["v_b"].partition_broadcast(P)),
               dma("attn_w", proj_b[:, :], a["proj_b"].partition_broadcast(P)),
               dma("attn_w", rel[:, :, :, :], a["rel"])][-1]
    SCORE_BANKS, MISC, GU_BANKS, PV_BANKS = [0, 1], [2, 3], [4, 5], [6, 7]
    FIRST_TILES = 8
    top[0] = s_base + FIRST_TILES * D * 4
    logit0 = place("logit0", [P, NT, E0])
    tmp0 = place("tmp0", [P, NT, E0])
    hot0 = place("hot0", [P, NT, E0])
    totals0 = place("totals0", [P, E0, NT])
    running0 = place("running0", [P, E0, NT])
    reset0 = place("reset0", [P, E0, NT])
    assert top[0] <= work
    routed, normed0, turned0 = {}, [], []

    def start0():
        roots, lg_marks = {}, []
        for g in range(0, NT, 8):
            roots[g] = ln_statistics(g, lambda t: [x_in[t // 4]])
            if g:
                ln_normalize(g - 8, roots[g - 8], GU_BANKS)
                lg_marks.append(router_logits(g - 8, router0, router0_in, E0, PV_BANKS))
                yield
        ln_normalize(g, roots[g], GU_BANKS)
        lg_marks.append(router_logits(g, router0, router0_in, E0, PV_BANKS))
        normed0[:], turned0[:] = normed, turned
        per = 512 // E0
        reset_ready = make_reset(reset0[:, :, :], [])
        for i in range(2):
            m = copy("route", logit0[:, i * per:(i + 1) * per, :],
                     PS[:, PV_BANKS[i], :].rearrange("p (t e) -> p t e", e=E0), [lg_marks])
            bank_busy[PV_BANKS[i]] = [m]
        mb = reduce("route", best0[:, :], logit0[:, :, :], ALU.max, [m])
        yield
        hot_ready = first_best(logit0[:, :, :], best0[:, :], C["iota0_low"], E0, tmp0[:, :, :], hot0[:, :, :],
                               first0[:, :], mb)
        pos_ready = count_before(hot0[:, :, :], E0, hot_ready, [4, 5, 6, 7], reset0[:, :, :], reset_ready,
                                 totals0[:, :, :], running0[:, :, :], tmp0[:, :, :])
        yield
        m = tt("route", tmp0[:, :, :], tmp0[:, :, :], hot0[:, :, :], ALU.mult, [pos_ready])
        m = reduce("route", pos0[:, :], tmp0[:, :, :], ALU.add, [m])
        tk = ts("route", taken0[:, :], pos0[:, :], float(CAP), None, ALU.is_lt, after=[m])
        m = stt("route", pos0[:, :], first0[:, :], float(CAP), pos0[:, :], ALU.mult, ALU.add, [tk])
        m = ts("route", pos0[:, :], pos0[:, :], float(SLOTS0), None, ALU.add, after=[m])
        m = stt("route", pos0[:, :], taken0[:, :], -float(2 * SLOTS0), pos0[:, :], ALU.mult, ALU.add, [m])
        m = ts("route", pos0[:, :], pos0[:, :], float(2 * SLOTS0), None, ALU.add, after=[m])
        put_ready = copy("route", slot_put[:, :], pos0[:, :], [m])
        for t in range(NT):
            routed["scattered"] = scatter("scatter0", table0, SLOTS0, slot_put[:, t:t + 1], XN[:, t, :],
                                          [put_ready, normed0[t], table0_zeroed])
        yield
        m = ts("route", pos0[:, :], pos0[:, :], float(SLOTS0 - 1), None, ALU.min, after=[put_ready])
        routed["get"] = copy("route", slot_get[:, :], pos0[:, :], [m])
        m = tt("route", logit0[:, :, :], logit0[:, :, :], over_experts(best0[:, :], E0), ALU.subtract, [hot_ready])
        m = activate("route_exp", logit0[:, :, :], logit0[:, :, :], ACT.Exp, [m])
        yield
        m = reduce("route", gate_eff[:, :], logit0[:, :, :], ALU.add, [m])
        m = recip("route", gate_eff[:, :], gate_eff[:, :], [m])
        routed["gate"] = tt("route", gate_eff[:, :], gate_eff[:, :], taken0[:, :], ALU.mult, [m, tk])
        yield

    UNITS, UW, UT, SR, PR0, STEPS = NT // 2, 4, 2 * P, 2, 3, 2 * NT
    top[0] = l0_work
    Q2 = place("Q2", [P, 2, KD, UW, 2, WIN])
    KB = place("KB", [P, KD, UW, 4, WIN])
    VW = 2 * HD + 1
    VB = place("VB", [P, 2, 2, PAIRS, 2, VW])
    sc = place("sc", [P, SR, KD, 4, WIN])
    prob = place("prob", [P, PR0, KD, 4, 2, WIN])
    sc_max = place("sc_max", [P, SR, KD * 4])
    PT = place("PT", [P, 2, KD, 4, P])
    inv_sum = place("inv_sum", [P, KD, 4, 2])
    O = place("O", [P, 2, PAIRS, HD])
    OT = place("OT", [P, 2, P])
    after_ot = top[0]
    y0 = place("y0", [P, 2, 2, D])
    top[0] = after_ot
    got0 = place("got0", [P, 2, 4, D])
    top[0] = persistent_top
    GROUP = 4
    GT = GROUP * CAP // P
    rows0 = place("rows0", [P, 2, D])
    rowsT = place("rowsT", [P, 2, KD, GROUP * CAP])
    wgt0 = place("wgt0", [P, 2, 3, KD, F0])
    silu0 = place("silu0", [P, 2, KD, CAP])
    hT0 = place("hT0", [P, 2, KD, CAP])
    assert top[0] <= xn_base
    kb_zeroed = fill("kb_zero", KB[:, :, :, :, :], 0.0, on=pool)
    vb_zeroed = fill("vb_zero", VB[:, :, :, :, :, :], 0.0, on=pool)
    for w2 in range(2):
        v_ones = fill("v_ones", VB[64 * w2:64 * w2 + 64, :, :, :, w2, HD:HD + 1], 1.0, [vb_zeroed], on=pool)
    turn_of = {"misc": 0, "gu": 0}

    def next_bank(kind, banks):
        turn_of[kind] += 1
        return banks[turn_of[kind] % 2]

    q_done, k_done, v_done, exp_done, pt_done, norm_done, ot_done, s_done = {}, {}, {}, {}, {}, {}, {}, {}
    q2_free, kb_free, v_free, pt_free = [[], []], [], [[], []], [[], []]
    sc_free, prob_free = [[]] * SR, [[]] * PR0
    o_free, ot_free, inv_free = [], [], []

    def project_qk(u, which):
        i = u % 2
        b = next_bank("misc", MISC)
        for c in range(KD):
            for k in range(KD):
                col = which * D + c * P
                m = mm("qkv", PS[:, b, c * UT:(c + 1) * UT], qkv_w[:, k, col:col + P], XT[:, u, k, :],
                       k == 0, k == KD - 1, [qkv_w_in, turned[u], bank_busy[b]])
        outs = []
        for c in range(KD):
            src = PS[:, b, c * UT:(c + 1) * UT].rearrange("p (w q) -> p w q", w=UW)
            if which == 0:
                for e in range(2):
                    outs.append(activate("q_out", Q2[:, i, c, :, e, :], src, ACT.Identity, [m, qb, q2_free[i]],
                                         bias=q_bias[:, e, c:c + 1], scale=C["head_scale"][:, e:e + 1]))
            else:
                for g in range(4):
                    rows = slice(32 * g, 32 * g + 32)
                    after = [m, attn_in, kb_zeroed, list(kb_free)]
                    bias = qkv_b[rows, KD + c:KD + c + 1]
                    if g < 2:
                        outs.append(activate("k_out", KB[rows, c, :, g, :], src[rows], ACT.Identity, after, bias=bias))
                    else:
                        outs.append(ts("k_out", KB[rows, c, :, g, :], src[rows], bias, None, ALU.add, after=after))
        bank_busy[b] = outs
        (q_done, k_done)[which][u] = outs

    def project_v(u):
        i = u % 2
        b = next_bank("misc", MISC)
        for j in range(2):
            for k in range(KD):
                m = mm("qkv", PS[:, b, j * D:(j + 1) * D], XT[:, u, k, j * P:(j + 1) * P], qkv_w[:, k, 2 * D:3 * D],
                       k == 0, k == KD - 1, [qkv_w_in, turned[u], bank_busy[b]])
        split = "p (r e h) -> p r e h"
        for w2 in range(2):
            rows = slice(64 * w2, 64 * w2 + 64)
            for e in range(2):
                src = PS[rows, b, :].rearrange(split, e=2, h=HD)[:, :, e, :]
                bias = v_bias[rows, :, :].rearrange("p j n -> p (j n)").rearrange(split, e=2, h=HD)[:, :, e, :]
                o = VB[rows, i, :, :, w2, e * (HD + 1):e * (HD + 1) + HD].rearrange("p j r h -> p (j r) h")
                m2 = tt("v_out", o, src, bias, ALU.add, [m, attn_in, v_ones, v_free[i]])
        bank_busy[b] = [m2]
        v_done[u] = m2

    def score(s):
        u, w = divmod(s, UW)
        i, b, r = u % 2, SCORE_BANKS[s % 2], s % SR
        for c in range(KD):
            m = mm("scores", PS[:, b, c * 256:(c + 1) * 256], Q2[:, i, c, w, :, :].rearrange("p e q -> p (e q)"),
                   KB[:, c, w, :, :].rearrange("p g k -> p (g k)"), True, True,
                   [q_done[u], k_done[u], bank_busy[b]])
        if w == UW - 1:
            q2_free[i] = [m]
            kb_free[:] = [m]
        flat = sc[:, r, :, :, :].rearrange("p c g k -> p (c g k)")
        m2 = tt("sc_bias", flat, PS[:, b, :], rel[:, :, :, :].rearrange("p c g k -> p (c g k)"), ALU.add,
                [m, attn_in, sc_free[r]])
        bank_busy[b] = [m2]
        by_head = sc[:, r, :, :, :].rearrange("p c g k -> p (c g) k")
        m = reduce("sc_max", sc_max[:, r, :], by_head, ALU.max, [m2])
        m = tt("sc_sub", by_head, by_head, sc_max[:, r, :].unsqueeze(2).to_broadcast([P, KD * 4, WIN]), ALU.subtract,
               [m])
        t, w2 = divmod(s, 2)
        exp_done[s] = activate("sc_exp", prob[:, t % PR0, :, :, w2, :].rearrange("p c g k -> p (c g) k"), by_head,
                               ACT.Exp, [m, prob_free[t % PR0]])
        sc_free[r] = [exp_done[s]]

    def turn_probabilities(t, c):
        b, r = next_bank("misc", MISC), t % PR0
        for g in range(4):
            m = turn("p_turn", PS[:, b, g * P:(g + 1) * P], prob[:, r, c, g, :, :].rearrange("p w k -> p (w k)"), ident,
                     [exp_done[2 * t], exp_done[2 * t + 1], bank_busy[b]])
        if c == KD - 1:
            prob_free[r] = [m]
        pt_done[t] = activate("pt_out", PT[:, t % 2, c, :, :].rearrange("p g n -> p (g n)"), PS[:, b, :], ACT.Copy,
                              [m, pt_free[t % 2]])
        bank_busy[b] = [pt_done[t]]

    def attend(t):
        u, j = divmod(t, 2)
        for c in range(KD):
            for g in range(4):
                m = mm("pv", PS[:, PV_BANKS[c], g * 2 * VW:(g + 1) * 2 * VW], PT[:, t % 2, c, g, :],
                       VB[:, u % 2, j, 4 * c + g, :, :].rearrange("p w n -> p (w n)"), True, True,
                       [pt_done[t], v_done[u], [bank_busy[x] for x in PV_BANKS]])
        pt_free[t % 2] = [m]
        if j == 1:
            v_free[u % 2] = [m]
        av = PS[:, PV_BANKS[0]:PV_BANKS[1] + 1, 0:4 * 2 * VW].rearrange("p c (g w n) -> p c g w n", g=4, w=2)
        for c in range(KD):
            r = recip("pv_inv", inv_sum[:, c, :, :], av[:, c, :, :, HD], [m, list(inv_free)])
        for e in range(2):
            rows = slice(64 * e, 64 * e + 64)
            for c in range(KD):
                n = tt("pv_norm", O[rows, :, 4 * c:4 * c + 4, :],
                       av[rows, c, :, :, e * (HD + 1):e * (HD + 1) + HD].rearrange("p g w h -> p w g h"),
                       inv_sum[rows, c, :, :].rearrange("p g w -> p w g").unsqueeze(3).to_broadcast([64, 2, 4, HD]),
                       ALU.mult, [r, list(o_free)])
        for x in PV_BANKS:
            bank_busy[x] = [n]
        inv_free[:] = [n]
        norm_done[t] = n

    def turn_heads(t):
        b = next_bank("misc", MISC)
        for w in range(2):
            m = turn("o_turn", PS[:, b, w * P:(w + 1) * P], O[:, w, :, :].rearrange("p r h -> p (r h)"), ident,
                     [norm_done[t], bank_busy[b]])
        o_free[:] = [m]
        m2 = activate("ot_out", OT[:, :, :].rearrange("p e (w q) -> p w e q", w=2),
                      PS[:, b, 0:2 * P].rearrange("p (w e q) -> p w e q", w=2, e=2), ACT.Copy, [m, list(ot_free)])
        bank_busy[b] = [m2]
        ot_done[t] = m2

    def project_out(t):
        b = next_bank("misc", MISC)
        for e in range(2):
            m = mm("proj", PS[:, b, 0:D], OT[:, e, :], proj_w[:, e, :], e == 0, e == 1,
                   [ot_done[t], attn_in, bank_busy[b]])
        ot_free[:] = [m]
        s_done[t] = tt("s_out", S[:, t, :], PS[:, b, 0:D], proj_b[:, :], ALU.add,
                       [m, routed["gate"] if t >= FIRST_TILES else None])
        bank_busy[b] = [s_done[t]]

    tail = CAP - P
    rowsT_ready, rowsT_free = {}, [[], []]
    y_stored = [[], []]

    def expert0():
        x_done = list(normed0)
        rows_free, w_free = [x_done] * 2, [x_done] * 2
        silu_free, h_free = [x_done] * 2, [x_done] * 2
        for i in range(2):
            rowsT_free[i] = x_done

        def load_weights(ex):
            i = ex % 2
            for n, name in enumerate(("w_gate", "w_up", "w_down")):
                m = dma(f"w0_{i}", wgt0[:, i, n, :, :], a[name][ex].rearrange("(k p) n -> p k n", p=P), w_free[i])
            return m

        def turn_rows(grp, t):
            gi, i = grp % 2, t % 2
            row = (grp * GT + t) * P
            rows_in = dma(f"rows0_{i}", rows0[:, i, :], table0[row:row + P, :], [routed["scattered"], rows_free[i]])
            b = next_bank("misc", MISC)
            for k in range(KD):
                m = turn("rows_turn", PS[:, b, k * P:(k + 1) * P], rows0[:, i, k * P:(k + 1) * P], ident,
                         [rows_in, bank_busy[b]])
            rows_free[i] = [m]
            rt = activate("rowsT_out", rowsT[:, gi, :, t * P:(t + 1) * P],
                          PS[:, b, 0:KD * P].rearrange("p (k n) -> p k n", k=KD), ACT.Copy, [m, rowsT_free[gi]])
            bank_busy[b] = [rt]
            rowsT_ready[grp] = rt

        w_in = {0: load_weights(0)}
        for t in range(GT):
            turn_rows(0, t)
            if t % 2:
                yield
        for ex in range(E0):
            grp, j = divmod(ex, GROUP)
            gi, i = grp % 2, ex % 2
            if ex + 1 < E0:
                w_in[ex + 1] = load_weights(ex + 1)
            for f in range(KD):
                b = next_bank("gu", GU_BANKS)
                for n in range(2):
                    for k in range(KD):
                        m = mm("gate_up", PS[:, b, n * CAP:(n + 1) * CAP], wgt0[:, i, n, k, f * P:(f + 1) * P],
                               rowsT[:, gi, k, j * CAP:(j + 1) * CAP], k == 0, k == KD - 1,
                               [w_in[ex], rowsT_ready[grp], bank_busy[b]])
                s = activate("silu0", silu0[:, i, f, :], PS[:, b, 0:CAP], ACT.Tanh, [m, silu_free[i]], scale=0.5)
                s = stt("h0", silu0[:, i, f, :], silu0[:, i, f, :], 1.0, PS[:, b, 0:CAP], ALU.add, ALU.mult, [s])
                h = stt("h0", hT0[:, i, f, :], silu0[:, i, f, :], 0.5, PS[:, b, CAP:2 * CAP], ALU.mult, ALU.mult,
                        [s, h_free[i]])
                bank_busy[b] = [h]
                yield
            if j == GROUP - 1:
                rowsT_free[gi] = [m]
            silu_free[i] = [h]
            if grp + 1 < E0 // GROUP:
                for t in ((0,), (1,), (2,), (3, 4))[j]:
                    turn_rows(grp + 1, t)
            b = next_bank("misc", MISC)
            for f in range(KD):
                m = mm("down0", PS[:, b, 0:D], hT0[:, i, f, 0:P], wgt0[:, i, 2, f, :], f == 0, f == KD - 1,
                       [h, bank_busy[b]])
            for f in range(KD):
                m = mm("down0", PS[0:tail, b, D:2 * D], hT0[:, i, f, P:CAP], wgt0[:, i, 2, f, :], f == 0,
                       f == KD - 1)
            w_free[i] = [m]
            h_free[i] = [m]
            c1 = copy("y0", y0[:, i, 0, :], PS[:, b, 0:D], [m, y_stored[i]])
            c2 = copy("y0", y0[0:tail, i, 1, :], PS[0:tail, b, D:2 * D], [])
            bank_busy[b] = [c2]
            at = ex * CAP
            y_stored[i] = [dma(f"y0_{i}", result0[at:at + P, :], y0[:, i, 0, :], [c1]),
                           dma(f"y0_{i}", result0[at + P:at + CAP, :], y0[0:tail, i, 1, :], [c2])]
            yield

    EXPERT_PIECES = (2, 3)

    def advance(generator, n=1):
        return [next(generator, generator) for _ in range(n)][-1] is generator

    x1_ready, x1_saved, x_again = [], [], []
    got_free = [[]] * 2
    x1_view = x1_dram.rearrange("(t p) d -> p t d", p=P)
    y_written = []

    def combine_gather(q):
        i = q % 2
        for j in range(4):
            t = 4 * q + j
            gm = gather(f"got0_{i}", result0, SLOTS0, slot_get[:, t:t + 1], got0[:, i, j, :],
                        [routed["get"], y_written, got_free[i]])
        return gm

    def combine_gate(q, gathered):
        i = q % 2
        for j in range(4):
            t = 4 * q + j
            m = stt("mix0", got0[:, i, j, :], got0[:, i, j, :], gate_eff[:, t:t + 1], XN[:, t, :], ALU.mult, ALU.add,
                    [gathered, routed["gate"]])
        return activate("silu_mix0", got0[:, i, :, :], got0[:, i, :, :], ACT.Silu, [m])

    def combine_add(q, gated):
        i, four = q % 2, slice(4 * q, 4 * q + 4)
        m = tt("mix0", got0[:, i, :, :], got0[:, i, :, :], S[:, four, :], ALU.mult, [gated, s_done[4 * q + 3]])
        m = tt("mix0", X[:, four, :], X[:, four, :], got0[:, i, :, :], ALU.add, [m, x_again[q]])
        got_free[i] = [m]
        x1_saved.append(dma("x1_save", x1_view[:, four, :], X[:, four, :], [m]))
        x1_ready.append(m)

    def combination0():
        y_written[:] = y_stored[0] + y_stored[1]
        for i in range(NT // 4):
            x_again.append(dma(f"xa{i}", X[:, 4 * i:4 * i + 4, :], x_view[:, 4 * i:4 * i + 4, :], y_written))
        gathered, gated, roots = {}, {}, {}
        for q in range(NT // 4 + 2):
            if q >= 2:
                while 4 * (q - 2) + 3 not in s_done:
                    yield
                combine_add(q - 2, gated[q - 2])
            if q < NT // 4:
                gathered[q] = combine_gather(q)
            if 1 <= q <= NT // 4:
                gated[q - 1] = combine_gate(q - 1, gathered[q - 1])
            if q >= 2 and q % 2:
                g = 4 * (q - 3)
                roots[g] = ln_statistics(g, lambda t: [x1_ready[t // 4]])
                yield
                ln_normalize(g, roots[g], GU_BANKS)
            yield

    start, experts, combination = start0(), expert0(), combination0()
    advance(start, 3)
    qb = None
    for e in range(2):
        qb = ts("q_bias", q_bias[:, e, :], qkv_b[:, 0:KD], C["head_scale"][:, e:e + 1], None, ALU.mult,
                after=[attn_in, const_in])
    project_qk(0, 0)
    project_qk(0, 1)
    project_v(0)
    advance(start, 3)
    score(0)
    score(1)
    for s in range(STEPS + 5):
        u, g = divmod(s, UW)
        if s + 2 < STEPS:
            score(s + 2)
        if u + 1 < UNITS and g < 3:
            (lambda: project_qk(u + 1, 0), lambda: project_qk(u + 1, 1), lambda: project_v(u + 1))[g]()
        advance(start)
        if u >= 1 and advance(experts, EXPERT_PIECES[s % len(EXPERT_PIECES)]):
            advance(combination)
        if s % 2 and 0 <= s - 3 < STEPS:
            attend((s - 3) // 2)
        if s % 2 and 0 <= s - 5 < STEPS:
            project_out((s - 5) // 2)
        if s % 2 == 0 and 0 <= s - 4 < STEPS:
            turn_heads((s - 4) // 2)
        if 0 <= s - 1 < STEPS:
            turn_probabilities(*divmod(s - 1, 2))
    last = NT - 1
    for _ in combination:
        pass

    layer0_end = [s_done[last], y_written]
    top[0] = persistent_top
    sc1 = place("sc1", [P, NT, E1])
    prob1 = place("prob1", [P, NT, E1])
    tmp1 = place("tmp1", [P, NT, E1])
    hot1 = place("hot1", [P, TOPK, NT, E1])
    both1 = place("both1", [P, NT, E1])
    totals1 = place("totals1", [P, E1, NT])
    running1 = place("running1", [P, E1, NT])
    reset1 = place("reset1", [P, E1, NT])
    best1 = place("best1", [P, TOPK, NT])
    first1 = place("first1", [P, NT])
    sum1 = place("sum1", [P, NT])
    pad_i = place("pad_i", [P, E1], I32)
    pad_f = place("pad_f", [P, E1])
    pad_end = place("pad_end", [P, E1])
    pad_base = place("pad_base", [P, E1])
    owner = place("owner", [P, TILES1, E1])
    owner_f = place("owner_f", [P, TILES1])
    assert top[0] <= xn_base
    top[0] = work
    NB = D + 1
    RN = E1 + 3
    router1 = place("router1", [P, KD, RN])
    router1_b = place("router1_b", [P, E1])
    inv = place("inv", [P, 2, D])
    Wf = place("Wf", [P, 3, KD, NB])
    bn = place("bn", [P, 3, KD])
    bf = place("bf", [P, 3, 2])
    nyq_b = place("nyq_b", [P, 3])
    nyq = place("nyq", [P, 3, NT])
    nyq_abs = place("nyq_abs", [P, 3, NT])
    nyq_sum = place("nyq_sum", [P, NT])
    nyq_scan = place("nyq_scan", [P, NT])
    nyq_reset = place("nyq_reset", [P, NT])
    nyq_T = place("nyq_T", [NT, P])
    CH = 2 * P
    z_base = top[0]
    Z = place("Z", [P, 3, 3, 2, CH])
    z_top = top[0]
    SQ = place("SQ", [P, 2, 3, 2, CH])
    MAG = place("MAG", [P, 3, 3, CH])
    PR = place("PR", [P, 2, 4, CH])
    RUN = place("RUN", [P, 2, 2, CH])
    U = place("U", [P, 2, 2, CH])
    s1 = place("s1", [P, 2, 2, D])
    attn1_top = top[0]
    top[0] = z_base
    dft = place("dft", [P, KD, NB])
    Wn = place("Wn", [P, 3, KD, D])
    b_rep = place("b_rep", [P, KD, P])
    assert top[0] <= z_top

    QQ, KK, VV = 0, 1, 2
    router1_in = dma("router1", router1[:, :, 0:E1], a["Wg"].rearrange("(k p) e -> p k e", p=P), layer0_end)
    dft_in = [dma("dft", dft[:, :, :], a["dft"].rearrange("(k p) n -> p k n", p=P), layer0_end),
              dma("dft", inv[:, :, :], a["inv"], layer0_end),
              dma("dft", router1_b[:, :], a["bg"].partition_broadcast(P), layer0_end),
              dma("dft", bn[:, :, :], a["attn1_b"], layer0_end)][-1]
    wn_in = [dma(f"wn{n}", Wn[:, n, :, :], a[name].rearrange("(k p) n -> p k n", p=P), layer0_end)
             for n, name in enumerate(("Wq", "Wk", "Wv"))]
    for n in range(3):
        for c in range(KD):
            for k in range(KD):
                m = mm("wf", PS[:, c, 0:NB], Wn[:, n, k, c * P:(c + 1) * P], dft[:, k, :], k == 0, k == KD - 1,
                       [wn_in[n], dft_in, bank_busy[c]])
            wf_ready = copy("wf_out", Wf[:, n, c, :], PS[:, c, 0:NB], [m])
            bank_busy[c] = [wf_ready]
        for part in range(2):
            for k in range(KD):
                m = mm("bf", PS[:, 2, 2 * n + part:2 * n + part + 1], dft[:, k, part * P:(part + 1) * P],
                       bn[:, n, k:k + 1], k == 0, k == KD - 1, [bank_busy[2]])
        r = copy("b_rep", b_rep[:, :, :], bn[:, n, :].unsqueeze(2).to_broadcast([P, KD, P]), [dft_in, m])
        for k in range(KD):
            m = mm("bf", PS[:, 2, 8 + n:9 + n], b_rep[:, k, :], dft[:, k, D:NB], k == 0, k == KD - 1, [r])
    copy("bf_out", bf[:, :, :], PS[:, 2, 0:6].rearrange("p (n r) -> p n r", n=3), [m])
    bf_ready = copy("bf_out", nyq_b[:, :], PS[:, 2, 8:11], [m])
    bank_busy[2] = [bf_ready]
    router1_ready = copy("rn_out", router1[:, :, E1:RN].rearrange("p k n -> p n k"), Wf[:, :, :, D], [wf_ready])
    nyq_reset_ready = fill("nyq", nyq_reset[:, :].rearrange("p (b t) -> p b t", b=BATCH)[:, :, 0:1], 0.0,
                           [fill("nyq", nyq_reset[:, :], 1.0, layer0_end)])

    ROUTER_BANK = 7
    for g in range(0, NT, 8):
        routed1 = router_logits(g, router1, [router1_in, router1_ready], RN, [ROUTER_BANK])
    normed1, turned1 = list(normed), list(turned)
    both_out = PS[:, ROUTER_BANK, 0:NT * RN].rearrange("p (t n) -> p t n", n=RN)

    out_view = out.rearrange("(t p) d -> p t d", p=P)
    if stop_at == "layer0":
        finish = [dma("out", out_view, X[:, :, :], [x1_ready[-1]]), x1_saved]
        return replay(nc, (pe, dve, act, pool, sp), finish + y_written, sp)

    setup1_end = [bf_ready, wf_ready]
    x_free = x1_saved + [normed1[-1]]
    CHUNKS, PER_BATCH = T // CH, SEQ // CH
    mag_of, root_of, bound, z_free, mag_free, sq_free = {}, {}, {}, [setup1_end] * 3, [x1_ready[-1:]] * 3, [setup1_end] * 2
    run_free, u_free, s1_free, pr_free = [[x1_ready[-1:]] * 2 for _ in range(4)]
    dft_done, z_done = {}, {}

    def spectra(ch):
        i3, i = ch % 3, ch % 2
        for n in (KK, VV, QQ):
            b = 3 * i + n
            for part in range(2):
                for k in range(KD):
                    m = mm("dft", PS[:, b, part * CH:(part + 1) * CH], Wf[:, n, k, part * P:(part + 1) * P],
                           XT[:, ch, k, :], k == 0, k == KD - 1, [wf_ready, turned1[ch], bank_busy[b]])
            for part in range(2):
                zz = activate("z", Z[:, i3, n, part, :], PS[:, b, part * CH:(part + 1) * CH], ACT.Identity,
                              [m, bf_ready, z_free[i3]], bias=bf[:, n, part:part + 1])
            bank_busy[b] = [zz]
            sq = activate("zsq", SQ[:, i, n, :, :], Z[:, i3, n, :, :], ACT.Square, [zz, sq_free[i]])
        dft_done[ch], z_done[ch] = m, sq
        mag_of[ch] = tt("mag", MAG[:, i3, :, :], SQ[:, i, :, 0, :], SQ[:, i, :, 1, :], ALU.add, [sq, mag_free[i3]],
                        on=pool)
        sq_free[i] = [mag_of[ch]]

    def magnitudes(ch):
        root_of[ch] = activate("mag_sqrt", MAG[:, ch % 3, :, :], MAG[:, ch % 3, :, :], ACT.Sqrt, [mag_of[ch]])

    run_last = []

    def bind(ch):
        i3, i = ch % 3, ch % 2
        z = lambda n, part: Z[:, i3, n, part, :]
        mag = lambda n: MAG[:, i3, n, :]
        wide = lambda n: MAG[:, i3, n, :].unsqueeze(1).to_broadcast([P, 2, CH])
        m = ts("inv", MAG[:, i3, :, :], MAG[:, i3, :, :], UNIT_EPS, None, ALU.add, after=[root_of[ch]])
        m = tt("inv", mag(VV), mag(VV), mag(KK), ALU.mult, [m])
        m = tt("inv", mag(KK), mag(VV), mag(QQ), ALU.mult, [m])
        r = recip("inv", mag(KK), mag(KK), [m])
        m = tt("inv", mag(QQ), mag(QQ), mag(KK), ALU.mult, [r])
        mq = tt("inv", mag(VV), mag(VV), mag(KK), ALU.mult, [r])
        m = tt("bind", Z[:, i3, KK, :, :], Z[:, i3, KK, :, :], wide(QQ), ALU.mult, [m, z_done[ch]])
        w = [m, pr_free[0]]
        m1 = tt("bind", PR[:, 0, 0:2, :], Z[:, i3, KK, :, :], Z[:, i3, VV, :, :], ALU.mult, w)
        tt("bind", PR[:, 0, 2, :], z(KK, 0), z(VV, 1), ALU.mult, w)
        m2 = tt("bind", PR[:, 0, 3, :], z(KK, 1), z(VV, 0), ALU.mult, w)
        qn = tt("unbind", Z[:, i3, QQ, :, :], Z[:, i3, QQ, :, :], wide(VV), ALU.mult, [mq])
        mag_free[i3] = [qn]
        runs = []
        for part, (x0, x1, op, mk) in enumerate(((0, 1, ALU.subtract, m1), (2, 3, ALU.add, m2))):
            initial = 0.0 if ch % PER_BATCH == 0 else RUN[:, 1 - i, part, CH - 1:CH]
            runs.append(dve.add("running", lambda e, o=RUN[:, i, part, :], x0=x0, x1=x1, op=op, initial=initial:
                                e.tensor_tensor_scan(o, PR[:, 0, x0, :], PR[:, 0, x1, :], initial, ALU.add, op),
                                [mk, list(run_last), run_free[i]]))
        pr_free[0] = list(runs)
        run_last[:] = runs
        on = pool if ch in UNBIND_ON_POOL else dve
        w = [qn, runs, pr_free[1]]
        m1 = tt("unbind", PR[:, 1, 0:2, :], RUN[:, i, :, :], Z[:, i3, QQ, :, :], ALU.mult, w, on=on)
        m2 = tt("unbind", PR[:, 1, 2, :], RUN[:, i, 1, :], z(QQ, 0), ALU.mult, w, on=on)
        m3 = tt("unbind", PR[:, 1, 3, :], RUN[:, i, 0, :], z(QQ, 1), ALU.mult, w, on=on)
        run_free[i], z_free[i3] = [m1, m2, m3], [m1, m2, m3]
        ur = tt("unbind", U[:, i, 0, :], PR[:, 1, 0, :], PR[:, 1, 1, :], ALU.add, [m1, u_free[i]], on=on)
        ui = tt("unbind", U[:, i, 1, :], PR[:, 1, 2, :], PR[:, 1, 3, :], ALU.subtract, [m2, m3, u_free[i]], on=on)
        pr_free[1] = [ur, ui]
        ny = dma(f"nyq_row{i}", U[0:1, i, 1, :].rearrange("o (t n) -> o t n", n=P), nyq_T[2 * ch:2 * ch + 2, :],
                 [nyq_ready, ui])
        bound[ch] = [ur, ny]

    def inverse(ch):
        i, b = ch % 2, 6 + ch % 2
        for j in range(2):
            for part in range(2):
                m = mm("idft", PS[:, b, j * D:(j + 1) * D], U[:, i, part, j * P:(j + 1) * P], inv[:, part, :],
                       part == 0, part == 1, [bound[ch], bank_busy[b]])
        u_free[i] = [m]
        c = activate("s1_out", s1[:, i, :, :].rearrange("p j d -> p (j d)"), PS[:, b, :], ACT.Copy, [m, s1_free[i]])
        bank_busy[b] = [c]
        s1_free[i] = [dma(f"s1_save{i}", s1_dram[ch * CH:(ch + 1) * CH, :].rearrange("(t p) d -> p t d", p=P),
                          s1[:, i, :, :], [c])]

    UNBIND_ON_POOL = range(11, CHUNKS)
    spectra(0)
    spectra(1)
    magnitudes(0)

    m = tt("route", sc1[:, :, :], both_out[:, :, 0:E1], over_tiles(router1_b[:, :], E1), ALU.add,
           [routed1, dft_in, x_free])
    m = reduce("route", first1[:, :], sc1[:, :, :], ALU.max, [m])
    m = tt("route", sc1[:, :, :], sc1[:, :, :], over_experts(first1[:, :], E1), ALU.subtract, [m])
    m = activate("route_exp", prob1[:, :, :], sc1[:, :, :], ACT.Exp, [m])
    n = tt("nyq", nyq[:, :, :], both_out[:, :, E1:RN].rearrange("p t n -> p n t"),
           nyq_b[:, :].unsqueeze(2).to_broadcast([P, 3, NT]), ALU.add, [routed1, bf_ready])
    bank_busy[ROUTER_BANK] = [n]
    n = stt("nyq", nyq_abs[:, :, :], nyq[:, :, :], -1.0, nyq[:, :, :], ALU.mult, ALU.max, [n])
    n = ts("nyq", nyq_abs[:, :, :], nyq_abs[:, :, :], UNIT_EPS, None, ALU.add, after=[n])
    n = recip("nyq", nyq_abs[:, :, :], nyq_abs[:, :, :], [n])
    n = tt("nyq", nyq[:, :, :], nyq[:, :, :], nyq_abs[:, :, :], ALU.mult, [n])
    n = tt("nyq", nyq_sum[:, :], nyq[:, KK, :], nyq[:, VV, :], ALU.mult, [n])
    n1 = mm("nyq", PS[:, 6, 0:NT], C["upto"], nyq_sum[:, :], True, True, [n, bank_busy[6]])
    n2 = mm("nyq", PS[:, 7, 0:NT], C["ones"], nyq_sum[:, :], True, True, [bank_busy[7]])

    m = reduce("route", sum1[:, :], prob1[:, :, :], ALU.add, [m])
    m = recip("route", sum1[:, :], sum1[:, :], [m])
    m = tt("route", prob1[:, :, :], prob1[:, :, :], over_experts(sum1[:, :], E1), ALU.mult, [m])
    for k in range(TOPK):
        m = reduce("route", best1[:, k, :], prob1[:, :, :], ALU.max, [m])
        m = first_best(prob1[:, :, :], best1[:, k, :], C["iota1_low"], E1, tmp1[:, :, :], hot1[:, k, :, :],
                       first1[:, :], m)
        if k == 0:
            m = stt("route", prob1[:, :, :], hot1[:, k, :, :], -2.0, prob1[:, :, :], ALU.mult, ALU.add, [m])
    hot1_ready = tt("route", both1[:, :, :], hot1[:, 0, :, :], hot1[:, 1, :, :], ALU.add, [m])

    n = copy("nyq", nyq_sum[:, :], PS[:, 7, 0:NT], [n2])
    bank_busy[7] = [n]
    s = dve.add("nyq", lambda e: e.tensor_tensor_scan(nyq_scan[:, :], nyq_reset[:, :], nyq_sum[:, :], 0.0, ALU.mult,
                                                      ALU.add), [n, nyq_reset_ready])
    n = tt("nyq", nyq_scan[:, :], nyq_scan[:, :], nyq_sum[:, :], ALU.subtract, [s])
    n = tt("nyq", nyq_scan[:, :], PS[:, 6, 0:NT], nyq_scan[:, :], ALU.add, [n, n1])
    bank_busy[6] = [n]
    n = tt("nyq", nyq_scan[:, :], nyq_scan[:, :], nyq[:, QQ, :], ALU.mult, [n])
    nyq_turned = n

    reset_ready = make_reset(reset1[:, :, :], [x_free])
    m = count_before(both1[:, :, :], E1, hot1_ready, [6, 7], reset1[:, :, :], reset_ready,
                     totals1[:, :, :], running1[:, :, :], tmp1[:, :, :])
    m = tt("route", pad_f[:, :], running1[:, :, NT - 1], totals1[:, :, NT - 1], ALU.add, [m])
    m = ts("route", pad_f[:, :], pad_f[:, :], float(P - 1), None, ALU.add, after=[m])
    m = copy("route", pad_i[:, :], pad_f[:, :], [m])
    m = ts("route", pad_i[:, :], pad_i[:, :], 7, 7, ALU.logical_shift_right, ALU.logical_shift_left, after=[m])
    m = copy("route", pad_f[:, :], pad_i[:, :], [m])
    ones8 = C["ones"][:, 0:E1]
    m = dve.add("route", lambda e: e.tensor_tensor_scan(pad_end[:, :], ones8, pad_f[:, :], 0.0, ALU.mult, ALU.add),
                [m, const_in])
    m = tt("route", pad_base[:, :], pad_end[:, :], pad_f[:, :], ALU.subtract, [m])
    m = tt("route", both1[:, :, :], tmp1[:, :, :], over_tiles(pad_base[:, :], E1), ALU.add, [m])
    for k in range(TOPK):
        m = tt("route", tmp1[:, :, :], both1[:, :, :], hot1[:, k, :, :], ALU.mult, [m])
        m = reduce("route", first1[:, :], tmp1[:, :, :], ALU.add, [m])
        m = copy("route", slot1[:, k, :], first1[:, :], [m])
    slot1_ready = m
    n = turn("nyq_turn", PS[0:NT, 6, 0:P], nyq_scan[:, :], ident, [nyq_turned, bank_busy[6]])
    nyq_ready = copy("nyq", nyq_T[:, :], PS[0:NT, 6, 0:P], [n])
    bank_busy[6] = [nyq_ready]

    def routing1_rest():
        m = tt("route", sum1[:, :], best1[:, 0, :], best1[:, 1, :], ALU.add, [hot1_ready])
        m = ts("route", sum1[:, :], sum1[:, :], TOPK_EPS, None, ALU.add, after=[m])
        m = recip("route", sum1[:, :], sum1[:, :], [m])
        for k in range(TOPK):
            w = tt("route", weight1[:, k, :], best1[:, k, :], sum1[:, :], ALU.mult, [m])
        m = tt("route", owner[:, :, :], pad_end[:, :].unsqueeze(1).to_broadcast([P, TILES1, E1]),
               C["tile_start"].unsqueeze(2).to_broadcast([P, TILES1, E1]), ALU.is_le, [slot1_ready])
        m = reduce("route", owner_f[:, :], owner[:, :, :], ALU.add, [m])
        m = ts("route", owner_f[:, :], owner_f[:, :], float(E1 - 1), None, ALU.min, after=[m])
        return w, copy("route", tile_expert[:, :], owner_f[0:1, :], [m])

    top[0] = persistent_top
    W1 = place("W1", [P, E1, KD, F1])
    assert top[0] == after_xn
    KF = F1 // P
    W2 = place("W2", [P, E1, KF, D])
    assert top[0] == work
    to_scatter = [(t, k) for t in range(NT) for k in range(TOPK)]
    SCATTERS = 6

    def load_w1(ex, after):
        return dma("w1", W1[:, ex, :, :], a["W1"][ex].rearrange("(k p) n -> p k n", p=P), after)

    def load_w2(ex, after):
        return dma("w2", W2[:, ex, :, :], a["W2"][ex].rearrange("(k p) n -> p k n", p=P), after)

    XT_EXPERTS = 4
    per_expert = CHUNKS // XT_EXPERTS
    for ch in range(CHUNKS + 1):
        if ch + 2 < CHUNKS:
            spectra(ch + 2)
            if (ch + 3) % per_expert == 0:
                w2_in = load_w2((ch + 3) // per_expert - 1, [dft_done[ch + 2]])
        if ch + 1 < CHUNKS:
            magnitudes(ch + 1)
        if ch >= 1:
            inverse(ch - 1)
        if ch < CHUNKS:
            bind(ch)
        for t, k in to_scatter[SCATTERS * ch:SCATTERS * (ch + 1)]:
            scattered1 = scatter("scatter1", table1, SLOTS1, slot1[:, k, t:t + 1], XN[:, t, :],
                                 [slot1_ready, normed1[t], table1_zeroed])
        if ch == 0:
            weight1_ready, owner_ready = routing1_rest()
            for ex in range(XT_EXPERTS, E1):
                w2_in = load_w2(ex, [x1_ready[-1]])
        if ch == 2:
            for ex in range(E1 // 2):
                w1_in = load_w1(ex, [x_free, slot1_ready, weight1_ready, owner_ready])
        if ch == len(to_scatter) // SCATTERS + 2:
            for ex in range(E1 // 2, E1):
                w1_in = load_w1(ex, [scattered1])
    s1_saved = s1_free[0] + s1_free[1]
    attn1_end = [m for i in range(2) for m in (s1_free[i], u_free[i], pr_free[i])]

    top[0] = work
    b2 = place("b2", [P, E1, D])
    b1 = place("b1", [P, E1, KF])
    xg = place("xg", [P, 3, D])
    xgT = place("xgT", [P, 2, KD, P])
    hid = place("hid", [P, 2, F1])
    hidT = place("hidT", [P, 2, KF, P])
    y1 = place("y1", [P, 2, D])
    free2 = attn1_end
    b_in = [dma("b12", b1[:, :, :], a["b1"], free2),
            dma("b12", b2[:, :, :], a["b2"].partition_broadcast(P), free2)][-1]
    xg_free, xgT_free, hid_free, hidT_free, y1_free = ([free2] * 3, [free2] * 2, [free2] * 2, [free2] * 2,
                                                       [free2] * 2)
    HID_BANKS, HT_BANKS, Y_BANKS, TURN_BANKS = (0, 1), (2, 3), (4, 5), (6, 7)
    expert_on, xg_in, xgT_ready, hid_copied, hid_done = {}, {}, {}, {}, {}
    HALF = KF // 2

    def load_expert(queue, n):
        def issue(e):
            expert_on[queue.name] = e.value_load(tile_expert[0:1, n:n + 1], min_val=0, max_val=E1 - 1)
        queue.add("expert", issue, [owner_ready])

    def load_rows(n):
        xg_in[n] = dma(f"xg{n % 3}", xg[:, n % 3, :], table1[n * P:(n + 1) * P, :], [scattered1, xg_free[n % 3]])

    def turn_tile(n):
        i, b = n % 2, TURN_BANKS[n % 2]
        for k in range(KD):
            m = turn("xg_turn", PS[:, b, k * P:(k + 1) * P], xg[:, n % 3, k * P:(k + 1) * P], ident,
                     [xg_in[n], bank_busy[b]])
        xg_free[n % 3] = [m]
        xgT_ready[n] = activate("xgT_out", xgT[:, i, :, :].rearrange("p k n -> p (k n)"), PS[:, b, 0:KD * P],
                                ACT.Copy, [m, xgT_free[i]])
        bank_busy[b] = [xgT_ready[n]]

    def first_product(n):
        i = n % 2
        load_expert(pe, n)
        hid_copied[n] = []
        for half in range(2):
            b = HID_BANKS[half]
            cols = slice(half * HALF * P, (half + 1) * HALF * P)
            for k in range(KD):
                def issue(e, b=b, k=k, cols=cols):
                    w = W1[:, bass.ds(expert_on["pe"], 1), k, cols].rearrange("p o n -> p (o n)")
                    return e.matmul(PS[:, b, :], xgT[:, i, k, :], w, start=(k == 0), stop=(k == KD - 1))
                m = pe.add("w1", issue, [xgT_ready[n], w1_in, bank_busy[b]])
            if half == 0:
                c = activate("hid", hid[:, i, cols], PS[:, b, :], ACT.Copy, [m, hid_free[i]])
            else:
                c = copy("hid", hid[:, i, cols], PS[:, b, :], [m, hid_free[i]])
            bank_busy[b] = [c]
            hid_copied[n].append(c)
        xgT_free[i] = [m]

    def turn_hidden(n):
        i = n % 2
        load_expert(dve, n)
        hid_done[n] = []
        for half in range(2):
            b = HT_BANKS[half]
            for j in range(HALF):
                c = half * HALF + j
                m = turn("h_turn", PS[:, b, j * P:(j + 1) * P], hid[:, i, c * P:(c + 1) * P], ident,
                         [hid_copied[n][half], bank_busy[b]])
            cs = slice(half * HALF, (half + 1) * HALF)

            def add_bias(e, b=b, cs=cs):
                bias = b1[:, bass.ds(expert_on["dve"], 1), cs].rearrange("p o c -> p (o c)")
                return e.tensor_tensor(hidT[:, i, cs, :], PS[:, b, :].rearrange("p (c n) -> p c n", n=P),
                                       bias.unsqueeze(2).to_broadcast([P, HALF, P]), ALU.add)
            m2 = dve.add("b1", add_bias, [m, b_in, hidT_free[i]])
            bank_busy[b] = [m2]
            hid_done[n].append(activate("gelu", hidT[:, i, cs, :], hidT[:, i, cs, :], ACT.Gelu_apprx_tanh, [m2]))
        hid_free[i] = [m]

    def second_product(n):
        i, b = n % 2, Y_BANKS[n % 2]
        load_expert(pe, n)
        load_expert(dve, n)
        for c in range(KF):
            def issue(e, c=c):
                w = W2[:, bass.ds(expert_on["pe"], 1), c, :].rearrange("p o n -> p (o n)")
                return e.matmul(PS[:, b, 0:D], hidT[:, i, c, :], w, start=(c == 0), stop=(c == KF - 1))
            m = pe.add("w2", issue, [hid_done[n][c // HALF], w2_in, bank_busy[b]])
        hidT_free[i] = [m]

        def add_bias(e):
            bias = b2[:, bass.ds(expert_on["dve"], 1), :].rearrange("p o n -> p (o n)")
            return e.tensor_tensor(y1[:, i, :], PS[:, b, 0:D], bias, ALU.add)
        m = dve.add("b2", add_bias, [m, b_in, y1_free[i]])
        bank_busy[b] = [m]
        y1_free[i] = [dma(f"y1_{i}", result1[n * P:(n + 1) * P, :], y1[:, i, :], [m])]

    for n in range(3):
        load_rows(n)
    turn_tile(0)
    for n in range(TILES1 + 1):
        if n + 1 < TILES1:
            turn_tile(n + 1)
        if n + 3 < TILES1:
            load_rows(n + 3)
        if n:
            turn_hidden(n - 1)
        if n < TILES1:
            first_product(n)
        if n:
            second_product(n - 1)
    y1_written = y1_free[0] + y1_free[1]

    top[0] = persistent_top
    NB2 = 3
    xe = place("xe", [P, NB2, 4, D])
    se = place("se", [P, NB2, 4, D])
    ge = place("ge", [P, NB2, TOPK, 4, D])
    experts_done = [hidT_free[0], hidT_free[1]]
    e_free = [experts_done] * NB2
    s1_view = s1_dram.rearrange("(t p) d -> p t d", p=P)
    stored = []
    for q in range(NT // 4):
        i = q % NB2
        four = slice(4 * q, 4 * q + 4)
        dma(f"xe{i}", xe[:, i, :, :], x1_view[:, four, :], [x1_saved, e_free[i]])
        x_ready = dma(f"xe{i}", se[:, i, :, :], s1_view[:, four, :], [s1_saved, e_free[i]])
        for j in range(4):
            for k in range(TOPK):
                gm = gather(f"ge{i}", result1, SLOTS1, slot1[:, k, 4 * q + j:4 * q + j + 1], ge[:, i, k, j, :],
                            [y1_written, slot1_ready, e_free[i]])
        for j in range(4):
            t = 4 * q + j
            m = ts("mix1", ge[:, i, 0, j, :], ge[:, i, 0, j, :], weight1[:, 0, t:t + 1], None, ALU.mult,
                   after=[gm, weight1_ready])
            m = stt("mix1", ge[:, i, 0, j, :], ge[:, i, 1, j, :], weight1[:, 1, t:t + 1], ge[:, i, 0, j, :],
                    ALU.mult, ALU.add, [m])
        m = activate("silu1", ge[:, i, 0, :, :], ge[:, i, 0, :, :], ACT.Silu, [m])
        m = tt("mix1", ge[:, i, 0, :, :], ge[:, i, 0, :, :], se[:, i, :, :], ALU.mult, [m, x_ready])
        m = tt("mix1", xe[:, i, :, :], xe[:, i, :, :], ge[:, i, 0, :, :], ALU.add, [m])
        o = dma(f"out{i}", out_view[:, four, :], xe[:, i, :, :], [m])
        e_free[i] = [o]
        stored.append(o)
    replay(nc, (pe, dve, act, pool, sp), stored, sp)


def replay(nc, queues, finish, sp):
    sp.add("end", lambda e: e.nop(), finish)
    sems = {}
    for q in queues:
        for stage in q.count():
            sems[stage] = nc.alloc_semaphore(stage)
    pe, dve, act, pool, sp = queues
    with nc.Block() as block:
        block.tensor(lambda e: pe.emit(e, sems))
        block.vector(lambda e: dve.emit(e, sems))
        block.scalar(lambda e: act.emit(e, sems))
        block.gpsimd(lambda e: pool.emit(e, sems))
        block.sync(lambda e: sp.emit(e, sems))


STOP_AT = None


def kernel(**inputs):
    import concourse.bacc as bacc
    from concourse.bass_utils import run_bass_kernel_spmd

    as_np = {k: np.ascontiguousarray(v) for k, v in inputs.items()}
    const, dft, inv = CONSTS
    rel_at = np.arange(WIN)[:, None] - np.arange(WIN)[None, :] + WIN - 1
    rel = as_np["L0_attn_rel_bias"][rel_at].transpose(2, 0, 1)
    rel = rel.reshape(KD, 4, 2, WIN, WIN).transpose(2, 3, 0, 1, 4).reshape(P, KD, 4, WIN)
    proj = as_np["L0_attn_proj_w"].reshape(PAIRS, 2, HD, D).transpose(0, 2, 1, 3).reshape(P, 2, D)
    attn1_b = np.stack([as_np[f"L1_attn_b{c}"].reshape(KD, P).T for c in "qkv"], 1)
    data = {
        "const": const, "dft": dft, "inv": inv,
        "x": as_np["L0_attn_x"].reshape(T, D),
        "qkv_w": as_np["L0_attn_qkv_w"], "proj_w": proj, "proj_b": as_np["L0_attn_proj_b"],
        "qkv_b": as_np["L0_attn_qkv_b"].reshape(3 * KD, P).T, "v_b": as_np["L0_attn_qkv_b"][2 * D:],
        "rel": rel, "w_router": as_np["L0_ffn_w_router"], "w_gate": as_np["L0_ffn_w_gate"],
        "w_up": as_np["L0_ffn_w_up"], "w_down": as_np["L0_ffn_w_down"],
        "Wq": as_np["L1_attn_Wq"], "Wk": as_np["L1_attn_Wk"], "Wv": as_np["L1_attn_Wv"], "attn1_b": attn1_b,
        "Wg": as_np["L1_ffn_Wg"], "bg": as_np["L1_ffn_bg"], "W1": as_np["L1_ffn_W1"], "b1": as_np["L1_ffn_b1"].reshape(E1, F1 // P, P).transpose(2, 0, 1),
        "W2": as_np["L1_ffn_W2"], "b2": as_np["L1_ffn_b2"],
    }
    nc = bacc.Bacc("TRN2", target_bir_lowering=False, num_devices=1)
    arrays, a = {}, {}
    for name, v in data.items():
        arrays[f"in_{name}"] = np.ascontiguousarray(v)
        a[name] = nc.dram_tensor(f"in_{name}", v.shape, mybir.dt.from_np(v.dtype), kind="ExternalInput").ap()
    out = nc.dram_tensor("out", (T, D), F32, kind="ExternalOutput").ap()
    build(nc, a, out, STOP_AT)
    r = run_bass_kernel_spmd(nc, [arrays], core_ids=[0])
    return r.results[0]["out"].reshape(BATCH, SEQ, D)
```

```python
import numpy as np
import concourse.bass as bass
from concourse import mybir

F32 = mybir.dt.float32
I32 = mybir.dt.int32
ALU = mybir.AluOpType
ACT = mybir.ActivationFunctionType
AX = mybir.AxisListType

P = 128
BATCH, SEQ, D = 4, 1024, 256
T = BATCH * SEQ
NT = T // P
KD = D // P
LN_EPS = 1e-5
HEADS, WIN = 16, 64
HD = D // HEADS
PAIRS = HEADS // 2
E0, F0 = 32, 256
CAP = -(-5 * T // (4 * E0))
SLOTS0 = E0 * CAP
E1, F1, TOPK = 8, 1024, 2
TILES1 = (T * TOPK + E1 * (P - 1)) // P
SLOTS1 = TILES1 * P
UNIT_EPS, TOPK_EPS = 1e-8, 1e-8

CONST_COLS = {}


def constants():
    p = np.arange(P)
    parts = [
        ("ident", np.eye(P)),
        ("before", (p[:, None] < p[None, :])),
        ("upto", (p[:, None] <= p[None, :])),
        ("ones", np.ones((P, P))),
        ("head_scale", np.stack([(p // HD % 2 == e) * HD ** -0.5 for e in range(2)], 1)),
        ("iota0", np.tile(np.arange(E0), (P, 1))),
        ("iota0_low", np.tile(np.arange(E0) - E0, (P, 1))),
        ("iota1_low", np.tile(np.arange(E1) - E1, (P, 1))),
        ("result_row", (np.arange(TOPK * NT) * P)[None, :] + p[:, None]),
        ("tile_start", np.tile(np.arange(TILES1) * P, (P, 1))),
    ]
    at = 0
    for name, a in parts:
        CONST_COLS[name] = (at, at + a.shape[1])
        at += a.shape[1]
    const = np.concatenate([a for _, a in parts], 1).astype(np.float32)
    n, f = np.arange(D), np.arange(P)
    ang = 2 * np.pi * (np.outer(n, f) % D) / D
    alt = (-1.0) ** n
    dft = np.concatenate([np.cos(ang), -np.sin(ang), alt[:, None]], 1)
    dft[:, P] = 0.0
    w = np.where(f == 0, 1.0, 2.0)[:, None] / D
    inv_im = -w * np.sin(ang.T)
    inv_im[0] = alt / D
    inv = np.stack([w * np.cos(ang.T), inv_im], 1)
    return const, dft.astype(np.float32), inv.astype(np.float32)


CONSTS = constants()


class Mark:

    def __init__(self, stage):
        self.stage, self.awaited, self.count = stage, False, 0


def named(marks):
    if isinstance(marks, Mark):
        return [marks]
    return [x for m in marks or () for x in named(m)]


class Queue:

    def __init__(self, name):
        self.name, self.steps = name, []

    def add(self, stage, issue, after, dma=False):
        waits = named(after)
        for m in waits:
            m.awaited = True
        mark = Mark(f"{self.name}_{stage}")
        self.steps.append((issue, waits, mark, dma))
        return mark

    def count(self):
        values = {}
        for _, _, mark, dma in self.steps:
            if dma or mark.awaited:
                values[mark.stage] = values.get(mark.stage, 0) + (16 if dma else 1)
                mark.count = values[mark.stage]
        return values

    def emit(self, engine, sems):
        seen = {}
        for issue, waits, mark, dma in self.steps:
            need = {}
            for m in waits:
                need[m.stage] = max(need.get(m.stage, 0), m.count)
            for name, count in need.items():
                if seen.get(name, 0) < count:
                    engine.wait_ge(sems[name], count)
                    seen[name] = count
            instruction = issue(engine)
            if dma:
                instruction.then_inc(sems[mark.stage], 16)
            elif mark.awaited:
                instruction.then_inc(sems[mark.stage], 1)


def build(nc, a, out):
    pe, dve, act, pool, sp = Queue("pe"), Queue("dve"), Queue("act"), Queue("pool"), Queue("sp")

    def mm(stage, o, lhsT, rhs, start, stop, after=()):
        return pe.add(stage, lambda e: e.matmul(o, lhsT, rhs, start=start, stop=stop), after)

    def turn(stage, o, i, ident, after=()):
        return pe.add(stage, lambda e: e.transpose(o, i, ident), after)

    def activate(stage, o, i, func, after=(), bias=0.0, scale=1.0):
        if func == ACT.Copy:
            return act.add(stage, lambda e: e.activation(o, i, func), after)
        return act.add(stage, lambda e: e.activation(o, i, func, bias=bias, scale=scale), after)

    def tt(stage, o, i0, i1, op, after=(), on=dve):
        return on.add(stage, lambda e: e.tensor_tensor(o, i0, i1, op), after)

    def ts(stage, o, i, s1, s2, op0, op1=None, after=(), on=dve):
        if op1 is None:
            return on.add(stage, lambda e: e.tensor_scalar(o, i, s1, None, op0), after)
        return on.add(stage, lambda e: e.tensor_scalar(o, i, s1, s2, op0, op1), after)

    def stt(stage, o, i0, s, i1, op0, op1, after=()):
        return dve.add(stage, lambda e: e.scalar_tensor_tensor(out=o, in0=i0, scalar=s, in1=i1, op0=op0, op1=op1),
                       after)

    def reduce(stage, o, i, op, after=()):
        return dve.add(stage, lambda e: e.tensor_reduce(o, i, AX.X, op), after)

    def copy(stage, o, i, after=(), on=dve):
        return on.add(stage, lambda e: e.tensor_copy(o, i), after)

    def recip(stage, o, i, after=()):
        return dve.add(stage, lambda e: e.reciprocal(o, i), after)

    def fill(stage, o, value, after=(), on=dve):
        return on.add(stage, lambda e: e.memset(o, value), after)

    def dma(stage, o, i, after=(), on=sp):
        return on.add(stage, lambda e: e.dma_start(o, i), after, dma=True)

    top, SBUF_END = [16512], 229344

    def place(name, shape, dtype=F32):
        size = 4
        for n in shape[1:]:
            size *= n
        t = nc.alloc_sbuf_tensor_at(name, list(shape), dtype, offset=top[0])
        top[0] += -(-size // 32) * 32
        assert top[0] <= SBUF_END, (name, top[0])
        return t

    PS = nc.alloc_psum_tensor("PS", [P, 8, 512], F32)
    bank_busy = [[] for _ in range(8)]

    def dram(name, shape):
        return nc.dram_tensor(name, shape, F32, kind="Internal").ap()

    table0, result0 = dram("table0", (SLOTS0, D)), dram("result0", (SLOTS0, D))
    table1, result1 = dram("table1", (SLOTS1, D)), dram("result1", (TOPK * T, D))
    row_of = dram("row_of", (SLOTS1, 1))
    wf_dram = dram("wf_dram", (P, 3 * KD * (D + 1)))
    x1_dram, s1_dram = dram("x1_dram", (T, D)), dram("s1_dram", (T, D))

    const = place("const", [P, CONSTS[0].shape[1]])
    C = {n: const[:, lo:hi] for n, (lo, hi) in CONST_COLS.items()}
    const_in = dma("const", const[:, :], a["const"])
    ident = C["ident"]
    gate_eff = place("gate_eff", [P, NT])
    slot_put = place("slot_put", [P, NT], I32)
    slot_get = place("slot_get", [P, NT], I32)
    slot1 = place("slot1", [P, TOPK, NT], I32)
    weight1 = place("weight1", [P, TOPK, NT])
    row_of_slot = place("row_of_slot", [P, TILES1], I32)
    tile_expert = place("tile_expert", [1, TILES1], I32)
    stats = place("stats", [P, NT, 6])
    mean_var = place("mean_var", [P, NT, 2])
    rstd = place("rstd", [P, NT])
    NB = D + 1
    RN = E1 + 3
    router1 = place("router1", [P, KD, RN])
    router1_out = place("router1_out", [P, NT, RN])
    router1_b = place("router1_b", [P, E1])
    bn = place("bn", [P, 3, KD])
    bf = place("bf", [P, 3, 2])
    nyq_b = place("nyq_b", [P, 3])
    persistent_top = top[0]
    X = place("X", [P, NT, D])
    xn_base = top[0]
    XN = place("XN", [P, NT, D])
    after_xn = top[0]
    XT = place("XT", [P, NT // 2, KD, 2 * P])
    s_base = top[0]
    S = place("S", [P, NT, D])
    work = top[0]

    x_view = a["x"].rearrange("(t p) d -> p t d", p=P)
    x_in = [dma(f"x{i}", X[:, 4 * i:4 * i + 4, :], x_view[:, 4 * i:4 * i + 4, :]) for i in range(NT // 4)]

    top[0] = SBUF_END - 12 * D
    zeros = place("zeros", [P, D])
    zeroed = fill("zero", zeros[:, :], 0.0, on=pool)

    def zero_table(n, table, slots, after):
        rows = slots // P
        return dma(f"zero{n}", table.rearrange("(p r) d -> p r d", p=P),
                   zeros[:, :].unsqueeze(1).to_broadcast([P, rows, D]), [zeroed, after], on=pool)

    table0_zeroed = zero_table(0, table0, SLOTS0, x_in[-1])
    table1_zeroed = zero_table(1, table1, SLOTS1, x_in[-1])
    top[0] = SBUF_END - 8 * D
    no_row = place("no_row", [P, TILES1])
    m = fill("no_row", no_row[:, :], float(TOPK * T), on=pool)
    row_of_filled = dma("no_row_out", row_of.rearrange("(p r) o -> p (r o)", p=P), no_row[:, :], [m], on=pool)

    normed, turned = [None] * NT, [None] * (NT // 2)

    def ln_statistics(g, ready):
        for t in range(g, g + 8):
            s = dve.add("ln_stat", lambda e, t=t: e.bn_stats(stats[:, t, :], X[:, t, :]), ready(t))
            m = dve.add("ln_aggr", lambda e, t=t: e.bn_aggr(mean_var[:, t, :], stats[:, t, :]), [s])
        r = ts("ln_var", rstd[:, g:g + 8], mean_var[:, g:g + 8, 1], LN_EPS, None, ALU.add, after=[m])
        return activate("ln_sqrt", rstd[:, g:g + 8], rstd[:, g:g + 8], ACT.Sqrt, [r])

    def ln_normalize(g, root):
        r = recip("ln_rstd", rstd[:, g:g + 8], rstd[:, g:g + 8], [root])
        for t in range(g, g + 8):
            normed[t] = ts("ln_xn", XN[:, t, :], X[:, t, :], mean_var[:, t, 0:1], rstd[:, t:t + 1],
                           ALU.subtract, ALU.mult, [r])

    def ln_turn(g, banks):
        for t in range(g, g + 8, 2):
            b = banks[(t // 2) % 2]
            out_v = PS[:, b, :].rearrange("p (k n) -> p k n", k=KD)
            for k in range(KD):
                for j in range(2):
                    m = turn("ln_turn", out_v[:, k, j * P:(j + 1) * P], XN[:, t + j, k * P:(k + 1) * P], ident,
                             [normed[t + j], const_in, bank_busy[b]])
            turned[t // 2] = activate("ln_xt", XT[:, t // 2, :, :], out_v, ACT.Copy, [m])
            bank_busy[b] = [turned[t // 2]]

    def router_logits(g, router, router_in, n_e, banks):
        per = NT // len(banks)
        for t in range(g, g + 8):
            b = banks[t // per % len(banks)]
            for k in range(KD):
                o = PS[:, b, (t % per) * n_e:(t % per + 1) * n_e]
                m = mm("router", o, XT[:, t // 2, k, (t % 2) * P:(t % 2 + 1) * P], router[:, k, :], k == 0,
                       k == KD - 1, [turned[t // 2], router_in, bank_busy[b]])
        return m

    def over_experts(v, n_e):
        return v.unsqueeze(2).to_broadcast([P, NT, n_e])

    def over_tiles(v, n_e):
        return v.unsqueeze(1).to_broadcast([P, NT, n_e])

    def first_best(scores, best, iota_low, n_e, tmp, hot, first, ready):
        m = tt("route", tmp, scores, over_experts(best, n_e), ALU.is_equal, [ready])
        m = stt("route", tmp, tmp, -float(n_e), over_tiles(iota_low, n_e), ALU.mult, ALU.add, [m])
        m = reduce("route", first, tmp, ALU.min, [m])
        m = ts("route", first, first, float(n_e), None, ALU.add, after=[m])
        return tt("route", hot, over_tiles(iota_low, n_e), over_experts(first, n_e), ALU.is_equal, [m])

    def count_before(hot, n_e, hot_ready, banks, reset, reset_ready, totals, running, pos):
        w = NT * n_e
        flat = hot.rearrange("p t e -> p (t e)")
        n = -(-w // 512)
        m = None
        for i in range(n):
            lo, hi = i * 512, min((i + 1) * 512, w)
            m = mm("count", PS[:, banks[i], 0:hi - lo], C["before"], flat[:, lo:hi], True, True,
                   [hot_ready, const_in, bank_busy[banks[i]]])
            m = mm("count", PS[:, banks[n + i], 0:hi - lo], C["ones"], flat[:, lo:hi], True, True,
                   [bank_busy[banks[n + i]]])
        tot_te = totals.rearrange("p e t -> p t e")
        per = 512 // n_e
        for i in range(n):
            t0, t1 = i * per, min((i + 1) * per, NT)
            src = PS[:, banks[n + i], 0:(t1 - t0) * n_e].rearrange("p (t e) -> p t e", e=n_e)
            c = copy("route", tot_te[:, t0:t1, :], src, [m])
            bank_busy[banks[n + i]] = [c]
        f = lambda v: v.rearrange("p e t -> p (e t)")
        s = dve.add("route", lambda e: e.tensor_tensor_scan(f(running), f(reset), f(totals), 0.0,
                                                            ALU.mult, ALU.add), [c, reset_ready])
        d = tt("route", f(running), f(running), f(totals), ALU.subtract, [s])
        run_te = running.rearrange("p e t -> p t e")
        for i in range(n):
            t0, t1 = i * per, min((i + 1) * per, NT)
            src = PS[:, banks[i], 0:(t1 - t0) * n_e].rearrange("p (t e) -> p t e", e=n_e)
            c = tt("route", pos[:, t0:t1, :], src, run_te[:, t0:t1, :], ALU.add, [d])
            bank_busy[banks[i]] = [c]
        return c

    def make_reset(reset, after):
        m = fill("route", reset, 1.0, after)
        return fill("route", reset[:, :, 0:1], 0.0, [m])

    def scatter(stage, table, slots, idx, row, after):
        return pool.add(stage, lambda e: e.indirect_dma_start(
            out=table, out_offset=bass.IndirectOffsetOnAxis(ap=idx, axis=0), in_=row, in_offset=None,
            bounds_check=slots - 1, oob_is_err=False), after, dma=True)

    def gather(stage, table, slots, idx, row, after):
        return pool.add(stage, lambda e: e.indirect_dma_start(
            out=row, out_offset=None, in_=table, in_offset=bass.IndirectOffsetOnAxis(ap=idx, axis=0),
            bounds_check=slots - 1, oob_is_err=False), after, dma=True)

    top[0] = work
    router0 = place("router0", [P, KD, E0])
    qkv_w = place("qkv_w", [P, KD, 3 * D])
    qkv_w_top = top[0]
    proj_w = place("proj_w", [P, 2, D])
    qkv_b = place("qkv_b", [P, 3 * KD])
    q_bias = place("q_bias", [P, 2, KD])
    v_bias = place("v_bias", [P, 2, D])
    proj_b = place("proj_b", [P, D])
    rel = place("rel", [P, KD, 4, WIN])
    best0 = place("best0", [P, NT])
    first0 = place("first0", [P, NT])
    pos0 = place("pos0", [P, NT])
    taken0 = place("taken0", [P, NT])
    l0_work = top[0]
    router0_in = dma("router0", router0[:, :, :], a["w_router"].rearrange("(k p) e -> p k e", p=P))
    qkv_w_in = dma("qkv_w", qkv_w[:, :, :], a["qkv_w"].rearrange("(k p) n -> p k n", p=P))
    attn_in = [dma("attn_w", proj_w[:, :, :], a["proj_w"]),
               dma("attn_w", qkv_b[:, :], a["qkv_b"]),
               dma("attn_w", v_bias[:, 0, :], a["v_b"].partition_broadcast(P)),
               dma("attn_w", v_bias[:, 1, :], a["v_b"].partition_broadcast(P)),
               dma("attn_w", proj_b[:, :], a["proj_b"].partition_broadcast(P)),
               dma("attn_w", rel[:, :, :, :], a["rel"])][-1]
    SCORE_BANKS, MISC, GU_BANKS, PV_BANKS = [0, 1], [2, 3], [4, 5], [6, 7]
    FIRST_TILES = 8
    top[0] = s_base + FIRST_TILES * D * 4
    logit0 = place("logit0", [P, NT, E0])
    tmp0 = place("tmp0", [P, NT, E0])
    hot0 = place("hot0", [P, NT, E0])
    totals0 = place("totals0", [P, E0, NT])
    running0 = place("running0", [P, E0, NT])
    reset0 = place("reset0", [P, E0, NT])
    assert top[0] <= work
    routed, normed0, turned0 = {}, [], []

    def start0():
        roots, lg_marks = {}, []
        for g in range(0, NT, 8):
            roots[g] = ln_statistics(g, lambda t: [x_in[t // 4]])
            if g:
                ln_normalize(g - 8, roots[g - 8])
                ln_turn(g - 8, GU_BANKS)
                lg_marks.append(router_logits(g - 8, router0, router0_in, E0, PV_BANKS))
                yield
        ln_normalize(g, roots[g])
        ln_turn(g, GU_BANKS)
        lg_marks.append(router_logits(g, router0, router0_in, E0, PV_BANKS))
        normed0[:], turned0[:] = normed, turned
        per = 512 // E0
        reset_ready = make_reset(reset0[:, :, :], [])
        for i in range(2):
            m = copy("route", logit0[:, i * per:(i + 1) * per, :],
                     PS[:, PV_BANKS[i], :].rearrange("p (t e) -> p t e", e=E0), [lg_marks])
            bank_busy[PV_BANKS[i]] = [m]
        mb = reduce("route", best0[:, :], logit0[:, :, :], ALU.max, [m])
        yield
        hot_ready = first_best(logit0[:, :, :], best0[:, :], C["iota0_low"], E0, tmp0[:, :, :], hot0[:, :, :],
                               first0[:, :], mb)
        pos_ready = count_before(hot0[:, :, :], E0, hot_ready, [4, 5, 6, 7], reset0[:, :, :], reset_ready,
                                 totals0[:, :, :], running0[:, :, :], tmp0[:, :, :])
        yield
        m = tt("route", tmp0[:, :, :], tmp0[:, :, :], hot0[:, :, :], ALU.mult, [pos_ready])
        m = reduce("route", pos0[:, :], tmp0[:, :, :], ALU.add, [m])
        tk = ts("route", taken0[:, :], pos0[:, :], float(CAP), None, ALU.is_lt, after=[m])
        m = stt("route", pos0[:, :], first0[:, :], float(CAP), pos0[:, :], ALU.mult, ALU.add, [tk])
        m = ts("route", pos0[:, :], pos0[:, :], float(SLOTS0), None, ALU.add, after=[m])
        m = stt("route", pos0[:, :], taken0[:, :], -float(2 * SLOTS0), pos0[:, :], ALU.mult, ALU.add, [m])
        m = ts("route", pos0[:, :], pos0[:, :], float(2 * SLOTS0), None, ALU.add, after=[m])
        put_ready = copy("route", slot_put[:, :], pos0[:, :], [m])
        for t in range(NT):
            routed["scattered"] = scatter("scatter0", table0, SLOTS0, slot_put[:, t:t + 1], XN[:, t, :],
                                          [put_ready, normed0[t], table0_zeroed])
        yield
        m = ts("route", pos0[:, :], pos0[:, :], float(SLOTS0 - 1), None, ALU.min, after=[put_ready])
        routed["get"] = copy("route", slot_get[:, :], pos0[:, :], [m])
        m = tt("route", logit0[:, :, :], logit0[:, :, :], over_experts(best0[:, :], E0), ALU.subtract, [hot_ready])
        m = activate("route_exp", logit0[:, :, :], logit0[:, :, :], ACT.Exp, [m])
        yield
        m = reduce("route", gate_eff[:, :], logit0[:, :, :], ALU.add, [m])
        m = recip("route", gate_eff[:, :], gate_eff[:, :], [m])
        routed["gate"] = tt("route", gate_eff[:, :], gate_eff[:, :], taken0[:, :], ALU.mult, [m, tk])
        yield

    UNITS, UW, UT, SR, PR0, STEPS = NT // 2, 4, 2 * P, 2, 3, 2 * NT
    top[0] = l0_work
    Q2 = place("Q2", [P, 2, KD, UW, 2, WIN])
    KB = place("KB", [P, KD, UW, 4, WIN])
    VW = 2 * HD + 1
    VB = place("VB", [P, 2, 2, PAIRS, 2, VW])
    sc = place("sc", [P, SR, KD, 4, WIN])
    sc_max = place("sc_max", [P, SR, KD * 4])
    prob_base = top[0]
    prob = place("prob", [P, PR0, KD, 4, 2, WIN])
    PT = place("PT", [P, 2, KD, 4, P])
    after_pt = top[0]
    inv_sum = place("inv_sum", [P, KD, 4, 2])
    O = place("O", [P, 2, PAIRS, HD])
    OT = place("OT", [P, 2, P])
    after_ot = top[0]
    y0 = place("y0", [P, 2, 2, D])
    top[0] = after_ot
    got0 = place("got0", [P, 2, 4, D])
    top[0] = persistent_top
    GROUP = 4
    GT = GROUP * CAP // P
    rows0 = place("rows0", [P, 2, D])
    rowsT = place("rowsT", [P, 2, KD, GROUP * CAP])
    wgt0 = place("wgt0", [P, 2, 3, KD, F0])
    silu0 = place("silu0", [P, 2, KD, CAP])
    hT0 = place("hT0", [P, 2, KD, CAP])
    assert top[0] <= xn_base
    kb_zeroed = fill("kb_zero", KB[:, :, :, :, :], 0.0, on=pool)
    vb_zeroed = fill("vb_zero", VB[:, :, :, :, :, :], 0.0, on=pool)
    for w2 in range(2):
        v_ones = fill("v_ones", VB[64 * w2:64 * w2 + 64, :, :, :, w2, HD:HD + 1], 1.0, [vb_zeroed], on=pool)
    turn_of = {"misc": 0, "gu": 0}

    def next_bank(kind, banks):
        turn_of[kind] += 1
        return banks[turn_of[kind] % 2]

    q_done, k_done, v_done, exp_done, pt_done, norm_done, ot_done, s_done = {}, {}, {}, {}, {}, {}, {}, {}
    q2_free, kb_free, v_free, pt_free = [[], []], [], [[], []], [[], []]
    sc_free, prob_free = [[]] * SR, [[]] * PR0
    o_free, ot_free, inv_free, qkv_done = [], [], [], []

    def project_qk(u, which):
        i = u % 2
        b = next_bank("misc", MISC)
        for c in range(KD):
            for k in range(KD):
                col = which * D + c * P
                m = mm("qkv", PS[:, b, c * UT:(c + 1) * UT], qkv_w[:, k, col:col + P], XT[:, u, k, :],
                       k == 0, k == KD - 1, [qkv_w_in, turned[u], bank_busy[b]])
        outs = []
        for c in range(KD):
            src = PS[:, b, c * UT:(c + 1) * UT].rearrange("p (w q) -> p w q", w=UW)
            if which == 0:
                for e in range(2):
                    outs.append(activate("q_out", Q2[:, i, c, :, e, :], src, ACT.Identity, [m, qb, q2_free[i]],
                                         bias=q_bias[:, e, c:c + 1], scale=C["head_scale"][:, e:e + 1]))
            else:
                for g in range(4):
                    rows = slice(32 * g, 32 * g + 32)
                    after = [m, attn_in, kb_zeroed, list(kb_free)]
                    bias = qkv_b[rows, KD + c:KD + c + 1]
                    if g < 2:
                        outs.append(activate("k_out", KB[rows, c, :, g, :], src[rows], ACT.Identity, after, bias=bias))
                    else:
                        outs.append(ts("k_out", KB[rows, c, :, g, :], src[rows], bias, None, ALU.add, after=after))
        bank_busy[b] = outs
        (q_done, k_done)[which][u] = outs

    def project_v(u):
        i = u % 2
        b = next_bank("misc", MISC)
        for j in range(2):
            for k in range(KD):
                m = mm("qkv", PS[:, b, j * D:(j + 1) * D], XT[:, u, k, j * P:(j + 1) * P], qkv_w[:, k, 2 * D:3 * D],
                       k == 0, k == KD - 1, [qkv_w_in, turned[u], bank_busy[b]])
        split = "p (r e h) -> p r e h"
        for w2 in range(2):
            rows = slice(64 * w2, 64 * w2 + 64)
            for e in range(2):
                src = PS[rows, b, :].rearrange(split, e=2, h=HD)[:, :, e, :]
                bias = v_bias[rows, :, :].rearrange("p j n -> p (j n)").rearrange(split, e=2, h=HD)[:, :, e, :]
                o = VB[rows, i, :, :, w2, e * (HD + 1):e * (HD + 1) + HD].rearrange("p j r h -> p (j r) h")
                m2 = tt("v_out", o, src, bias, ALU.add, [m, attn_in, v_ones, v_free[i]])
        bank_busy[b] = [m2]
        v_done[u] = m2
        qkv_done[:] = [m]

    def score(s):
        u, w = divmod(s, UW)
        i, b, r = u % 2, SCORE_BANKS[s % 2], s % SR
        for c in range(KD):
            m = mm("scores", PS[:, b, c * 256:(c + 1) * 256], Q2[:, i, c, w, :, :].rearrange("p e q -> p (e q)"),
                   KB[:, c, w, :, :].rearrange("p g k -> p (g k)"), True, True,
                   [q_done[u], k_done[u], bank_busy[b]])
        if w == UW - 1:
            q2_free[i] = [m]
            kb_free[:] = [m]
        flat = sc[:, r, :, :, :].rearrange("p c g k -> p (c g k)")
        m2 = tt("sc_bias", flat, PS[:, b, :], rel[:, :, :, :].rearrange("p c g k -> p (c g k)"), ALU.add,
                [m, attn_in, sc_free[r]])
        bank_busy[b] = [m2]
        by_head = sc[:, r, :, :, :].rearrange("p c g k -> p (c g) k")
        m = reduce("sc_max", sc_max[:, r, :], by_head, ALU.max, [m2])
        m = tt("sc_sub", by_head, by_head, sc_max[:, r, :].unsqueeze(2).to_broadcast([P, KD * 4, WIN]), ALU.subtract,
               [m], on=dve if s < DVE_BUSY_STEP else pool)
        t, w2 = divmod(s, 2)
        exp_done[s] = activate("sc_exp", prob[:, t % PR0, :, :, w2, :].rearrange("p c g k -> p (c g) k"), by_head,
                               ACT.Exp, [m, prob_free[t % PR0]])
        sc_free[r] = [exp_done[s]]

    def turn_probabilities(t, c):
        b, r = next_bank("misc", MISC), t % PR0
        for g in range(4):
            m = turn("p_turn", PS[:, b, g * P:(g + 1) * P], prob[:, r, c, g, :, :].rearrange("p w k -> p (w k)"), ident,
                     [exp_done[2 * t], exp_done[2 * t + 1], bank_busy[b]])
        if c == KD - 1:
            prob_free[r] = [m]
        pt_done[t] = activate("pt_out", PT[:, t % 2, c, :, :].rearrange("p g n -> p (g n)"), PS[:, b, :], ACT.Copy,
                              [m, pt_free[t % 2]])
        bank_busy[b] = [pt_done[t]]

    def attend(t):
        u, j = divmod(t, 2)
        for c in range(KD):
            for g in range(4):
                m = mm("pv", PS[:, PV_BANKS[c], g * 2 * VW:(g + 1) * 2 * VW], PT[:, t % 2, c, g, :],
                       VB[:, u % 2, j, 4 * c + g, :, :].rearrange("p w n -> p (w n)"), True, True,
                       [pt_done[t], v_done[u], [bank_busy[x] for x in PV_BANKS]])
        pt_free[t % 2] = [m]
        if j == 1:
            v_free[u % 2] = [m]
        av = PS[:, PV_BANKS[0]:PV_BANKS[1] + 1, 0:4 * 2 * VW].rearrange("p c (g w n) -> p c g w n", g=4, w=2)
        for c in range(KD):
            r = recip("pv_inv", inv_sum[:, c, :, :], av[:, c, :, :, HD], [m, list(inv_free)])
        for e in range(2):
            rows = slice(64 * e, 64 * e + 64)
            for c in range(KD):
                n = tt("pv_norm", O[rows, :, 4 * c:4 * c + 4, :],
                       av[rows, c, :, :, e * (HD + 1):e * (HD + 1) + HD].rearrange("p g w h -> p w g h"),
                       inv_sum[rows, c, :, :].rearrange("p g w -> p w g").unsqueeze(3).to_broadcast([64, 2, 4, HD]),
                       ALU.mult, [r, list(o_free)])
        for x in PV_BANKS:
            bank_busy[x] = [n]
        inv_free[:] = [n]
        norm_done[t] = n

    def turn_heads(t):
        b = next_bank("misc", MISC)
        for w in range(2):
            m = turn("o_turn", PS[:, b, w * P:(w + 1) * P], O[:, w, :, :].rearrange("p r h -> p (r h)"), ident,
                     [norm_done[t], bank_busy[b]])
        o_free[:] = [m]
        m2 = activate("ot_out", OT[:, :, :].rearrange("p e (w q) -> p w e q", w=2),
                      PS[:, b, 0:2 * P].rearrange("p (w e q) -> p w e q", w=2, e=2), ACT.Copy, [m, list(ot_free)])
        bank_busy[b] = [m2]
        ot_done[t] = m2

    def project_out(t):
        b = next_bank("misc", MISC)
        for e in range(2):
            m = mm("proj", PS[:, b, 0:D], OT[:, e, :], proj_w[:, e, :], e == 0, e == 1,
                   [ot_done[t], attn_in, bank_busy[b]])
        ot_free[:] = [m]
        s_done[t] = tt("s_out", S[:, t, :], PS[:, b, 0:D], proj_b[:, :], ALU.add,
                       [m, routed["gate"] if t >= FIRST_TILES else None])
        bank_busy[b] = [s_done[t]]

    top[0] = prob_base
    dft = place("dft", [P, KD, NB])
    Wn = place("Wn", [P, 3, KD, D])
    WF0 = place("WF0", [P, 3, KD, NB])
    b_rep = place("b_rep", [P, KD, P])
    assert top[0] <= after_pt
    QQ, KK, VV = 0, 1, 2
    router1_in = dma("router1", router1[:, :, 0:E1], a["Wg"].rearrange("(k p) e -> p k e", p=P))
    dft_in = [dma("dft", dft[:, :, :], a["dft"].rearrange("(k p) n -> p k n", p=P)),
              dma("dft", router1_b[:, :], a["bg"].partition_broadcast(P)),
              dma("dft", bn[:, :, :], a["attn1_b"])][-1]
    wn_in = [dma(f"wn{n}", Wn[:, n, :, :], a[name].rearrange("(k p) n -> p k n", p=P))
             for n, name in enumerate(("Wq", "Wk", "Wv"))]

    def fold_dft():
        for n in range(3):
            for c in range(KD):
                for k in range(KD):
                    m = mm("wf", PS[:, c, 0:NB], Wn[:, n, k, c * P:(c + 1) * P], dft[:, k, :], k == 0, k == KD - 1,
                           [wn_in[n], dft_in, bank_busy[c]])
                w = activate("wf_out", WF0[:, n, c, :], PS[:, c, 0:NB], ACT.Copy, [m])
                bank_busy[c] = [w]
            for part in range(2):
                for k in range(KD):
                    m = mm("bf", PS[:, 2, 2 * n + part:2 * n + part + 1], dft[:, k, part * P:(part + 1) * P],
                           bn[:, n, k:k + 1], k == 0, k == KD - 1, [bank_busy[2]])
            r = activate("b_rep", b_rep[:, :, :], bn[:, n, :].unsqueeze(2).to_broadcast([P, KD, P]), ACT.Copy,
                         [dft_in, m])
            for k in range(KD):
                m = mm("bf", PS[:, 2, 8 + n:9 + n], b_rep[:, k, :], dft[:, k, D:NB], k == 0, k == KD - 1, [r])
        activate("bf_out", bf[:, :, :], PS[:, 2, 0:6].rearrange("p (n r) -> p n r", n=3), ACT.Copy, [m])
        b = activate("bf_out", nyq_b[:, :], PS[:, 2, 8:11], ACT.Copy, [m])
        bank_busy[2] = [b]
        r = activate("rn_out", router1[:, :, E1:RN].rearrange("p k n -> p n k"), WF0[:, :, :, D], ACT.Copy, [w])
        saved = dma("wf_save", wf_dram, WF0[:, :, :, :].rearrange("p n k f -> p (n k f)"), [w])
        return b, r, saved

    tail = CAP - P
    rowsT_ready, rowsT_free = {}, [[], []]
    y_stored = [[], []]

    def expert0():
        x_done = list(normed0)
        rows_free, gu_free, down_free = [x_done] * 2, [x_done] * 2, [x_done] * 2
        silu_free, h_free = [x_done] * 2, [x_done] * 2
        for i in range(2):
            rowsT_free[i] = x_done

        def load_gate_up(ex):
            i = ex % 2
            for n, name in enumerate(("w_gate", "w_up")):
                gu_in[ex] = dma(f"gu_{i}", wgt0[:, i, n, :, :], a[name][ex].rearrange("(k p) n -> p k n", p=P),
                                gu_free[i])

        def load_down(ex):
            i = ex % 2
            down_in[ex] = dma(f"dn_{i}", wgt0[:, i, 2, :, :], a["w_down"][ex].rearrange("(k p) n -> p k n", p=P),
                              down_free[i])

        def load_rows0(n):
            i = n % 2
            if n < SLOTS0 // P:
                rows_in[n] = dma(f"rows0_{i}", rows0[:, i, :], table0[n * P:(n + 1) * P, :],
                                 [routed["scattered"], rows_free[i]])

        def turn_rows(grp, t):
            n = grp * GT + t
            gi, i = grp % 2, n % 2
            b = next_bank("misc", MISC)
            for k in range(KD):
                m = turn("rows_turn", PS[:, b, k * P:(k + 1) * P], rows0[:, i, k * P:(k + 1) * P], ident,
                         [rows_in[n], bank_busy[b]])
            rows_free[i] = [m]
            load_rows0(n + 2)
            rt = activate("rowsT_out", rowsT[:, gi, :, t * P:(t + 1) * P],
                          PS[:, b, 0:KD * P].rearrange("p (k n) -> p k n", k=KD), ACT.Copy, [m, rowsT_free[gi]])
            bank_busy[b] = [rt]
            rowsT_ready[grp] = rt

        def gate_up(ex, f):
            grp, j = divmod(ex, GROUP)
            gi, i = grp % 2, ex % 2
            b = next_bank("gu", GU_BANKS)
            for n in range(2):
                for k in range(KD):
                    m = mm("gate_up", PS[:, b, n * CAP:(n + 1) * CAP], wgt0[:, i, n, k, f * P:(f + 1) * P],
                           rowsT[:, gi, k, j * CAP:(j + 1) * CAP], k == 0, k == KD - 1,
                           [gu_in[ex], rowsT_ready[grp], bank_busy[b]])
            s = activate("silu0", silu0[:, i, f, :], PS[:, b, 0:CAP], ACT.Tanh, [m, silu_free[i]], scale=0.5)
            s = stt("h0", silu0[:, i, f, :], silu0[:, i, f, :], 1.0, PS[:, b, 0:CAP], ALU.add, ALU.mult, [s])
            h = stt("h0", hT0[:, i, f, :], silu0[:, i, f, :], 0.5, PS[:, b, CAP:2 * CAP], ALU.mult, ALU.mult,
                    [s, h_free[i]])
            bank_busy[b] = [h]
            if f == KD - 1:
                silu_free[i], h_ready[ex], gu_free[i] = [h], h, [m]
                if j == GROUP - 1:
                    rowsT_free[gi] = [m]

        def down(ex):
            i, b = ex % 2, next_bank("misc", MISC)
            for f in range(KD):
                m = mm("down0", PS[:, b, 0:D], hT0[:, i, f, 0:P], wgt0[:, i, 2, f, :], f == 0, f == KD - 1,
                       [h_ready[ex], down_in[ex], bank_busy[b]])
            for f in range(KD):
                m = mm("down0", PS[0:tail, b, D:2 * D], hT0[:, i, f, P:CAP], wgt0[:, i, 2, f, :], f == 0,
                       f == KD - 1)
            down_free[i] = h_free[i] = [m]
            c1 = copy("y0", y0[:, i, 0, :], PS[:, b, 0:D], [m, y_stored[i]])
            c2 = copy("y0", y0[0:tail, i, 1, :], PS[0:tail, b, D:2 * D], [])
            bank_busy[b] = [c2]
            at = ex * CAP
            y_stored[i] = [dma(f"y0_{i}", result0[at:at + P, :], y0[:, i, 0, :], [c1], on=pool),
                           dma(f"y0_{i}", result0[at + P:at + CAP, :], y0[0:tail, i, 1, :], [c2], on=pool)]

        gu_in, down_in, h_ready, rows_in = {}, {}, {}, {}
        load_rows0(0)
        load_rows0(1)
        for ex in range(2):
            load_gate_up(ex)
            load_down(ex)
        for t in range(GT):
            turn_rows(0, t)
            if t % 2:
                yield
        for ex in range(E0):
            grp, j = divmod(ex, GROUP)
            gate_up(ex, 0)
            if grp + 1 < E0 // GROUP:
                for t in ((0,), (1,), (2,), (3, 4))[j]:
                    turn_rows(grp + 1, t)
            yield
            if ex:
                down(ex - 1)
                if 2 <= ex + 1 < E0:
                    load_down(ex + 1)
                yield
            gate_up(ex, 1)
            if ex + 2 < E0:
                load_gate_up(ex + 2)
            yield
        down(E0 - 1)
        yield

    FIRST_EXPERT_STEP = 7
    DVE_BUSY_STEP = 50
    EXPERT_PIECES = 2

    def advance(generator, n=1):
        return [next(generator, generator) for _ in range(n)][-1] is generator

    x1_ready, x1_saved, x_again = [], [], []
    got_free = [[table0_zeroed, table1_zeroed, row_of_filled]] * 2
    x1_view = x1_dram.rearrange("(t p) d -> p t d", p=P)
    y_written, to_route = [], []

    def route_group(g):
        b = GU_BANKS[0]
        m = router_logits(g, router1, [router1_in, router1_ready], RN, [b] * (NT // 8))
        r = activate("rn_keep", router1_out[:, g:g + 8, :],
                     PS[:, b, 0:8 * RN].rearrange("p (t n) -> p t n", n=RN), ACT.Copy, [m])
        bank_busy[b] = [r]
        routed["logits1"] = r

    def combine_gather(q):
        i = q % 2
        for j in range(4):
            t = 4 * q + j
            gm = gather(f"got0_{i}", result0, SLOTS0, slot_get[:, t:t + 1], got0[:, i, j, :],
                        [routed["get"], y_written, got_free[i]])
        return gm

    def combine_gate(q, gathered):
        i = q % 2
        for j in range(4):
            t = 4 * q + j
            m = stt("mix0", got0[:, i, j, :], got0[:, i, j, :], gate_eff[:, t:t + 1], XN[:, t, :], ALU.mult, ALU.add,
                    [gathered, routed["gate"]])
        return activate("silu_mix0", got0[:, i, :, :], got0[:, i, :, :], ACT.Silu, [m])

    def combine_add(q, gated):
        i, four = q % 2, slice(4 * q, 4 * q + 4)
        m = tt("mix0", got0[:, i, :, :], got0[:, i, :, :], S[:, four, :], ALU.mult, [gated, s_done[4 * q + 3]])
        m = tt("mix0", X[:, four, :], X[:, four, :], got0[:, i, :, :], ALU.add, [m, x_again[q]])
        got_free[i] = [m]
        x1_saved.append(dma("x1_save", x1_view[:, four, :], X[:, four, :], [m]))
        x1_ready.append(m)

    def combination0():
        y_written[:] = y_stored[0] + y_stored[1]
        for i in range(NT // 4):
            x_again.append(dma(f"x{i}", X[:, 4 * i:4 * i + 4, :], x_view[:, 4 * i:4 * i + 4, :], y_written))
        gathered, gated, roots = {}, {}, {}
        for q in range(NT // 4 + 2):
            if q >= 2:
                while 4 * (q - 2) + 3 not in s_done:
                    yield
                combine_add(q - 2, gated[q - 2])
            if q < NT // 4:
                gathered[q] = combine_gather(q)
                if q == 0:
                    yield
            if 1 <= q <= NT // 4:
                gated[q - 1] = combine_gate(q - 1, gathered[q - 1])
            if q >= 2 and q % 2:
                g = 4 * (q - 3)
                yield
                roots[g] = ln_statistics(g, lambda t: [x1_ready[t // 4]])
                yield
                ln_normalize(g, roots[g])
                yield
                ln_turn(g, GU_BANKS)
                to_route.append(g)
            elif to_route:
                route_group(to_route.pop())
            yield
        route_group(to_route.pop())

    start, experts, combination = start0(), expert0(), combination0()
    advance(start, 3)
    for e in range(2):
        qb = ts("q_bias", q_bias[:, e, :], qkv_b[:, 0:KD], C["head_scale"][:, e:e + 1], None, ALU.mult,
                after=[attn_in, const_in])
    project_qk(0, 0)
    project_qk(0, 1)
    project_v(0)
    bf_ready, router1_ready, wf_saved = fold_dft()
    prob_free[:] = [[bf_ready, wf_saved]] * PR0
    pt_free[:] = [[bf_ready, wf_saved]] * 2
    advance(start, 3)
    score(0)
    score(1)
    for s in range(STEPS + 5):
        u, g = divmod(s, UW)
        if s + 2 < STEPS:
            score(s + 2)
        if u + 1 < UNITS and g < 3:
            (lambda: project_qk(u + 1, 0), lambda: project_qk(u + 1, 1), lambda: project_v(u + 1))[g]()
        advance(start)
        if s >= FIRST_EXPERT_STEP and advance(experts, EXPERT_PIECES):
            advance(combination)
        if s % 2 and 0 <= s - 3 < STEPS:
            attend((s - 3) // 2)
        if s % 2 and 0 <= s - 5 < STEPS:
            project_out((s - 5) // 2)
        if s % 2 == 0 and 0 <= s - 4 < STEPS:
            turn_heads((s - 4) // 2)
        if 0 <= s - 1 < STEPS:
            turn_probabilities(*divmod(s - 1, 2))
    for _ in combination:
        pass

    layer0_end = [s_done[NT - 1], y_written]
    top[0] = persistent_top
    sc1 = place("sc1", [P, NT, E1])
    prob1 = place("prob1", [P, NT, E1])
    tmp1 = place("tmp1", [P, NT, E1])
    hot1 = place("hot1", [P, TOPK, NT, E1])
    both1 = place("both1", [P, NT, E1])
    totals1 = place("totals1", [P, E1, NT])
    running1 = place("running1", [P, E1, NT])
    reset1 = place("reset1", [P, E1, NT])
    best1 = place("best1", [P, TOPK, NT])
    first1 = place("first1", [P, NT])
    sum1 = place("sum1", [P, NT])
    pad_i = place("pad_i", [P, E1], I32)
    pad_f = place("pad_f", [P, E1])
    pad_end = place("pad_end", [P, E1])
    pad_base = place("pad_base", [P, E1])
    owner = place("owner", [P, TILES1, E1])
    owner_f = place("owner_f", [P, TILES1])
    assert top[0] <= xn_base
    top[0] = work
    Wf = place("Wf", [P, 3, KD, NB])
    assert top[0] <= qkv_w_top
    top[0] = qkv_w_top
    inv = place("inv", [P, 2, D])
    nyq = place("nyq", [P, 3, NT])
    nyq_abs = place("nyq_abs", [P, 3, NT])
    nyq_sum = place("nyq_sum", [P, NT])
    nyq_scan = place("nyq_scan", [P, NT])
    nyq_reset = place("nyq_reset", [P, NT])
    nyq_T = place("nyq_T", [NT, P])
    CH = 2 * P
    Z = place("Z", [P, 3, 3, 2, CH])
    SQ = place("SQ", [P, 2, 3, 2, CH])
    MAG = place("MAG", [P, 3, 3, CH])
    PR = place("PR", [P, 2, 4, CH])
    RUN = place("RUN", [P, 2, 2, CH])
    U = place("U", [P, 2, 2, CH])
    s1 = place("s1", [P, 2, 2, D])

    wf_ready = dma("wf_back", Wf[:, :, :, :].rearrange("p n k f -> p (n k f)"), wf_dram, [qkv_done, wf_saved])
    inv_in = dma("inv", inv[:, :, :], a["inv"], layer0_end)
    nyq_reset_ready = fill("nyq", nyq_reset[:, :].rearrange("p (b t) -> p b t", b=BATCH)[:, :, 0:1], 0.0,
                           [fill("nyq", nyq_reset[:, :], 1.0, layer0_end)])

    routed1 = routed["logits1"]
    normed1, turned1 = list(normed), list(turned)

    out_view = out.rearrange("(t p) d -> p t d", p=P)
    x_free = x1_saved + [normed1[-1]]
    CHUNKS, PER_BATCH = T // CH, SEQ // CH
    mag_of, root_of, bound = {}, {}, {}
    z_free, mag_free, sq_free = [layer0_end] * 3, [x1_ready[-1:]] * 3, [layer0_end] * 2
    run_free, u_free, s1_free, pr_free = [[x1_ready[-1:]] * 2 for _ in range(4)]
    dft_done, z_done = {}, {}

    def spectra(ch):
        i3, i = ch % 3, ch % 2
        for n in (KK, VV, QQ):
            b = 3 * i + n
            for part in range(2):
                for k in range(KD):
                    m = mm("dft", PS[:, b, part * CH:(part + 1) * CH], Wf[:, n, k, part * P:(part + 1) * P],
                           XT[:, ch, k, :], k == 0, k == KD - 1, [wf_ready, turned1[ch], layer0_end, bank_busy[b]])
            for part in range(2):
                zz = activate("z", Z[:, i3, n, part, :], PS[:, b, part * CH:(part + 1) * CH], ACT.Identity,
                              [m, bf_ready, z_free[i3]], bias=bf[:, n, part:part + 1])
            bank_busy[b] = [zz]
            sq = activate("zsq", SQ[:, i, n, :, :], Z[:, i3, n, :, :], ACT.Square, [zz, sq_free[i]])
        dft_done[ch], z_done[ch] = m, sq
        mag_of[ch] = tt("mag", MAG[:, i3, :, :], SQ[:, i, :, 0, :], SQ[:, i, :, 1, :], ALU.add, [sq, mag_free[i3]],
                        on=pool)
        sq_free[i] = [mag_of[ch]]

    def magnitudes(ch):
        root_of[ch] = activate("mag_sqrt", MAG[:, ch % 3, :, :], MAG[:, ch % 3, :, :], ACT.Sqrt, [mag_of[ch]])

    run_last = []

    def bind(ch):
        i3, i = ch % 3, ch % 2
        z = lambda n, part: Z[:, i3, n, part, :]
        mag = lambda n: MAG[:, i3, n, :]
        wide = lambda n: MAG[:, i3, n, :].unsqueeze(1).to_broadcast([P, 2, CH])
        m = ts("inv", MAG[:, i3, :, :], MAG[:, i3, :, :], UNIT_EPS, None, ALU.add, after=[root_of[ch]])
        m = tt("inv", mag(VV), mag(VV), mag(KK), ALU.mult, [m])
        m = tt("inv", mag(KK), mag(VV), mag(QQ), ALU.mult, [m])
        r = recip("inv", mag(KK), mag(KK), [m])
        m = tt("inv", mag(QQ), mag(QQ), mag(KK), ALU.mult, [r])
        mq = tt("inv", mag(VV), mag(VV), mag(KK), ALU.mult, [r])
        m = tt("bind", Z[:, i3, KK, :, :], Z[:, i3, KK, :, :], wide(QQ), ALU.mult, [m, z_done[ch]])
        w = [m, pr_free[0]]
        m1 = tt("bind", PR[:, 0, 0:2, :], Z[:, i3, KK, :, :], Z[:, i3, VV, :, :], ALU.mult, w)
        tt("bind", PR[:, 0, 2, :], z(KK, 0), z(VV, 1), ALU.mult, w)
        m2 = tt("bind", PR[:, 0, 3, :], z(KK, 1), z(VV, 0), ALU.mult, w)
        qn = tt("unbind", Z[:, i3, QQ, :, :], Z[:, i3, QQ, :, :], wide(VV), ALU.mult, [mq])
        mag_free[i3] = [qn]
        runs = []
        for part, (x0, x1, op, mk) in enumerate(((0, 1, ALU.subtract, m1), (2, 3, ALU.add, m2))):
            initial = 0.0 if ch % PER_BATCH == 0 else RUN[:, 1 - i, part, CH - 1:CH]
            runs.append(dve.add("running", lambda e, o=RUN[:, i, part, :], x0=x0, x1=x1, op=op, initial=initial:
                                e.tensor_tensor_scan(o, PR[:, 0, x0, :], PR[:, 0, x1, :], initial, ALU.add, op),
                                [mk, list(run_last), run_free[i]]))
        pr_free[0] = list(runs)
        run_last[:] = runs
        on = pool if ch in UNBIND_ON_POOL else dve
        w = [qn, runs, pr_free[1]]
        m1 = tt("unbind", PR[:, 1, 0:2, :], RUN[:, i, :, :], Z[:, i3, QQ, :, :], ALU.mult, w, on=on)
        m2 = tt("unbind", PR[:, 1, 2, :], RUN[:, i, 1, :], z(QQ, 0), ALU.mult, w, on=on)
        m3 = tt("unbind", PR[:, 1, 3, :], RUN[:, i, 0, :], z(QQ, 1), ALU.mult, w, on=on)
        run_free[i], z_free[i3] = [m1, m2, m3], [m1, m2, m3]
        ur = tt("unbind", U[:, i, 0, :], PR[:, 1, 0, :], PR[:, 1, 1, :], ALU.add, [m1, u_free[i]], on=on)
        ui = tt("unbind", U[:, i, 1, :], PR[:, 1, 2, :], PR[:, 1, 3, :], ALU.subtract, [m2, m3, u_free[i]], on=on)
        pr_free[1] = [ur, ui]
        ny = dma(f"nyq_row{i}", U[0:1, i, 1, :].rearrange("o (t n) -> o t n", n=P), nyq_T[2 * ch:2 * ch + 2, :],
                 [nyq_ready, ui])
        bound[ch] = [ur, ny]

    def inverse(ch):
        i, b = ch % 2, 6 + ch % 2
        for j in range(2):
            for part in range(2):
                m = mm("idft", PS[:, b, j * D:(j + 1) * D], U[:, i, part, j * P:(j + 1) * P], inv[:, part, :],
                       part == 0, part == 1, [bound[ch], inv_in, bank_busy[b]])
        u_free[i] = [m]
        c = activate("s1_out", s1[:, i, :, :].rearrange("p j d -> p (j d)"), PS[:, b, :], ACT.Copy, [m, s1_free[i]])
        bank_busy[b] = [c]
        s1_free[i] = [dma(f"s1_save{i}", s1_dram[ch * CH:(ch + 1) * CH, :].rearrange("(t p) d -> p t d", p=P),
                          s1[:, i, :, :], [c])]

    UNBIND_ON_POOL = range(11, CHUNKS)

    n = tt("nyq", nyq[:, :, :], router1_out[:, :, E1:RN].rearrange("p t n -> p n t"),
           nyq_b[:, :].unsqueeze(2).to_broadcast([P, 3, NT]), ALU.add, [routed1, bf_ready, layer0_end])
    m = tt("route", sc1[:, :, :], router1_out[:, :, 0:E1], over_tiles(router1_b[:, :], E1), ALU.add,
           [routed1, dft_in, x_free])
    spectra(0)
    spectra(1)
    magnitudes(0)
    m = reduce("route", first1[:, :], sc1[:, :, :], ALU.max, [m])
    m = tt("route", sc1[:, :, :], sc1[:, :, :], over_experts(first1[:, :], E1), ALU.subtract, [m])
    m = activate("route_exp", prob1[:, :, :], sc1[:, :, :], ACT.Exp, [m])
    n = stt("nyq", nyq_abs[:, :, :], nyq[:, :, :], -1.0, nyq[:, :, :], ALU.mult, ALU.max, [n])
    n = ts("nyq", nyq_abs[:, :, :], nyq_abs[:, :, :], UNIT_EPS, None, ALU.add, after=[n])
    n = recip("nyq", nyq_abs[:, :, :], nyq_abs[:, :, :], [n])
    n = tt("nyq", nyq[:, :, :], nyq[:, :, :], nyq_abs[:, :, :], ALU.mult, [n])
    n = tt("nyq", nyq_sum[:, :], nyq[:, KK, :], nyq[:, VV, :], ALU.mult, [n])
    n1 = mm("nyq", PS[:, 6, 0:NT], C["upto"], nyq_sum[:, :], True, True, [n, bank_busy[6]])
    n2 = mm("nyq", PS[:, 7, 0:NT], C["ones"], nyq_sum[:, :], True, True, [bank_busy[7]])

    m = reduce("route", sum1[:, :], prob1[:, :, :], ALU.add, [m])
    m = recip("route", sum1[:, :], sum1[:, :], [m])
    m = tt("route", prob1[:, :, :], prob1[:, :, :], over_experts(sum1[:, :], E1), ALU.mult, [m])
    for k in range(TOPK):
        m = reduce("route", best1[:, k, :], prob1[:, :, :], ALU.max, [m])
        m = first_best(prob1[:, :, :], best1[:, k, :], C["iota1_low"], E1, tmp1[:, :, :], hot1[:, k, :, :],
                       first1[:, :], m)
        if k == 0:
            m = stt("route", prob1[:, :, :], hot1[:, k, :, :], -2.0, prob1[:, :, :], ALU.mult, ALU.add, [m])
    hot1_ready = tt("route", both1[:, :, :], hot1[:, 0, :, :], hot1[:, 1, :, :], ALU.add, [m])

    n = copy("nyq", nyq_sum[:, :], PS[:, 7, 0:NT], [n2])
    bank_busy[7] = [n]
    s = dve.add("nyq", lambda e: e.tensor_tensor_scan(nyq_scan[:, :], nyq_reset[:, :], nyq_sum[:, :], 0.0, ALU.mult,
                                                      ALU.add), [n, nyq_reset_ready])
    n = tt("nyq", nyq_scan[:, :], nyq_scan[:, :], nyq_sum[:, :], ALU.subtract, [s])
    n = tt("nyq", nyq_scan[:, :], PS[:, 6, 0:NT], nyq_scan[:, :], ALU.add, [n, n1])
    bank_busy[6] = [n]
    n = tt("nyq", nyq_scan[:, :], nyq_scan[:, :], nyq[:, QQ, :], ALU.mult, [n])
    nyq_turned = n

    reset_ready = make_reset(reset1[:, :, :], [x_free])
    m = count_before(both1[:, :, :], E1, hot1_ready, [6, 7], reset1[:, :, :], reset_ready,
                     totals1[:, :, :], running1[:, :, :], tmp1[:, :, :])
    m = tt("route", pad_f[:, :], running1[:, :, NT - 1], totals1[:, :, NT - 1], ALU.add, [m])
    m = ts("route", pad_f[:, :], pad_f[:, :], float(P - 1), None, ALU.add, after=[m])
    m = copy("route", pad_i[:, :], pad_f[:, :], [m])
    m = ts("route", pad_i[:, :], pad_i[:, :], 7, 7, ALU.logical_shift_right, ALU.logical_shift_left, after=[m])
    m = copy("route", pad_f[:, :], pad_i[:, :], [m])
    ones8 = C["ones"][:, 0:E1]
    m = dve.add("route", lambda e: e.tensor_tensor_scan(pad_end[:, :], ones8, pad_f[:, :], 0.0, ALU.mult, ALU.add),
                [m, const_in])
    m = tt("route", pad_base[:, :], pad_end[:, :], pad_f[:, :], ALU.subtract, [m])
    m = tt("route", both1[:, :, :], tmp1[:, :, :], over_tiles(pad_base[:, :], E1), ALU.add, [m])
    for k in range(TOPK):
        m = tt("route", tmp1[:, :, :], both1[:, :, :], hot1[:, k, :, :], ALU.mult, [m])
        m = reduce("route", first1[:, :], tmp1[:, :, :], ALU.add, [m])
        m = copy("route", slot1[:, k, :], first1[:, :], [m])
    slot1_ready = m
    n = turn("nyq_turn", PS[0:NT, 6, 0:P], nyq_scan[:, :], ident, [nyq_turned, bank_busy[6]])
    nyq_ready = copy("nyq", nyq_T[:, :], PS[0:NT, 6, 0:P], [n])
    bank_busy[6] = [nyq_ready]

    def routing1_rest():
        m = tt("route", sum1[:, :], best1[:, 0, :], best1[:, 1, :], ALU.add, [hot1_ready])
        m = ts("route", sum1[:, :], sum1[:, :], TOPK_EPS, None, ALU.add, after=[m])
        m = recip("route", sum1[:, :], sum1[:, :], [m])
        for k in range(TOPK):
            w = tt("route", weight1[:, k, :], best1[:, k, :], sum1[:, :], ALU.mult, [m])
        m = tt("route", owner[:, :, :], pad_end[:, :].unsqueeze(1).to_broadcast([P, TILES1, E1]),
               C["tile_start"].unsqueeze(2).to_broadcast([P, TILES1, E1]), ALU.is_le, [slot1_ready])
        m = reduce("route", owner_f[:, :], owner[:, :, :], ALU.add, [m])
        m = ts("route", owner_f[:, :], owner_f[:, :], float(E1 - 1), None, ALU.min, after=[m])
        return w, copy("route", tile_expert[:, :], owner_f[0:1, :], [m])

    top[0] = persistent_top
    W1 = place("W1", [P, E1, KD, F1])
    assert top[0] == after_xn
    KF = F1 // P
    W2 = place("W2", [P, E1, KF, D])
    assert top[0] == work
    to_scatter = [(t, k) for t in range(NT) for k in range(TOPK)]
    SCATTERS = 6

    def load_w1(ex, after):
        return dma("w1", W1[:, ex, :, :], a["W1"][ex].rearrange("(k p) n -> p k n", p=P), after)

    def load_w2(ex, after):
        return dma("w2", W2[:, ex, :, :], a["W2"][ex].rearrange("(k p) n -> p k n", p=P), after)

    XT_EXPERTS = 4
    per_expert = CHUNKS // XT_EXPERTS
    for ch in range(CHUNKS + 1):
        if ch + 2 < CHUNKS:
            spectra(ch + 2)
            if (ch + 3) % per_expert == 0:
                w2_in = load_w2((ch + 3) // per_expert - 1, [dft_done[ch + 2]])
        if ch + 1 < CHUNKS:
            magnitudes(ch + 1)
        if ch >= 1:
            inverse(ch - 1)
        if ch < CHUNKS:
            bind(ch)
        for t, k in to_scatter[SCATTERS * ch:SCATTERS * (ch + 1)]:
            scattered1 = scatter("scatter1", table1, SLOTS1, slot1[:, k, t:t + 1], XN[:, t, :],
                                 [slot1_ready, normed1[t], table1_zeroed])
        if ch == 0:
            weight1_ready, owner_ready = routing1_rest()
            for ex in range(XT_EXPERTS, E1):
                w2_in = load_w2(ex, [x1_ready[-1]])
        if ch == 2:
            for ex in range(E1 // 2):
                w1_in = load_w1(ex, [x_free, slot1_ready, weight1_ready, owner_ready])
        if ch == len(to_scatter) // SCATTERS + 2:
            for ex in range(E1 // 2, E1):
                w1_in = load_w1(ex, [scattered1])
    s1_saved = s1_free[0] + s1_free[1]
    attn1_end = [m for i in range(2) for m in (s1_free[i], u_free[i], pr_free[i])]

    top[0] = work
    b2 = place("b2", [P, E1, D])
    b1 = place("b1", [P, E1, KF])
    xg = place("xg", [P, 3, D])
    xgT = place("xgT", [P, 2, KD, P])
    hid = place("hid", [P, 2, F1])
    hidT = place("hidT", [P, 2, KF, P])
    row_of_tile = place("row_of_tile", [TILES1, P])
    YR = 12
    y1 = place("y1", [P, YR, D])
    ahead = 3
    xs = [place(f"xs{q}", [P, 2, 4, D]) for q in range(ahead)]
    free2 = attn1_end
    b_in = [dma("b12", b1[:, :, :], a["b1"], free2),
            dma("b12", b2[:, :, :], a["b2"].partition_broadcast(P), free2)][-1]
    xg_free, xgT_free, hid_free, hidT_free, y1_free = ([free2] * 3, [free2] * 2, [free2] * 2, [free2] * 2,
                                                       [free2] * YR)
    for t in range(NT):
        for k in range(TOPK):
            m = scatter("row_of", row_of, SLOTS1, slot1[:, k, t:t + 1], C["result_row"][:, k * NT + t:k * NT + t + 1],
                        [slot1_ready, const_in, row_of_filled])
    row_of_in = dma("row_of_in", row_of_tile[:, :], row_of.rearrange("(n p) o -> n (p o)", p=P), [m, free2], on=pool)
    HID_BANKS, HT_BANKS, Y_BANKS, TURN_BANKS = (0, 1), (2, 3), (4, 5), (6, 7)
    expert_on, xg_in, xgT_ready, hid_copied, hid_done = {}, {}, {}, {}, {}
    HALF = KF // 2

    def load_expert(queue, n):
        def issue(e):
            expert_on[queue.name] = e.value_load(tile_expert[0:1, n:n + 1], min_val=0, max_val=E1 - 1)
        queue.add("expert", issue, [owner_ready])

    def load_rows(n):
        xg_in[n] = dma(f"xg{n % 3}", xg[:, n % 3, :], table1[n * P:(n + 1) * P, :], [scattered1, xg_free[n % 3]])

    def turn_tile(n):
        i, b = n % 2, TURN_BANKS[n % 2]
        for k in range(KD):
            m = turn("xg_turn", PS[:, b, k * P:(k + 1) * P], xg[:, n % 3, k * P:(k + 1) * P], ident,
                     [xg_in[n], bank_busy[b]])
        xg_free[n % 3] = [m]
        xgT_ready[n] = activate("xgT_out", xgT[:, i, :, :].rearrange("p k n -> p (k n)"), PS[:, b, 0:KD * P],
                                ACT.Copy, [m, xgT_free[i]])
        bank_busy[b] = [xgT_ready[n]]

    def first_product(n):
        i = n % 2
        load_expert(pe, n)
        hid_copied[n] = []
        for half in range(2):
            b = HID_BANKS[half]
            cols = slice(half * HALF * P, (half + 1) * HALF * P)
            for k in range(KD):
                def issue(e, b=b, k=k, cols=cols):
                    w = W1[:, bass.ds(expert_on["pe"], 1), k, cols].rearrange("p o n -> p (o n)")
                    return e.matmul(PS[:, b, :], xgT[:, i, k, :], w, start=(k == 0), stop=(k == KD - 1))
                m = pe.add("w1", issue, [xgT_ready[n], w1_in, bank_busy[b]])
            if half == 0:
                c = activate("hid", hid[:, i, cols], PS[:, b, :], ACT.Copy, [m, hid_free[i]])
            else:
                c = copy("hid", hid[:, i, cols], PS[:, b, :], [m, hid_free[i]])
            bank_busy[b] = [c]
            hid_copied[n].append(c)
        xgT_free[i] = [m]

    def turn_hidden(n):
        i = n % 2
        load_expert(dve, n)
        hid_done[n] = []
        for half in range(2):
            b = HT_BANKS[half]
            for j in range(HALF):
                c = half * HALF + j
                m = turn("h_turn", PS[:, b, j * P:(j + 1) * P], hid[:, i, c * P:(c + 1) * P], ident,
                         [hid_copied[n][half], bank_busy[b]])
            cs = slice(half * HALF, (half + 1) * HALF)

            def add_bias(e, b=b, cs=cs):
                bias = b1[:, bass.ds(expert_on["dve"], 1), cs].rearrange("p o c -> p (o c)")
                return e.tensor_tensor(hidT[:, i, cs, :], PS[:, b, :].rearrange("p (c n) -> p c n", n=P),
                                       bias.unsqueeze(2).to_broadcast([P, HALF, P]), ALU.add)
            m2 = dve.add("b1", add_bias, [m, b_in, hidT_free[i]])
            bank_busy[b] = [m2]
            hid_done[n].append(activate("gelu", hidT[:, i, cs, :], hidT[:, i, cs, :], ACT.Gelu_apprx_tanh, [m2]))
        hid_free[i] = [m]

    def second_product(n):
        i, b = n % 2, Y_BANKS[n % 2]
        load_expert(pe, n)
        load_expert(dve, n)
        for c in range(KF):
            def issue(e, c=c):
                w = W2[:, bass.ds(expert_on["pe"], 1), c, :].rearrange("p o n -> p (o n)")
                return e.matmul(PS[:, b, 0:D], hidT[:, i, c, :], w, start=(c == 0), stop=(c == KF - 1))
            m = pe.add("w2", issue, [hid_done[n][c // HALF], w2_in, bank_busy[b]])
        hidT_free[i] = [m]

        def add_bias(e):
            bias = b2[:, bass.ds(expert_on["dve"], 1), :].rearrange("p o n -> p (o n)")
            return e.tensor_tensor(y1[:, n % YR, :], PS[:, b, 0:D], bias, ALU.add)
        m = dve.add("b2", add_bias, [m, b_in, y1_free[n % YR]])
        bank_busy[b] = [m]
        waiting.append((n, m))

    def scatter_results():
        while waiting:
            n, added = waiting.pop(0)
            y1_free[n % YR] = [scatter(f"y1_{n % YR}", result1, TOPK * T, row_of_slot[:, n:n + 1],
                                       y1[:, n % YR, :], [added, rows_known])]

    waiting, ROWS_KNOWN = [], YR - 2
    for n in range(3):
        load_rows(n)
    turn_tile(0)
    for n in range(TILES1 + 1):
        if n + 1 < TILES1:
            turn_tile(n + 1)
        if n + 3 < TILES1:
            load_rows(n + 3)
        if n:
            turn_hidden(n - 1)
        if n < TILES1:
            first_product(n)
        if n == ROWS_KNOWN:
            b = TURN_BANKS[n % 2]
            m = turn("row_turn", PS[:, b, 0:TILES1], row_of_tile[:, :], ident[0:TILES1, 0:TILES1],
                     [row_of_in, bank_busy[b]])
            rows_known = copy("rows_known", row_of_slot[:, :], PS[:, b, 0:TILES1], [m])
            bank_busy[b] = [rows_known]
        if n:
            second_product(n - 1)
        if n >= ROWS_KNOWN:
            scatter_results()
    y1_written = named(y1_free)

    top[0] = persistent_top
    QUARTERS = NT // 4
    both = [place(f"both{q}", [P, TOPK, 4, D]) for q in range(QUARTERS)]
    assert top[0] <= after_xn
    xs += [place(f"xs{q}", [P, 2, 4, D]) for q in range(ahead, QUARTERS)]
    assert top[0] <= work
    experts_done = [hidT_free[0], hidT_free[1]]
    s1_view = s1_dram.rearrange("(t p) d -> p t d", p=P)
    result_view = result1.rearrange("(k t p) d -> p k t d", k=TOPK, p=P)
    xs_in, both_in, stored = [], [], []

    def load_xs(q, after):
        four = slice(4 * q, 4 * q + 4)
        dma(f"x{q}", xs[q][:, 0, :, :], x1_view[:, four, :], [x1_saved, after])
        xs_in.append(dma(f"x{q}", xs[q][:, 1, :, :], s1_view[:, four, :], [s1_saved, after]))

    for q in range(ahead):
        load_xs(q, free2)
    for q in range(QUARTERS):
        for k in range(TOPK):
            m = dma(f"both{q}", both[q][:, k, :, :], result_view[:, k, 4 * q:4 * q + 4, :],
                    [y1_written, experts_done])
        both_in.append(m)
        if q + 1 >= ahead and q + 1 < QUARTERS:
            load_xs(q + 1, experts_done)
    for q in range(QUARTERS):
        first, second = both[q][:, 0, :, :], both[q][:, 1, :, :]
        for j in range(4):
            t = 4 * q + j
            m = activate("mix1", first[:, j, :], first[:, j, :], ACT.Identity, [both_in[q], weight1_ready],
                         scale=weight1[:, 0, t:t + 1])
            m = stt("mix1", first[:, j, :], second[:, j, :], weight1[:, 1, t:t + 1], first[:, j, :],
                    ALU.mult, ALU.add, [m])
        m = activate("silu1", first, first, ACT.Silu, [m])
        m = tt("mix1", first, first, xs[q][:, 1, :, :], ALU.mult, [m, xs_in[q]])
        m = tt("mix1", xs[q][:, 0, :, :], xs[q][:, 0, :, :], first, ALU.add, [m])
        stored.append(dma("out", out_view[:, 4 * q:4 * q + 4, :], xs[q][:, 0, :, :], [m]))
    replay(nc, (pe, dve, act, pool, sp), stored, sp)


def replay(nc, queues, finish, sp):
    sp.add("end", lambda e: e.nop(), finish)
    sems = {}
    for q in queues:
        for stage in q.count():
            sems[stage] = nc.alloc_semaphore(stage)
    pe, dve, act, pool, sp = queues
    with nc.Block() as block:
        block.tensor(lambda e: pe.emit(e, sems))
        block.vector(lambda e: dve.emit(e, sems))
        block.scalar(lambda e: act.emit(e, sems))
        block.gpsimd(lambda e: pool.emit(e, sems))
        block.sync(lambda e: sp.emit(e, sems))


def kernel(**inputs):
    import concourse.bacc as bacc
    from concourse.bass_utils import run_bass_kernel_spmd

    as_np = {k: np.ascontiguousarray(v) for k, v in inputs.items()}
    const, dft, inv = CONSTS
    rel_at = np.arange(WIN)[:, None] - np.arange(WIN)[None, :] + WIN - 1
    rel = as_np["L0_attn_rel_bias"][rel_at].transpose(2, 0, 1)
    rel = rel.reshape(KD, 4, 2, WIN, WIN).transpose(2, 3, 0, 1, 4).reshape(P, KD, 4, WIN)
    proj = as_np["L0_attn_proj_w"].reshape(PAIRS, 2, HD, D).transpose(0, 2, 1, 3).reshape(P, 2, D)
    attn1_b = np.stack([as_np[f"L1_attn_b{c}"].reshape(KD, P).T for c in "qkv"], 1)
    data = {
        "const": const, "dft": dft, "inv": inv,
        "x": as_np["L0_attn_x"].reshape(T, D),
        "qkv_w": as_np["L0_attn_qkv_w"], "proj_w": proj, "proj_b": as_np["L0_attn_proj_b"],
        "qkv_b": as_np["L0_attn_qkv_b"].reshape(3 * KD, P).T, "v_b": as_np["L0_attn_qkv_b"][2 * D:],
        "rel": rel, "w_router": as_np["L0_ffn_w_router"], "w_gate": as_np["L0_ffn_w_gate"],
        "w_up": as_np["L0_ffn_w_up"], "w_down": as_np["L0_ffn_w_down"],
        "Wq": as_np["L1_attn_Wq"], "Wk": as_np["L1_attn_Wk"], "Wv": as_np["L1_attn_Wv"], "attn1_b": attn1_b,
        "Wg": as_np["L1_ffn_Wg"], "bg": as_np["L1_ffn_bg"], "W1": as_np["L1_ffn_W1"],
        "b1": as_np["L1_ffn_b1"].reshape(E1, F1 // P, P).transpose(2, 0, 1),
        "W2": as_np["L1_ffn_W2"], "b2": as_np["L1_ffn_b2"],
    }
    nc = bacc.Bacc("TRN2", target_bir_lowering=False, num_devices=1)
    arrays, a = {}, {}
    for name, v in data.items():
        arrays[f"in_{name}"] = np.ascontiguousarray(v)
        a[name] = nc.dram_tensor(f"in_{name}", v.shape, mybir.dt.from_np(v.dtype), kind="ExternalInput").ap()
    out = nc.dram_tensor("out", (T, D), F32, kind="ExternalOutput").ap()
    build(nc, a, out)
    r = run_bass_kernel_spmd(nc, [arrays], core_ids=[0])
    return r.results[0]["out"].reshape(BATCH, SEQ, D)
```
